# Optimizing a Trainium2 kernel written in Bass

```python
import numpy as np
import jax
import jax.numpy as jnp

def _softmax(x, axis=-1):
    return jax.nn.softmax(x, axis=axis)

def _gelu(x):
    return jax.nn.gelu(x, approximate=True)

def _silu(x):
    return jax.nn.silu(x)

def _sigmoid(x):
    return jax.nn.sigmoid(x)

def _layernorm(x, axis=-1, eps=1e-05):
    m = jnp.mean(x, axis=axis, keepdims=True)
    v = jnp.var(x, axis=axis, keepdims=True)
    return (x - m) / jnp.sqrt(v + eps)

def _scatter_add(tgt, idx, src, axis=0):
    return tgt.at[idx].add(src)

def _segment_sum(src, seg, n):
    return jax.ops.segment_sum(src, seg, n)
kernel_name = 'mk_gnn_ffn_d2_gnn_r32_e97041'

def setup_inputs(seed: int=0):
    np.random.seed(seed)
    _w = jnp.asarray

    def _rec_inputs():
        import jax
        import jax.numpy as jnp
        _gk = jax.random.key(seed)
        x = -0.0002117 + 1 * jax.random.normal(jax.random.fold_in(_gk, 1), (3125, 256), jnp.float32)
        src = jax.random.randint(jax.random.fold_in(_gk, 2), (50000,), 0, 3125, jnp.int32)
        dst = jnp.minimum((3125 * jax.random.uniform(jax.random.fold_in(_gk, 3), (50000,)) ** 2.0).astype(jnp.int32), 99999)
        _o = jnp.argsort(dst, stable=True)
        src = src[_o]
        dst = dst[_o]
        edge_weight = jax.random.uniform(jax.random.fold_in(_gk, 13), (50000,), jnp.float32, 0.0, 1)
        return (x, src, dst, edge_weight)
    x, src, dst, edge_weight = _rec_inputs()

    def _L0_gnn_setup():
        import jax, jax.numpy as jnp
        import numpy as np
        N_NODES = 3125
        N_EDGES = 100000
        D_IN = 256
        D_OUT = 256
        key = jax.random.key(seed)
        k1, k2, k3, k4, k5 = jax.random.split(key, 5)
        x = jax.random.normal(k1, (N_NODES, D_IN), dtype=jnp.float32)
        weight = jax.random.normal(k2, (D_IN, D_OUT), dtype=jnp.float32) * (1.0 / np.sqrt(D_IN))
        adj_val = jax.random.uniform(k3, (N_EDGES,), dtype=jnp.float32)
        edge_row = jax.random.randint(k4, (N_EDGES,), 0, N_NODES, dtype=jnp.int32)
        edge_col = jax.random.randint(k5, (N_EDGES,), 0, N_NODES, dtype=jnp.int32)
        return {'x': x, 'weight': weight, 'adj_val': adj_val, 'edge_row': edge_row, 'edge_col': edge_col}
    _L0_gnn_all = _L0_gnn_setup()
    _L0_gnn_in = {k: v for k, v in _L0_gnn_all.items() if k in ('weight',)}
    del _L0_gnn_all

    def _L0_ffn_setup():
        import jax, jax.numpy as jnp
        import numpy as np
        TOP_K = 2
        LN_EPS = 1e-05
        key = jax.random.key(seed)
        ks = jax.random.split(key, 8)
        B, S, D, E, H = (16, 1024, 256, 8, 1024)
        x = jax.random.normal(ks[0], (B, S, D), dtype=jnp.float32)
        Wr = jax.random.normal(ks[1], (D, E), dtype=jnp.float32) * 0.1
        br = jnp.zeros((E,), dtype=jnp.float32)
        ln_g = jnp.ones((E, D), dtype=jnp.float32)
        ln_b = jnp.zeros((E, D), dtype=jnp.float32)
        W1 = jax.random.normal(ks[2], (E, D, H), dtype=jnp.float32) * (1.0 / np.sqrt(D))
        b1 = jnp.zeros((E, H), dtype=jnp.float32)
        W2 = jax.random.normal(ks[3], (E, H, D), dtype=jnp.float32) * (1.0 / np.sqrt(H))
        b2 = jnp.zeros((E, D), dtype=jnp.float32)
        return {'x': x, 'Wr': Wr, 'br': br, 'ln_g': ln_g, 'ln_b': ln_b, 'W1': W1, 'b1': b1, 'W2': W2, 'b2': b2}
    _L0_ffn_all = _L0_ffn_setup()
    _L0_ffn_in = {k: v for k, v in _L0_ffn_all.items() if k in ('Wr', 'br', 'ln_g', 'ln_b', 'W1', 'b1', 'W2', 'b2')}
    del _L0_ffn_all

    def _L1_gnn_setup():
        import jax, jax.numpy as jnp
        import numpy as np
        N_NODES = 3125
        BN_EPS = 1e-05

        def gcn_conv(x, src, dst, W, b, n):
            h = x @ W
            loop = jnp.arange(n, dtype=src.dtype)
            s = jnp.concatenate([src, loop])
            d = jnp.concatenate([dst, loop])
            deg = jax.ops.segment_sum(jnp.ones(s.shape, h.dtype), d, num_segments=n)
            dinv = jnp.where(deg > 0, jax.lax.rsqrt(jnp.maximum(deg, 1.0)), 0.0)
            norm = dinv[s] * dinv[d]
            msg = h[s] * norm[:, None]
            out = jax.ops.segment_sum(msg, d, num_segments=n)
            return out + b

        def batch_norm(x, gamma, beta):
            mean = jnp.mean(x, axis=0)
            var = jnp.mean(jnp.square(x - mean), axis=0)
            return (x - mean) * jax.lax.rsqrt(var + BN_EPS) * gamma + beta
        key = jax.random.key(seed)
        ks = jax.random.split(key, 10)
        d0, d1, d2 = (256, 128, 64)
        d_cat = d0 + d1 + d2
        inp = {'node_features': jax.random.normal(ks[0], (N_NODES, d0), jnp.float32), 'edge_idx': jax.random.randint(ks[1], (2, 50000), 0, N_NODES, jnp.int64), 'W1': jax.random.normal(ks[2], (d0, d1), jnp.float32) * (1.0 / np.sqrt(d0)), 'b1': jnp.zeros((d1,), jnp.float32), 'g1': jnp.ones((d1,), jnp.float32), 'be1': jnp.zeros((d1,), jnp.float32), 'W2': jax.random.normal(ks[3], (d1, d2), jnp.float32) * (1.0 / np.sqrt(d1)), 'b2': jnp.zeros((d2,), jnp.float32), 'g2': jnp.ones((d2,), jnp.float32), 'be2': jnp.zeros((d2,), jnp.float32), 'Wfc': jax.random.normal(ks[4], (d_cat, d0), jnp.float32) * (1.0 / np.sqrt(d_cat)), 'bfc': jnp.zeros((d0,), jnp.float32)}
        return inp
    _L1_gnn_all = _L1_gnn_setup()
    _L1_gnn_in = {k: v for k, v in _L1_gnn_all.items() if k in ('W1', 'b1', 'g1', 'be1', 'W2', 'b2', 'g2', 'be2', 'Wfc', 'bfc')}
    del _L1_gnn_all

    def _L1_ffn_setup():
        import math
        import jax, jax.numpy as jnp
        import numpy as np
        CAPACITY_FACTOR = 1.25
        TOP_K = 2
        LN_EPS = 1e-05

        def _layer_norm(x, gamma, beta):
            mu = jnp.mean(x, axis=-1, keepdims=True)
            var = jnp.var(x, axis=-1, keepdims=True)
            return (x - mu) * jax.lax.rsqrt(var + LN_EPS) * gamma + beta
        key = jax.random.key(seed)
        ks = jax.random.split(key, 4)
        B, S, D, F, E = (8, 128, 256, 512, 8)
        x = jax.random.normal(ks[0], (B, S, D), dtype=jnp.float32)
        Wr = jax.random.normal(ks[1], (D, E), dtype=jnp.float32) / np.sqrt(D)
        br = jnp.zeros((E,), jnp.float32)
        W1 = jax.random.normal(ks[2], (E, D, F), dtype=jnp.float32) / np.sqrt(D)
        b1 = jnp.zeros((E, F), jnp.float32)
        W2 = jax.random.normal(ks[3], (E, F, D), dtype=jnp.float32) / np.sqrt(F)
        b2 = jnp.zeros((E, D), jnp.float32)
        gamma = jnp.ones((D,), jnp.float32)
        beta = jnp.zeros((D,), jnp.float32)
        return {'x': x, 'Wr': Wr, 'br': br, 'W1': W1, 'b1': b1, 'W2': W2, 'b2': b2, 'gamma': gamma, 'beta': beta}
    _L1_ffn_all = _L1_ffn_setup()
    _L1_ffn_in = {k: v for k, v in _L1_ffn_all.items() if k in ('Wr', 'br', 'W1', 'b1', 'W2', 'b2', 'gamma', 'beta')}
    del _L1_ffn_all
    return {'x': x, 'src': src, 'dst': dst, 'edge_weight': edge_weight, 'L0_gnn_weight': _L0_gnn_in['weight'], 'L0_ffn_Wr': _L0_ffn_in['Wr'], 'L0_ffn_br': _L0_ffn_in['br'], 'L0_ffn_ln_g': _L0_ffn_in['ln_g'], 'L0_ffn_ln_b': _L0_ffn_in['ln_b'], 'L0_ffn_W1': _L0_ffn_in['W1'], 'L0_ffn_b1': _L0_ffn_in['b1'], 'L0_ffn_W2': _L0_ffn_in['W2'], 'L0_ffn_b2': _L0_ffn_in['b2'], 'L1_gnn_W1': _L1_gnn_in['W1'], 'L1_gnn_b1': _L1_gnn_in['b1'], 'L1_gnn_g1': _L1_gnn_in['g1'], 'L1_gnn_be1': _L1_gnn_in['be1'], 'L1_gnn_W2': _L1_gnn_in['W2'], 'L1_gnn_b2': _L1_gnn_in['b2'], 'L1_gnn_g2': _L1_gnn_in['g2'], 'L1_gnn_be2': _L1_gnn_in['be2'], 'L1_gnn_Wfc': _L1_gnn_in['Wfc'], 'L1_gnn_bfc': _L1_gnn_in['bfc'], 'L1_ffn_Wr': _L1_ffn_in['Wr'], 'L1_ffn_br': _L1_ffn_in['br'], 'L1_ffn_W1': _L1_ffn_in['W1'], 'L1_ffn_b1': _L1_ffn_in['b1'], 'L1_ffn_W2': _L1_ffn_in['W2'], 'L1_ffn_b2': _L1_ffn_in['b2'], 'L1_ffn_gamma': _L1_ffn_in['gamma'], 'L1_ffn_beta': _L1_ffn_in['beta']}

def reference(x, src, dst, edge_weight, L0_gnn_weight, L0_ffn_Wr, L0_ffn_br, L0_ffn_ln_g, L0_ffn_ln_b, L0_ffn_W1, L0_ffn_b1, L0_ffn_W2, L0_ffn_b2, L1_gnn_W1, L1_gnn_b1, L1_gnn_g1, L1_gnn_be1, L1_gnn_W2, L1_gnn_b2, L1_gnn_g2, L1_gnn_be2, L1_gnn_Wfc, L1_gnn_bfc, L1_ffn_Wr, L1_ffn_br, L1_ffn_W1, L1_ffn_b1, L1_ffn_W2, L1_ffn_b2, L1_ffn_gamma, L1_ffn_beta):
    import jax
    import jax.numpy as jnp

    def _L0_gnn_ref(x, weight, adj_val, edge_row, edge_col):
        import jax, jax.numpy as jnp
        import numpy as np
        N_NODES = 3125
        N_EDGES = 100000
        D_IN = 256
        D_OUT = 256
        support = jnp.matmul(x, weight)
        msgs = adj_val[:, None] * support[edge_col]
        out = jax.ops.segment_sum(msgs, edge_row, num_segments=x.shape[0])
        return out

    def _L0_ffn_ref(x, Wr, br, ln_g, ln_b, W1, b1, W2, b2):
        import jax, jax.numpy as jnp
        import numpy as np
        TOP_K = 2
        LN_EPS = 1e-05
        B, S, D = x.shape
        N = B * S
        xt = x.reshape(N, D)
        logits = xt @ Wr + br
        probs = jax.nn.softmax(logits, axis=-1)
        top_p, top_idx = jax.lax.top_k(probs, TOP_K)
        weights = top_p / top_p.sum(axis=-1, keepdims=True)
        mu = xt.mean(axis=-1, keepdims=True)
        var = ((xt - mu) ** 2).mean(axis=-1, keepdims=True)
        xn = (xt - mu) * jax.lax.rsqrt(var + LN_EPS)
        xe = xn[None, :, :] * ln_g[:, None, :] + ln_b[:, None, :]
        h = jax.nn.gelu(jnp.einsum('end,edh->enh', xe, W1) + b1[:, None, :], approximate=False)
        y = jnp.einsum('enh,ehd->end', h, W2) + b2[:, None, :]
        y_tok = jnp.transpose(y, (1, 0, 2))
        sel = jnp.take_along_axis(y_tok, top_idx[:, :, None], axis=1)
        out = (weights[:, :, None] * sel).sum(axis=1)
        return out.reshape(B, S, D)

    def _L1_gnn_ref(node_features, edge_idx, W1, b1, g1, be1, W2, b2, g2, be2, Wfc, bfc):
        import jax, jax.numpy as jnp
        import numpy as np
        N_NODES = 3125
        BN_EPS = 1e-05

        def gcn_conv(x, src, dst, W, b, n):
            h = x @ W
            loop = jnp.arange(n, dtype=src.dtype)
            s = jnp.concatenate([src, loop])
            d = jnp.concatenate([dst, loop])
            deg = jax.ops.segment_sum(jnp.ones(s.shape, h.dtype), d, num_segments=n)
            dinv = jnp.where(deg > 0, jax.lax.rsqrt(jnp.maximum(deg, 1.0)), 0.0)
            norm = dinv[s] * dinv[d]
            msg = h[s] * norm[:, None]
            out = jax.ops.segment_sum(msg, d, num_segments=n)
            return out + b

        def batch_norm(x, gamma, beta):
            mean = jnp.mean(x, axis=0)
            var = jnp.mean(jnp.square(x - mean), axis=0)
            return (x - mean) * jax.lax.rsqrt(var + BN_EPS) * gamma + beta
        n = node_features.shape[0]
        src, dst = (edge_idx[0], edge_idx[1])
        feats = [node_features]
        x = node_features
        x = gcn_conv(x, src, dst, W1, b1, n)
        x = jax.nn.relu(batch_norm(x, g1, be1))
        feats.append(x)
        x = gcn_conv(x, src, dst, W2, b2, n)
        x = jax.nn.relu(batch_norm(x, g2, be2))
        feats.append(x)
        cat = jnp.concatenate(feats, axis=1)
        return jax.nn.relu(cat @ Wfc + bfc)

    def _L1_ffn_ref(x, Wr, br, W1, b1, W2, b2, gamma, beta):
        import math
        import jax, jax.numpy as jnp
        import numpy as np
        CAPACITY_FACTOR = 1.25
        TOP_K = 2
        LN_EPS = 1e-05

        def _layer_norm(x, gamma, beta):
            mu = jnp.mean(x, axis=-1, keepdims=True)
            var = jnp.var(x, axis=-1, keepdims=True)
            return (x - mu) * jax.lax.rsqrt(var + LN_EPS) * gamma + beta
        B, S, D = x.shape
        E = Wr.shape[1]
        N = B * S
        K = TOP_K
        logits = jnp.mean(x, axis=1) @ Wr + br
        routing_weights = jax.nn.softmax(logits, axis=-1)
        capacity = float(math.ceil(N * CAPACITY_FACTOR / E))
        expected_loads = routing_weights.sum(axis=0) * (N / B)
        scale = jnp.where(expected_loads > capacity, capacity / expected_loads, 1.0)
        routing_weights = jax.nn.softmax(routing_weights * scale, axis=-1)
        rw_tok = jnp.broadcast_to(routing_weights[:, None, :], (B, S, E)).reshape(N, E)
        top_w, top_i = jax.lax.top_k(rw_tok, K)
        top_w = jax.nn.softmax(top_w, axis=-1)
        xf = x.reshape(N, D)
        h = jax.nn.gelu(jnp.einsum('nd,edf->enf', xf, W1) + b1[:, None, :], approximate=False)
        y = jnp.einsum('enf,efd->end', h, W2) + b2[:, None, :]
        w_dense = jnp.zeros((N, E), x.dtype).at[jnp.arange(N)[:, None], top_i].add(top_w)
        out = jnp.einsum('ne,end->nd', w_dense, y).reshape(B, S, D)
        out = _layer_norm(out + x, gamma, beta)
        return out
    edge_index = jnp.stack([src, dst])
    x = x + _L0_gnn_ref(_layernorm(x, axis=-1), L0_gnn_weight, edge_weight, src, dst)
    x = x + _L0_ffn_ref(_layernorm(x, axis=-1)[None], L0_ffn_Wr, L0_ffn_br, L0_ffn_ln_g, L0_ffn_ln_b, L0_ffn_W1, L0_ffn_b1, L0_ffn_W2, L0_ffn_b2)[0]
    x = x + _L1_gnn_ref(_layernorm(x, axis=-1), edge_index, L1_gnn_W1, L1_gnn_b1, L1_gnn_g1, L1_gnn_be1, L1_gnn_W2, L1_gnn_b2, L1_gnn_g2, L1_gnn_be2, L1_gnn_Wfc, L1_gnn_bfc)
    x = x + _L1_ffn_ref(_layernorm(x, axis=-1)[None], L1_ffn_Wr, L1_ffn_br, L1_ffn_W1, L1_ffn_b1, L1_ffn_W2, L1_ffn_b2, L1_ffn_gamma, L1_ffn_beta)[0]
    return x

_drawn_inputs = setup_inputs


def setup_inputs(seed=0):
    import zlib

    import numpy as np

    out = dict(_drawn_inputs(seed))
    spreads = {'L0_ffn_br': (0.0, 0.1),
     'L0_ffn_ln_g': (1.0, 0.2),
     'L0_ffn_ln_b': (0.0, 0.377),
     'L0_ffn_b1': (0.0, 0.373),
     'L0_ffn_b2': (0.0, 0.1),
     'L1_gnn_b1': (0.0, 0.8),
     'L1_gnn_g1': (1.0, 0.574),
     'L1_gnn_be1': (0.0, 0.58),
     'L1_gnn_b2': (0.0, 0.8),
     'L1_gnn_g2': (1.0, 0.6),
     'L1_gnn_be2': (0.0, 0.8),
     'L1_gnn_bfc': (0.0, 0.272),
     'L1_ffn_br': (0.0, 0.8),
     'L1_ffn_b1': (0.0, 0.656),
     'L1_ffn_b2': (0.0, 0.435),
     'L1_ffn_gamma': (1.0, 0.2),
     'L1_ffn_beta': (0.0, 0.301)}
    factors = {}
    for name, (base, spread) in spreads.items():
        noise = np.random.default_rng([zlib.crc32(name.encode()), seed]).standard_normal(out[name].shape)
        drawn = base * np.exp(spread * noise) if base else spread * noise
        out[name] = jnp.asarray(drawn.astype(out[name].dtype))
    for name, factor in factors.items():
        out[name] = (out[name] * factor).astype(out[name].dtype)
    return out
```

```python
from contextlib import ExitStack

import concourse.bass as bass
import numpy as np
from concourse import mybir
from concourse.alu_op_type import AluOpType as ALU

F32 = mybir.dt.float32
I32 = mybir.dt.int32
U32 = mybir.dt.uint32
BF16 = mybir.dt.bfloat16
ACT = mybir.ActivationFunctionType
AX = mybir.AxisListType

NODES, D = 3125, 256
P = 125
T = NODES // P
EDGES = 50000
EC = EDGES // P
S = 128
SLOTS = 420
assert (EDGES + T * (S - 1)) // S <= SLOTS
EXPERTS, TOPK = 8, 2
H0, H1 = 1024, 512
B = 256
BLOCKS = (NODES * TOPK + EXPERTS * (B - 1)) // B
C1, C2 = 128, 64
ROUND = 12582912.0
U = 5
LN_EPS = BN_EPS = 1e-5
ds = bass.ds


class Core:

    def __init__(self, nc, ctx, args):
        self.nc, self.ctx, self.args = nc, ctx, args

    def keep(self, name, shape, dt=F32):
        return self.ctx.enter_context(self.nc.sbuf_tensor(name, shape, dt))

    def semaphore(self, name):
        return self.nc.alloc_semaphore(name)


def bank(c, stack, name):
    return stack.enter_context(c.nc.psum_tensor(name, [128, 512], F32))


def linker(engine, sem, base=0):
    count = [0]

    def link(instruction):
        count[0] += 1
        instruction.then_inc(sem, 1)
        engine.wait_ge(sem, base + count[0])

    return link


def wait_slot(engine, sem, value):
    engine.wait_ge(sem, value)
    engine.nop(nofuse=True)


def row_to_all(ap, parts):
    return ap.rearrange("(a f) -> a f", a=1).broadcast_to([parts, ap.shape[0]])


def stage_constants(c):
    nc = c.nc
    c.iota = c.keep("iota", [128, 512])
    c.ident = c.keep("ident", [128, 128])
    c.ones = c.keep("ones", [128, 128])
    c.before = c.keep("before", [128, 128])
    c.x = c.keep("x_now", [P, T, D])
    with ExitStack() as s:
        iota_i = s.enter_context(nc.sbuf_tensor("iota_i", [128, 512], I32))
        sem = lambda n: c.semaphore(n)
        x_in, filled, selected, iota_made, iota_cast = (sem(n) for n in ("x_in", "filled", "selected", "iota_made", "iota_cast"))
        block = s.enter_context(nc.Block())

        @block.sync
        def _(sp):
            sp.dma_start(c.x[:, :, :], c.args["x"].rearrange("(t p) f -> p t f", p=P)).then_inc(x_in, 16)
            sp.wait_ge(x_in, 16)

        @block.gpsimd
        def _(pool):
            nc.gpsimd.iota(iota_i[:, :], pattern=[[1, 512]], base=0, channel_multiplier=0).then_inc(iota_made, 1)
            nc.gpsimd.memset(c.ident[:, :], 0.0).then_inc(filled, 1)
            nc.gpsimd.memset(c.before[:, :], 1.0).then_inc(filled, 1)
            nc.gpsimd.memset(c.ones[:, :], 1.0).then_inc(filled, 1)
            pool.wait_ge(filled, 3)
            nc.gpsimd.affine_select(out=c.ident[:, :], in_=c.ident[:, :], compare_op=ALU.not_equal, fill=1.0, base=0,
                                    pattern=[[-1, 128]], channel_multiplier=1).then_inc(selected, 1)
            nc.gpsimd.affine_select(out=c.before[:, :], in_=c.before[:, :], compare_op=ALU.is_gt, fill=0.0, base=0,
                                    pattern=[[1, 128]], channel_multiplier=-1).then_inc(selected, 1)

        @block.vector
        def _(dve):
            dve.wait_ge(iota_made, 1)
            nc.vector.tensor_copy(c.iota[:, :], iota_i[:, :]).then_inc(iota_cast, 1)


def stage_norm_stats(c, tag, src, mean, rstd):
    nc = c.nc
    with ExitStack() as s:
        st = s.enter_context(nc.sbuf_tensor(tag + "_st", [P, T, 6], F32))
        dm = s.enter_context(nc.sbuf_tensor(tag + "_dm", [P, T], F32))
        var = s.enter_context(nc.sbuf_tensor(tag + "_var", [P, T], F32))
        std = s.enter_context(nc.sbuf_tensor(tag + "_std", [P, T], F32))
        stats_done = c.semaphore(tag + "_stats")
        chain = c.semaphore(tag + "_chain")
        var_ready = c.semaphore(tag + "_var_ready")
        std_ready = c.semaphore(tag + "_std_ready")
        block = s.enter_context(nc.Block())

        @block.vector
        def _(dve):
            with dve.Fori(0, T // U) as i:
                for k in range(U):
                    nc.vector.bn_stats(st[:, ds(i * U + k, 1), :].rearrange("p a f -> p (a f)"),
                                       src[:, ds(i * U + k, 1), :].rearrange("p a f -> p (a f)")).then_inc(stats_done, 1)
            dve.wait_ge(stats_done, T)
            link = linker(dve, chain)
            link(nc.vector.tensor_tensor(dm[:, :], st[:, :, 1], st[:, :, 4], ALU.subtract))
            link(nc.vector.tensor_tensor(mean[:, :], st[:, :, 1], st[:, :, 4], ALU.add))
            link(nc.vector.tensor_scalar(mean[:, :], mean[:, :], 0.5, None, ALU.mult))
            link(nc.vector.tensor_tensor(dm[:, :], dm[:, :], dm[:, :], ALU.mult))
            link(nc.vector.tensor_tensor(var[:, :], st[:, :, 2], st[:, :, 5], ALU.add))
            link(nc.vector.scalar_tensor_tensor(out=var[:, :], in0=dm[:, :], scalar=D / 4.0, in1=var[:, :],
                                                op0=ALU.mult, op1=ALU.add))
            nc.vector.tensor_scalar(var[:, :], var[:, :], 1.0 / D, LN_EPS, ALU.mult, ALU.add).then_inc(var_ready, 1)
            dve.wait_ge(std_ready, 1)
            nc.vector.reciprocal(rstd[:, :], std[:, :]).then_inc(chain, 1)

        @block.scalar
        def _(act):
            act.wait_ge(var_ready, 1)
            nc.scalar.activation(std[:, :], var[:, :], ACT.Sqrt).then_inc(std_ready, 1)


def stage_project(c, tag, src, width, rhs, m, outs, norm=None, keep_t=None, dram=None):
    nc = c.nc
    chunks = [(a, min(128, width - a)) for a in range(0, width, 128)]
    with ExitStack() as s:
        rows = s.enter_context(nc.sbuf_tensor(tag + "_rows", [P, U, width], F32))
        rows_t = s.enter_context(nc.sbuf_tensor(tag + "_rows_t", [128, 2, len(chunks), P], F32))
        ps_t = [bank(c, s, f"{tag}_ps_t{b}")[:, 0:len(chunks) * P].rearrange("p (j r) -> p j r", r=P) for b in range(2)]
        ps_o = [bank(c, s, f"{tag}_ps_o{b}")[0:P, 0:max(m, 1)] for b in range(2)]
        sem = lambda n: c.semaphore(f"{tag}_{n}")
        rows_ready, turned, copied, multiplied, taken, stored = (
            sem(n) for n in ("rows_ready", "turned", "copied", "multiplied", "taken", "stored"))
        block = s.enter_context(nc.Block())

        def free_after(i, k):
            return i * U if k < 2 else i * U + k - 1

        @block.vector
        def _(dve):
            def prepare(i):
                wait_slot(dve, turned, i * U)
                for k in range(U):
                    t = i * U + k
                    tile_in = src[:, ds(t, 1), 0:width].rearrange("p a f -> p (a f)")
                    if norm is None:
                        nc.vector.tensor_copy(rows[:, k, :], tile_in).then_inc(rows_ready, 1)
                    else:
                        nc.vector.tensor_scalar(rows[:, k, :], tile_in, norm[0][:, ds(t, 1)], norm[1][:, ds(t, 1)],
                                                ALU.subtract, ALU.mult).then_inc(rows_ready, 1)

            with dve.Fori(0, T // U) as i:
                prepare(i)
                if m:
                    for k in range(U):
                        wait_slot(dve, multiplied, i * U + k + 1)
                        steps = outs(i * U + k, ps_o[k % 2])
                        for step in steps[:-1]:
                            step().then_inc(stored, 1)
                        steps[-1]().then_inc(taken, 1)

        @block.scalar
        def _(act):
            with act.Fori(0, T // U) as i:
                for k in range(U):
                    if m:
                        act.wait_ge(multiplied, free_after(i, k))
                    wait_slot(act, turned, i * U + k + 1)
                    for j, (_, w) in enumerate(chunks):
                        if keep_t is None:
                            nc.scalar.copy(rows_t[0:w, k % 2, j, :], ps_t[k % 2][0:w, j, :]).then_inc(copied, 1)
                        else:
                            nc.scalar.copy(keep_t[0:w, j, ds((i * U + k) * P, P)], ps_t[k % 2][0:w, j, :]).then_inc(copied, 1)

        @block.tensor
        def _(pe):
            n = len(chunks)
            with pe.Fori(0, T // U) as i:
                for k in range(U):
                    pe.wait_ge(copied, free_after(i, k) * n)
                    wait_slot(pe, rows_ready, i * U + k + 1)
                    for j, (a, w) in enumerate(chunks):
                        last = nc.tensor.transpose(ps_t[k % 2][0:w, j, :], rows[:, k, a:a + w], c.ident[0:P, 0:P])
                    last.then_inc(turned, 1)
                    if m:
                        pe.wait_ge(taken, free_after(i, k))
                        wait_slot(pe, copied, (i * U + k + 1) * n)
                        for j, (_, w) in enumerate(chunks):
                            last = nc.tensor.matmul(ps_o[k % 2][:, :], rows_t[0:w, k % 2, j, :], rhs[0:w, j, :],
                                                    start=(j == 0), stop=(j == n - 1))
                        last.then_inc(multiplied, 1)

    if dram is not None:
        with ExitStack() as s:
            rows_out = c.semaphore(tag + "_rows_out")
            block = s.enter_context(nc.Block())

            @block.sync
            def _(sp):
                sp.dma_start(dram[0].rearrange("(t p) f -> p t f", p=P), dram[1]).then_inc(rows_out, 16)
                sp.wait_ge(rows_out, 16)


def stage_edge_records(c, tag, add_to, other, weight, rec, bucket):
    nc = c.nc
    with ExitStack() as s:
        to_i = s.enter_context(nc.sbuf_tensor(tag + "_to_i", [P, EC], I32))
        ot_i = s.enter_context(nc.sbuf_tensor(tag + "_ot_i", [P, EC], I32))
        w_in = s.enter_context(nc.sbuf_tensor(tag + "_w", [P, EC], F32))
        to_f = s.enter_context(nc.sbuf_tensor(tag + "_to_f", [P, EC], F32))
        loaded = c.semaphore(tag + "_loaded")
        chain = c.semaphore(tag + "_chain")
        block = s.enter_context(nc.Block())

        @block.sync
        def _(sp):
            sp.dma_start(to_i[:, :], add_to.rearrange("(p c) -> p c", p=P)).then_inc(loaded, 16)
            sp.dma_start(ot_i[:, :], other.rearrange("(p c) -> p c", p=P)).then_inc(loaded, 16)
            sp.dma_start(w_in[:, :], weight.rearrange("(p c) -> p c", p=P)).then_inc(loaded, 16)

        @block.vector
        def _(dve):
            link = linker(dve, chain)
            dve.wait_ge(loaded, 48)
            link(nc.vector.memset(rec[:, :, :], 0.0))
            link(nc.vector.tensor_copy(to_f[:, :], to_i[:, :]))
            link(nc.vector.tensor_scalar(bucket[:, :], to_f[:, :], 1.0 / P, -(P - 1) / (2.0 * P), ALU.mult, ALU.add))
            link(nc.vector.tensor_scalar(bucket[:, :], bucket[:, :], ROUND, ROUND, ALU.add, ALU.subtract))
            link(nc.vector.scalar_tensor_tensor(out=rec[:, :, 0], in0=bucket[:, :], scalar=-float(P), in1=to_f[:, :],
                                                op0=ALU.mult, op1=ALU.add))
            link(nc.vector.tensor_copy(rec[:, :, 1].bitcast(I32), ot_i[:, :]))
            link(nc.vector.tensor_copy(rec[:, :, 2], w_in[:, :]))


def stage_rank_buckets(c, tag, bucket, cols, n_buckets, group, q, ends):
    nc = c.nc
    with ExitStack() as s:
        sb = lambda n, shape: s.enter_context(nc.sbuf_tensor(f"{tag}_{n}", shape, F32))
        is_b, run = sb("is_b", [P, cols]), sb("run", [P, cols])
        count, groups, off = sb("count", [P, n_buckets]), sb("groups", [P, n_buckets]), sb("off", [P, n_buckets])
        ps = bank(c, s, tag + "_ps")[0:P, 0:2 * n_buckets].rearrange("p (a b) -> p a b", a=2)
        counted, chain, summed, ranked = (c.semaphore(f"{tag}_{n}")
                                          for n in ("counted", "chain", "summed", "ranked"))
        block = s.enter_context(nc.Block())

        @block.vector
        def _(dve):
            with dve.Fori(0, n_buckets) as b:
                dve.wait_ge(counted, b)
                nc.vector.tensor_scalar(is_b[:, :], bucket[:, :], c.iota[0:P, ds(b, 1)], 0.0, ALU.is_equal, ALU.add,
                                        accum_out=count[:, ds(b, 1)]).then_inc(counted, 1)
            dve.wait_ge(summed, 1)
            link = linker(dve, chain)
            link(nc.vector.tensor_scalar(groups[:, :], ps[:, 1, :], 1.0 / group, (group - 1) / (2.0 * group),
                                         ALU.mult, ALU.add))
            link(nc.vector.tensor_scalar(groups[:, :], groups[:, :], ROUND, ROUND, ALU.add, ALU.subtract))
            link(nc.vector.tensor_tensor_scan(ends[:, :], c.ones[0:P, 0:n_buckets], groups[:, :], 0.0, ALU.mult, ALU.add))
            link(nc.vector.tensor_tensor(off[:, :], ends[:, :], groups[:, :], ALU.subtract))
            link(nc.vector.scalar_tensor_tensor(out=off[:, :], in0=off[:, :], scalar=float(group), in1=ps[:, 0, :],
                                                op0=ALU.mult, op1=ALU.add))
            link(nc.vector.memset(q[:, :], 0.0))
            with dve.Fori(0, n_buckets) as b:
                link = linker(dve, ranked, base=b * 3)
                link(nc.vector.tensor_scalar(is_b[:, :], bucket[:, :], c.iota[0:P, ds(b, 1)], None, ALU.is_equal))
                dve.nop(nofuse=True)
                link(nc.vector.tensor_tensor_scan(run[:, :], c.ones[0:P, 0:1].broadcast_to([P, cols]), is_b[:, :],
                                                  off[:, ds(b, 1)], ALU.mult, ALU.add))
                dve.nop(nofuse=True)
                link(nc.vector.copy_predicated(q[:, :], is_b[:, :].bitcast(I32), run[:, :]))
                dve.nop(nofuse=True)
            nc.vector.tensor_scalar(q[:, :], q[:, :], -1.0, None, ALU.add).then_inc(chain, 1)

        @block.tensor
        def _(pe):
            pe.wait_ge(counted, n_buckets)
            nc.tensor.matmul(ps[:, 0, :], c.before[0:P, 0:P], count[:, :], start=True, stop=True)
            nc.tensor.matmul(ps[:, 1, :], c.ones[0:P, 0:P], count[:, :], start=True, stop=True).then_inc(summed, 1)


def stage_bucket_table(c, tag, ends, n_buckets, n_groups, table):
    nc = c.nc
    with ExitStack() as s:
        acc = s.enter_context(nc.sbuf_tensor(tag + "_acc", [1, n_groups], F32))
        chain = c.semaphore(tag + "_chain")
        block = s.enter_context(nc.Block())

        @block.vector
        def _(dve):
            nc.vector.memset(acc[:, :], 0.0).then_inc(chain, 1)
            with dve.Fori(0, n_buckets - 1) as b:
                dve.wait_ge(chain, b + 1)
                nc.vector.scalar_tensor_tensor(out=acc[:, :], in0=c.iota[0:1, 0:n_groups], scalar=ends[0:1, ds(b, 1)],
                                               in1=acc[:, :], op0=ALU.is_ge, op1=ALU.add).then_inc(chain, 1)
            dve.wait_ge(chain, n_buckets)
            nc.vector.tensor_copy(table[:, :], acc[:, :]).then_inc(chain, 1)


def stage_scatter_records(c, tag, rec, q, rows, table_sb):
    nc = c.nc
    W = 8
    with ExitStack() as s:
        sb = lambda n, shape, dt=F32: s.enter_context(nc.sbuf_tensor(f"{tag}_{n}", shape, dt))
        slot, place, place_i = sb("slot", [P, EC]), sb("place", [P, EC]), sb("place_i", [P, EC], I32)
        idx = sb("idx", [P, 2, W], I32)
        put = sb("put", [P, 2, W, 4])
        fill = sb("fill", [S, SLOTS, 4])
        sem = lambda n: c.semaphore(f"{tag}_{n}")
        chain, fill_ready, filled, staged, read = (sem(n) for n in ("chain", "fill_ready", "filled", "staged", "read"))
        scattered = [sem(f"scattered{h}") for h in range(2)]
        block = s.enter_context(nc.Block())

        @block.sync
        def _(sp):
            sp.wait_ge(fill_ready, 2)
            sp.dma_start(rows.rearrange("(r j) f -> r j f", r=S), fill[:, :, :]).then_inc(filled, 16)
            for h in range(2):
                sp.wait_ge(scattered[h], 16 * EC // 2)
            sp.dma_start(table_sb[:, :, :], rows.rearrange("(r j) f -> r j f", r=S)).then_inc(read, 16)
            sp.wait_ge(read, 16)

        @block.vector
        def _(dve):
            link = linker(dve, chain)
            nc.vector.memset(fill[:, :, :], 0.0).then_inc(fill_ready, 1)
            dve.wait_ge(fill_ready, 1)
            nc.vector.memset(fill[:, :, 0], -1.0).then_inc(fill_ready, 1)
            link(nc.vector.tensor_scalar(slot[:, :], q[:, :], 1.0 / S, -(S - 1) / (2.0 * S), ALU.mult, ALU.add))
            link(nc.vector.tensor_scalar(slot[:, :], slot[:, :], ROUND, ROUND, ALU.add, ALU.subtract))
            link(nc.vector.scalar_tensor_tensor(out=place[:, :], in0=slot[:, :], scalar=-float(S), in1=q[:, :],
                                                op0=ALU.mult, op1=ALU.add))
            link(nc.vector.scalar_tensor_tensor(out=place[:, :], in0=place[:, :], scalar=float(SLOTS),
                                                in1=slot[:, :], op0=ALU.mult, op1=ALU.add))
            link(nc.vector.tensor_copy(place_i[:, :], place[:, :]))
            with dve.Fori(0, EC // (2 * W)) as i:
                for h in range(2):
                    wait_slot(dve, scattered[h], i * (16 * W))
                    at = i * (2 * W) + h * W
                    nc.vector.tensor_copy(idx[:, h, :], place_i[:, ds(at, W)]).then_inc(staged, 1)
                    nc.vector.tensor_copy(put[:, h, :, :], rec[:, ds(at, W), :]).then_inc(staged, 1)

        @block.gpsimd
        def _(pool):
            pool.wait_ge(filled, 16)
            with pool.Fori(0, EC // (2 * W)) as i:
                for h in range(2):
                    wait_slot(pool, staged, i * 4 + 2 * h + 2)
                    for k in range(W):
                        nc.gpsimd.indirect_dma_start(
                            out=rows, out_offset=bass.IndirectOffsetOnAxis(ap=idx[:, h, k:k + 1], axis=0),
                            in_=put[:, h, k, :], in_offset=None).then_inc(scattered[h], 16)


def stage_aggregate(c, tag, table_sb, tiles_of, values, width, acc, weighted):
    nc = c.nc
    G = 10
    HG = G // 2
    with ExitStack() as s:
        sb = lambda n, shape, dt=F32: s.enter_context(nc.sbuf_tensor(f"{tag}_{n}", shape, dt))
        idx = sb("idx", [S, 2, HG], I32)
        got = sb("got", [S, G, width])
        hot = sb("hot", [S, G, P])
        ps = [bank(c, s, f"{tag}_ps{b}")[0:P, 0:width] for b in range(HG)]
        sem = lambda n: c.semaphore(f"{tag}_{n}")
        staged, hot_ready, summed, added = (sem(n) for n in ("staged", "hot_ready", "summed", "added"))
        gathered = [sem(f"gathered{k}") for k in range(G)]
        block = s.enter_context(nc.Block())
        n_iter = SLOTS // G

        @block.scalar
        def _(act):
            with act.Fori(0, n_iter) as i:
                for h in range(2):
                    for k in range(HG):
                        act.wait_ge(gathered[h * HG + k], i * 16)
                    act.nop(nofuse=True)
                    nc.scalar.copy(idx[:, h, :], table_sb[:, ds(i * G + h * HG, HG), 1].bitcast(I32)).then_inc(staged, 1)

        @block.gpsimd
        def _(pool):
            with pool.Fori(0, n_iter) as i:
                for h in range(2):
                    wait_slot(pool, staged, i * 2 + h + 1)
                    wait_slot(pool, summed, i * G if h == 0 else i * G)
                    for k in range(HG):
                        nc.gpsimd.indirect_dma_start(
                            out=got[:, h * HG + k, :], out_offset=None, in_=values,
                            in_offset=bass.IndirectOffsetOnAxis(ap=idx[:, h, k:k + 1], axis=0),
                        ).then_inc(gathered[h * HG + k], 16)

        @block.vector
        def _(dve):
            def make_hot(i):
                wait_slot(dve, summed, i * G)
                for k in range(G):
                    j = i * G + k
                    if weighted:
                        nc.vector.tensor_scalar(hot[:, k, :], c.iota[0:S, 0:P],
                                                table_sb[:, ds(j, 1), 0], table_sb[:, ds(j, 1), 2],
                                                ALU.is_equal, ALU.mult).then_inc(hot_ready, 1)
                    else:
                        nc.vector.tensor_scalar(hot[:, k, :], c.iota[0:S, 0:P], table_sb[:, ds(j, 1), 0], None,
                                                ALU.is_equal).then_inc(hot_ready, 1)

            with dve.Fori(0, n_iter) as i:
                make_hot(i)
                for k in range(G):
                    tile = dve.value_load(tiles_of[0:1, ds(i * G + k, 1)], min_val=0, max_val=T - 1)
                    dve.wait_ge(summed, i * G + k + 1)
                    wait_slot(dve, added, i * G + k)
                    here = acc[:, ds(tile, 1), :].rearrange("p a f -> p (a f)")
                    nc.vector.tensor_tensor(here, here, ps[k % HG][:, :], ALU.add).then_inc(added, 1)

        @block.tensor
        def _(pe):
            with pe.Fori(0, n_iter) as i:
                for k in range(G):
                    pe.wait_ge(gathered[k], i * 16 + 16)
                    pe.wait_ge(hot_ready, i * G + k + 1)
                    if k < HG:
                        wait_slot(pe, added, i * G)
                    else:
                        wait_slot(pe, added, i * G + k - HG + 1)
                    nc.tensor.matmul(ps[k % HG][:, :], hot[:, k, :], got[:, k, :], start=True, stop=True).then_inc(summed, 1)


def stage_normalise(c, tag, src, mean, rstd, dst):
    nc = c.nc
    with ExitStack() as s:
        done = c.semaphore(tag + "_done")
        block = s.enter_context(nc.Block())

        @block.vector
        def _(dve):
            with dve.Fori(0, T // U) as i:
                for k in range(U):
                    t = i * U + k
                    nc.vector.tensor_scalar(dst[:, ds(t, 1), :].rearrange("p a f -> p (a f)"),
                                            src[:, ds(t, 1), :].rearrange("p a f -> p (a f)"),
                                            mean[:, ds(t, 1)], rstd[:, ds(t, 1)],
                                            ALU.subtract, ALU.mult).then_inc(done, 1)


def stage_load(c, tag, pairs):
    nc = c.nc
    with ExitStack() as s:
        loaded = c.semaphore(tag + "_loaded")
        block = s.enter_context(nc.Block())

        @block.sync
        def _(sp):
            for dst, src in pairs:
                sp.dma_start(dst, src).then_inc(loaded, 16)
            sp.wait_ge(loaded, 16 * len(pairs))


def stage_route(c, tag, logits, bias, probs, top_i, weights):
    nc = c.nc
    E = EXPERTS
    with ExitStack() as s:
        sb = lambda n, shape, dt=F32: s.enter_context(nc.sbuf_tensor(f"{tag}_{n}", shape, dt))
        most, total, both = sb("most", [P, T]), sb("total", [P, T]), sb("both", [P, T])
        top_p = sb("top_p", [P, T, 8])
        raw = sb("raw", [P, T, 8], U32)
        chain, shifted, exped, top = (c.semaphore(f"{tag}_{n}") for n in ("chain", "shifted", "exped", "top"))
        block = s.enter_context(nc.Block())

        @block.vector
        def _(dve):
            link = linker(dve, chain)
            link(nc.vector.tensor_tensor(logits[:, :, :], logits[:, :, :],
                                         bias[0:P, :].unsqueeze(1).broadcast_to([P, T, E]), ALU.add))
            link(nc.vector.tensor_reduce(most[:, :], logits[:, :, :], AX.X, ALU.max))
            nc.vector.tensor_tensor(logits[:, :, :], logits[:, :, :], most[:, :].unsqueeze(2).broadcast_to([P, T, E]),
                                    ALU.subtract).then_inc(shifted, 1)
            dve.wait_ge(exped, 1)
            link(nc.vector.tensor_reduce(total[:, :], probs[:, :, :], AX.X, ALU.add))
            link(nc.vector.reciprocal(total[:, :], total[:, :]))
            link(nc.vector.tensor_tensor(probs[:, :, :], probs[:, :, :],
                                         total[:, :].unsqueeze(2).broadcast_to([P, T, E]), ALU.mult))
            for t in range(T):
                nc.vector.max(top_p[:, t, :], probs[:, t, :]).then_inc(top, 1)
            dve.wait_ge(top, T)
            for t in range(T):
                nc.vector.max_index(raw[:, t, :], top_p[:, t, :], probs[:, t, :]).then_inc(top, 1)
            link(nc.vector.tensor_tensor(both[:, :], top_p[:, :, 0], top_p[:, :, 1], ALU.add))
            link(nc.vector.reciprocal(both[:, :], both[:, :]))
            link(nc.vector.tensor_tensor(weights[:, :, :], top_p[:, :, 0:TOPK],
                                         both[:, :].unsqueeze(2).broadcast_to([P, T, TOPK]), ALU.mult))
            dve.wait_ge(top, 2 * T)
            nc.vector.tensor_copy(top_i[:, :, :], raw[:, :, 0:TOPK]).then_inc(chain, 1)

        @block.scalar
        def _(act):
            act.wait_ge(shifted, 1)
            nc.scalar.activation(probs[:, :, :], logits[:, :, :], ACT.Exp).then_inc(exped, 1)


def stage_dispatch(c, tag, src, mean, rstd, q, place, slots):
    nc = c.nc
    with ExitStack() as s:
        sb = lambda n, shape, dt=F32: s.enter_context(nc.sbuf_tensor(f"{tag}_{n}", shape, dt))
        pieces = BLOCKS + 1
        zero = sb("zero", [128, B * D // 128])
        rows = sb("rows", [P, U, D])
        idx = sb("idx", [P, U, TOPK], I32)
        sem = lambda n: c.semaphore(f"{tag}_{n}")
        zeroed, filled, staged, placed, cast = (sem(n) for n in ("zeroed", "filled", "staged", "placed", "cast"))
        block = s.enter_context(nc.Block())
        slots_v = slots.rearrange("(a p r) f -> a p (r f)", a=pieces, p=128)

        @block.sync
        def _(sp):
            sp.wait_ge(zeroed, 1)
            for a in range(pieces):
                sp.dma_start(slots_v[a], zero[:, :]).then_inc(filled, 16)

        @block.vector
        def _(dve):
            nc.vector.memset(zero[:, :], 0.0).then_inc(zeroed, 1)
            nc.vector.tensor_copy(place[:, :, :], q.rearrange("p (t e) -> p t e", e=TOPK)).then_inc(cast, 1)
            dve.wait_ge(cast, 1)
            with dve.Fori(0, T // U) as i:
                wait_slot(dve, placed, i * (16 * U * TOPK))
                nc.vector.tensor_copy(idx[:, :, :], place[:, ds(i * U, U), :]).then_inc(staged, 1)
                for k in range(U):
                    t = i * U + k
                    nc.vector.tensor_scalar(rows[:, k, :], src[:, ds(t, 1), :].rearrange("p a f -> p (a f)"),
                                            mean[:, ds(t, 1)], rstd[:, ds(t, 1)],
                                            ALU.subtract, ALU.mult).then_inc(staged, 1)

        @block.gpsimd
        def _(pool):
            pool.wait_ge(filled, 16 * pieces)
            with pool.Fori(0, T // U) as i:
                for k in range(U):
                    wait_slot(pool, staged, i * (U + 1) + k + 2)
                    for e in range(TOPK):
                        nc.gpsimd.indirect_dma_start(
                            out=slots, out_offset=bass.IndirectOffsetOnAxis(ap=idx[:, k, e:e + 1], axis=0),
                            in_=rows[:, k, :], in_offset=None).then_inc(placed, 16)
            pool.wait_ge(placed, 16 * T * TOPK)


def stage_expert_blocks(c, tag, slots, results, experts_of, w1, w2, gain, shift, bias1, bias2):
    nc = c.nc
    HC = H0 // 128
    KC = D // 128
    Q = B // 128
    assert BLOCKS % 2 == 0
    with ExitStack() as s:
        sb = lambda n, shape, dt=F32: s.enter_context(nc.sbuf_tensor(f"{tag}_{n}", shape, dt))
        w1_sb = [sb(f"w1_{b}", [128, KC, H0]) for b in range(2)]
        w2_sb = [sb(f"w2_{b}", [128, HC, D]) for b in range(2)]
        rows = [sb(f"rows_{b}", [128, Q, D]) for b in range(2)]
        rows_t = [sb(f"rows_t_{b}", [128, KC, B]) for b in range(2)]
        hidden = sb("hidden", [128, HC, B])
        y = [sb(f"y_{b}", [128, Q, D]) for b in range(2)]
        ps_t = bank(c, s, f"{tag}_ps_t")[:, 0:KC * B].rearrange("p (j n) -> p j n", j=KC)
        ps_h = [bank(c, s, f"{tag}_ps_h{b}")[:, 0:B] for b in range(4)]
        ps_y = [bank(c, s, f"{tag}_ps_y{b}")[:, 0:D] for b in range(Q)]
        sem = lambda n: c.semaphore(f"{tag}_{n}")
        turned, scaled, up, gelu_done, down, y_ready = (
            sem(n) for n in ("turned", "scaled", "up", "gelu_done", "down", "y_ready"))
        rows_in, w1_in, w2_in, y_out = ([sem(f"{n}{b}") for b in range(2)] for n in ("rows_in", "w1_in", "w2_in", "y_out"))
        block = s.enter_context(nc.Block())
        slots_v = slots.rearrange("(n q p) f -> n p q f", q=Q, p=128)
        results_v = results.rearrange("(n q p) f -> n p q f", q=Q, p=128)

        @block.sync
        def _(sp):
            def load_weights(n, b):
                e = sp.value_load(experts_of[0:1, ds(n, 1)], min_val=0, max_val=EXPERTS - 1)
                sp.dma_start(w1_sb[b][:, :, :], w1[ds(e, 1)].rearrange("a p j h -> (a p) j h")).then_inc(w1_in[b], 16)
                sp.dma_start(w2_sb[b][:, :, :], w2[ds(e, 1)].rearrange("a p j h -> (a p) j h")).then_inc(w2_in[b], 16)

            def load_rows(n, b):
                sp.dma_start(rows[b][:, :, :], slots_v[ds(n, 1)].rearrange("a p q f -> (a p) q f")).then_inc(rows_in[b], 16)

            for b in range(2):
                load_rows(b, b)
                load_weights(b, b)
            with sp.Fori(0, BLOCKS // 2 - 1) as i:
                for b in range(2):
                    n = i * 2 + b + 2
                    wait_slot(sp, turned, n - 1)
                    load_rows(n, b)
                    wait_slot(sp, down, (n - 1) * Q)
                    load_weights(n, b)
            sp.wait_ge(turned, BLOCKS - 1)
            load_rows(BLOCKS, 0)

        @block.vector
        def _(dve):
            def scale_rows(n, b):
                e = dve.value_load(experts_of[0:1, ds(n, 1)], min_val=0, max_val=EXPERTS - 1)
                wait_slot(dve, turned, n + 1)
                for j in range(KC):
                    last = nc.vector.tensor_scalar(rows_t[b][:, j, :], ps_t[:, j, :], gain[:, ds(e * KC + j, 1)],
                                                   shift[:, ds(e * KC + j, 1)], ALU.mult, ALU.add)
                last.then_inc(scaled, 1)

            scale_rows(0, 0)
            with dve.Fori(0, BLOCKS // 2) as i:
                for b in range(2):
                    n = i * 2 + b
                    scale_rows(n + 1, 1 - b)
                    e = dve.value_load(experts_of[0:1, ds(n, 1)], min_val=0, max_val=EXPERTS - 1)
                    wait_slot(dve, y_out[b], i * 16)
                    for q in range(Q):
                        wait_slot(dve, down, n * Q + q + 1)
                        nc.vector.tensor_tensor(y[b][:, q, :], ps_y[q], bias2[:, ds(e, 1), :].rearrange("p a f -> p (a f)"),
                                                ALU.add).then_inc(y_ready, 1)

        @block.scalar
        def _(act):
            with act.Fori(0, BLOCKS // 2) as i:
                for b in range(2):
                    n = i * 2 + b
                    e = act.value_load(experts_of[0:1, ds(n, 1)], min_val=0, max_val=EXPERTS - 1)
                    for h in range(HC):
                        wait_slot(act, up, n * HC + h + 1)
                        nc.scalar.activation(hidden[:, h, :], ps_h[h % 4], ACT.Gelu,
                                             bias=bias1[:, ds(e * HC + h, 1)]).then_inc(gelu_done, 1)

        @block.gpsimd
        def _(pool):
            with pool.Fori(0, BLOCKS // 2) as i:
                for b in range(2):
                    n = i * 2 + b
                    wait_slot(pool, y_ready, (n + 1) * Q)
                    pool.dma_start(results_v[ds(n, 1)].rearrange("a p q f -> (a p) q f"), y[b][:, :, :]).then_inc(y_out[b], 16)
            for b in range(2):
                pool.wait_ge(y_out[b], 16 * BLOCKS // 2)

        @block.tensor
        def _(pe):
            def turn_rows(b, arrived):
                wait_slot(pe, rows_in[b], arrived)
                for q in range(Q):
                    for j in range(KC):
                        last = nc.tensor.transpose(ps_t[:, j, q * 128:(q + 1) * 128],
                                                   rows[b][:, q, j * 128:(j + 1) * 128], c.ident[:, :])
                last.then_inc(turned, 1)

            turn_rows(0, 16)
            with pe.Fori(0, BLOCKS // 2) as i:
                for b in range(2):
                    n = i * 2 + b
                    pe.wait_ge(w1_in[b], i * 16 + 16)
                    wait_slot(pe, scaled, n + 1)
                    for h in range(HC):
                        wait_slot(pe, gelu_done, n * HC if h < 4 else n * HC + h - 3)
                        for j in range(KC):
                            last = nc.tensor.matmul(ps_h[h % 4], w1_sb[b][:, j, h * 128:(h + 1) * 128], rows_t[b][:, j, :],
                                                    start=(j == 0), stop=(j == KC - 1))
                        last.then_inc(up, 1)
                    turn_rows(1 - b, i * 16 + 16 + 16 * b)
                    pe.wait_ge(w2_in[b], i * 16 + 16)
                    pe.wait_ge(y_ready, n * Q)
                    wait_slot(pe, gelu_done, (n + 1) * HC)
                    for q in range(Q):
                        for h in range(HC):
                            last = nc.tensor.matmul(ps_y[q], hidden[:, h, q * 128:(q + 1) * 128], w2_sb[b][:, h, :],
                                                    start=(h == 0), stop=(h == HC - 1))
                        last.then_inc(down, 1)


def stage_combine(c, tag, results, place, weights, acc):
    nc = c.nc
    with ExitStack() as s:
        sb = lambda n, shape, dt=F32: s.enter_context(nc.sbuf_tensor(f"{tag}_{n}", shape, dt))
        got = sb("got", [P, U, TOPK, D])
        idx = sb("idx", [P, U, TOPK], I32)
        sem = lambda n: c.semaphore(f"{tag}_{n}")
        staged, added = sem("staged"), sem("added")
        gathered = [sem(f"gathered{k}") for k in range(U)]
        block = s.enter_context(nc.Block())

        @block.scalar
        def _(act):
            with act.Fori(0, T // U) as i:
                wait_slot(act, added, i * (U * TOPK))
                nc.scalar.copy(idx[:, :, :], place[:, ds(i * U, U), :]).then_inc(staged, 1)

        @block.gpsimd
        def _(pool):
            with pool.Fori(0, T // U) as i:
                wait_slot(pool, staged, i + 1)
                for k in range(U):
                    for e in range(TOPK):
                        nc.gpsimd.indirect_dma_start(
                            out=got[:, k, e, :], out_offset=None, in_=results,
                            in_offset=bass.IndirectOffsetOnAxis(ap=idx[:, k, e:e + 1], axis=0)).then_inc(gathered[k], 16)

        @block.vector
        def _(dve):
            with dve.Fori(0, T // U) as i:
                for k in range(U):
                    t = i * U + k
                    here = acc[:, ds(t, 1), :].rearrange("p a f -> p (a f)")
                    wait_slot(dve, gathered[k], (i + 1) * (16 * TOPK))
                    for e in range(TOPK):
                        wait_slot(dve, added, (i * U + k) * TOPK + e)
                        nc.vector.scalar_tensor_tensor(
                            out=here, in0=got[:, k, e, :], scalar=weights[:, ds(t, 1), e], in1=here,
                            op0=ALU.mult, op1=ALU.add).then_inc(added, 1)


def stage_degree(c, tag, rec, tile_of, deg):
    nc = c.nc
    W = 10
    with ExitStack() as s:
        sb = lambda n, shape, dt=BF16: s.enter_context(nc.sbuf_tensor(f"{tag}_{n}", shape, dt))
        of_row, of_tile = sb("of_row", [P, 2, W, P]), sb("of_tile", [P, 2, W, T])
        none = sb("none", [P, P])
        ps = bank(c, s, f"{tag}_ps")[0:P, 0:T]
        zeroed, made, used, whole = (c.semaphore(f"{tag}_{n}") for n in ("zeroed", "made", "used", "whole"))
        block = s.enter_context(nc.Block())

        @block.vector
        def _(dve):
            nc.vector.memset(none[:, :], 0.0).then_inc(zeroed, 1)
            with dve.Fori(0, EC // (2 * W)) as i:
                for h in range(2):
                    at = i * (2 * W) + h * W
                    wait_slot(dve, used, i * 2)
                    nc.vector.tensor_tensor(of_row[:, h, :, :], rec[:, ds(at, W), 0].unsqueeze(2).broadcast_to([P, W, P]),
                                            c.iota[0:P, 0:P].unsqueeze(1).broadcast_to([P, W, P]), ALU.is_equal)
                    nc.vector.tensor_tensor(of_tile[:, h, :, :], tile_of[:, ds(at, W)].unsqueeze(2).broadcast_to([P, W, T]),
                                            c.iota[0:P, 0:T].unsqueeze(1).broadcast_to([P, W, T]),
                                            ALU.is_equal).then_inc(made, 1)
            dve.wait_ge(whole, 1)
            nc.vector.tensor_copy(deg[:, :], ps).then_inc(made, 1)

        @block.tensor
        def _(pe):
            pe.wait_ge(zeroed, 1)
            nc.tensor.matmul(ps, none[:, 0:P], none[:, 0:T], start=True, stop=False)
            with pe.Fori(0, EC // (2 * W)) as i:
                for h in range(2):
                    wait_slot(pe, made, i * 2 + h + 1)
                    for k in range(W):
                        last = nc.tensor.matmul(ps, of_row[:, h, k, :], of_tile[:, h, k, :], start=False, stop=False)
                    last.then_inc(used, 1)
            nc.tensor.matmul(ps, none[:, 0:P], none[:, 0:T], start=False, stop=True).then_inc(whole, 1)


def stage_degree_norm(c, tag, deg, dinv):
    nc = c.nc
    with ExitStack() as s:
        root = s.enter_context(nc.sbuf_tensor(tag + "_root", [P, T], F32))
        chain, rooted = (c.semaphore(f"{tag}_{n}") for n in ("chain", "rooted"))
        block = s.enter_context(nc.Block())

        @block.vector
        def _(dve):
            nc.vector.tensor_scalar(deg[:, :], deg[:, :], 1.0, 1.0, ALU.add, ALU.max).then_inc(chain, 1)
            dve.wait_ge(rooted, 1)
            nc.vector.reciprocal(dinv[:, :], root[:, :]).then_inc(chain, 1)

        @block.scalar
        def _(act):
            act.wait_ge(chain, 1)
            nc.scalar.activation(root[:, :], deg[:, :], ACT.Sqrt).then_inc(rooted, 1)


def stage_batch_norm(c, tag, acc, width, dinv, bias, gain, shift):
    nc = c.nc
    with ExitStack() as s:
        sb = lambda n, shape: s.enter_context(nc.sbuf_tensor(f"{tag}_{n}", shape, F32))
        square, part = sb("square", [P, T, width]), sb("part", [P, width])
        mean, var, std = sb("mean", [P, width]), sb("var", [P, width]), sb("std", [P, width])
        ps = bank(c, s, f"{tag}_ps")[0:P, 0:width]
        chain, part_ready, summed, var_ready, std_ready = (
            c.semaphore(f"{tag}_{n}") for n in ("chain", "part_ready", "summed", "var_ready", "std_ready"))
        block = s.enter_context(nc.Block())
        rows = lambda v: v[0:P, 0:width].unsqueeze(1).broadcast_to([P, T, width])

        @block.vector
        def _(dve):
            V = nc.vector
            link = linker(dve, chain)
            link(V.tensor_tensor(acc[:, :, :], acc[:, :, :], dinv[:, :].unsqueeze(2).broadcast_to([P, T, width]), ALU.mult))
            link(V.tensor_tensor(acc[:, :, :], acc[:, :, :], rows(bias), ALU.add))
            V.tensor_reduce(part[:, :], acc[:, :, :].rearrange("p t f -> p f t"), AX.X, ALU.add).then_inc(part_ready, 1)
            dve.wait_ge(summed, 1)
            link(V.tensor_scalar(mean[:, :], ps, 1.0 / NODES, None, ALU.mult))
            link(V.tensor_tensor(acc[:, :, :], acc[:, :, :], rows(mean), ALU.subtract))
            link(V.tensor_tensor(square[:, :, :], acc[:, :, :], acc[:, :, :], ALU.mult))
            V.tensor_reduce(part[:, :], square[:, :, :].rearrange("p t f -> p f t"), AX.X, ALU.add).then_inc(part_ready, 1)
            dve.wait_ge(summed, 2)
            V.tensor_scalar(var[:, :], ps, 1.0 / NODES, BN_EPS, ALU.mult, ALU.add).then_inc(var_ready, 1)
            dve.wait_ge(std_ready, 1)
            link(V.reciprocal(var[:, :], std[:, :]))
            link(V.tensor_tensor(var[:, :], var[:, :], gain[0:P, :], ALU.mult))
            link(V.tensor_tensor(acc[:, :, :], acc[:, :, :], rows(var), ALU.mult))
            link(V.tensor_tensor(acc[:, :, :], acc[:, :, :], rows(shift), ALU.add))
            link(V.tensor_scalar(acc[:, :, :], acc[:, :, :], 0.0, None, ALU.max))

        @block.scalar
        def _(act):
            act.wait_ge(var_ready, 1)
            nc.scalar.activation(std[:, :], var[:, :], ACT.Sqrt).then_inc(std_ready, 1)

        @block.tensor
        def _(pe):
            for n in range(2):
                pe.wait_ge(part_ready, n + 1)
                nc.tensor.matmul(ps, c.ones[0:P, 0:P], part[:, :], start=True, stop=True).then_inc(summed, 1)


def stage_fc_end(c, tag, fc, bias, acc):
    nc = c.nc
    with ExitStack() as s:
        chain = c.semaphore(tag + "_chain")
        block = s.enter_context(nc.Block())

        @block.vector
        def _(dve):
            link = linker(dve, chain)
            link(nc.vector.tensor_tensor(fc[:, :, :], fc[:, :, :], bias[0:P, :].unsqueeze(1).broadcast_to([P, T, D]), ALU.add))
            link(nc.vector.scalar_tensor_tensor(out=acc[:, :, :], in0=fc[:, :, :], scalar=0.0, in1=acc[:, :, :],
                                                op0=ALU.max, op1=ALU.add))


def stage_pick_experts(c, tag, rows_t, router, bias, picked, picked_w):
    nc = c.nc
    E = EXPERTS
    capacity = float(-(-NODES * 125 // (100 * E)))
    with ExitStack() as s:
        sb = lambda n, shape, dt=F32: s.enter_context(nc.sbuf_tensor(f"{tag}_{n}", shape, dt))
        mean = sb("mean", [128, 2])
        z, p, load, one, top, top_w = (sb("z", [1, E]), sb("p", [1, E]), sb("load", [1, E]), sb("one", [1, 1]),
                                       sb("top", [1, 8]), sb("top_w", [1, TOPK]))
        top_i = sb("top_i", [1, 8], U32)
        ps_l, ps_w = bank(c, s, f"{tag}_ps_l")[0:1, 0:E], bank(c, s, f"{tag}_ps_w")[:, 0:TOPK]
        chain, mean_ready, product, to_exp, exped, weights_ready = (
            c.semaphore(f"{tag}_{n}")
            for n in ("chain", "mean_ready", "product", "to_exp", "exped", "weights_ready"))
        block = s.enter_context(nc.Block())

        @block.vector
        def _(dve):
            V = nc.vector
            link = linker(dve, chain)
            rounds = [0]

            def softmax(src, out, n):
                rounds[0] += 1
                link(V.tensor_reduce(one[:, :], src[0:1, 0:n], AX.X, ALU.max))
                V.tensor_scalar(z[0:1, 0:n], src[0:1, 0:n], one[0:1, 0:1], None, ALU.subtract).then_inc(to_exp, 1)
                dve.wait_ge(exped, rounds[0])
                link(V.tensor_reduce(one[:, :], p[0:1, 0:n], AX.X, ALU.add))
                link(V.reciprocal(one[:, :], one[:, :]))
                link(V.tensor_scalar(out[0:1, 0:n], p[0:1, 0:n], one[0:1, 0:1], None, ALU.mult))

            link(V.tensor_reduce(mean[:, :], rows_t[:, :, :], AX.X, ALU.add))
            V.tensor_scalar(mean[:, :], mean[:, :], 1.0 / NODES, None, ALU.mult).then_inc(mean_ready, 1)
            dve.wait_ge(product, 1)
            link(V.tensor_tensor(p[:, :], ps_l, bias[0:1, :], ALU.add))
            softmax(p, p, E)
            link(V.tensor_scalar(load[:, :], p[:, :], float(NODES), None, ALU.mult))
            link(V.reciprocal(load[:, :], load[:, :]))
            link(V.tensor_scalar(load[:, :], load[:, :], capacity, 1.0, ALU.mult, ALU.min))
            link(V.tensor_tensor(p[:, :], p[:, :], load[:, :], ALU.mult))
            softmax(p, p, E)
            link(V.max(top[:, :], p[:, :]))
            link(V.max_index(top_i[:, :], top[:, :], p[:, :]))
            link(V.tensor_copy(picked[:, :], top_i[0:1, 0:TOPK]))
            softmax(top, top_w, TOPK)
            link(V.tensor_copy(top_w[:, :], top_w[:, :]))
            dve.nop(nofuse=True)
            V.tensor_copy(one[:, :], one[:, :]).then_inc(weights_ready, 1)
            dve.wait_ge(product, 2)
            V.tensor_copy(picked_w[:, :], ps_w).then_inc(chain, 1)

        @block.scalar
        def _(act):
            for n, width in enumerate((E, E, TOPK)):
                act.wait_ge(to_exp, n + 1)
                nc.scalar.activation(p[0:1, 0:width], z[0:1, 0:width], ACT.Exp).then_inc(exped, 1)

        @block.tensor
        def _(pe):
            pe.wait_ge(mean_ready, 1)
            for j in range(2):
                last = nc.tensor.matmul(ps_l, mean[:, j:j + 1], router[:, j, :], start=(j == 0), stop=(j == 1))
            last.then_inc(product, 1)
            pe.wait_ge(weights_ready, 1)
            nc.tensor.matmul(ps_w, c.ones[0:1, :], top_w[:, :], start=True, stop=True).then_inc(product, 1)


def stage_shared_ffn(c, tag, rows_t, picked, picked_w, w1, w2, b1, b2, mean, rstd, out_z):
    nc = c.nc
    FC, KC = H1 // 128, D // 128
    F = TOPK * FC
    with ExitStack() as s:
        sb = lambda n, shape, dt=F32: s.enter_context(nc.sbuf_tensor(f"{tag}_{n}", shape, dt))
        w1_sb, w2_sb = sb("w1", [128, TOPK, KC, H1]), sb("w2", [128, F, D])
        b1_sb, b2_sb = sb("b1", [128, TOPK, FC]), sb("b2", [P, TOPK, D])
        hidden = [sb(f"hidden{b}", [128, F, P]) for b in range(2)]
        ps_h = [bank(c, s, f"{tag}_ps_h{b}")[:, 0:P] for b in range(4)]
        ps_y = [bank(c, s, f"{tag}_ps_y{b}")[0:P, 0:D] for b in range(2)]
        sem = lambda n: c.semaphore(f"{tag}_{n}")
        w1_in, w2_in, b2_in, chain, w2_scaled, up, gelu_done, down, taken, normal = (
            sem(n) for n in ("w1_in", "w2_in", "b2_in", "chain", "w2_scaled", "up", "gelu_done", "down", "taken", "normal"))
        block = s.enter_context(nc.Block())

        @block.sync
        def _(sp):
            for k in range(TOPK):
                e = sp.value_load(picked[0:1, k:k + 1], min_val=0, max_val=EXPERTS - 1)
                sp.dma_start(w1_sb[:, k, :, :], w1[ds(e, 1)].rearrange("a p j h -> (a p) j h")).then_inc(w1_in, 16)
                sp.dma_start(b1_sb[:, k, :], b1[ds(e, 1)].rearrange("a p j -> (a p) j")).then_inc(w1_in, 16)
                sp.dma_start(w2_sb[:, k * FC:(k + 1) * FC, :], w2[ds(e, 1)].rearrange("a p j h -> (a p) j h")).then_inc(w2_in, 16)
                sp.dma_start(b2_sb[:, k, :], b2[ds(e, 1), :].broadcast_to([P, D])).then_inc(b2_in, 16)

        @block.vector
        def _(dve):
            V = nc.vector
            link = linker(dve, chain)
            dve.wait_ge(w2_in, 32)
            for k in range(TOPK):
                V.tensor_scalar(w2_sb[:, k * FC:(k + 1) * FC, :], w2_sb[:, k * FC:(k + 1) * FC, :],
                                picked_w[:, k:k + 1], None, ALU.mult).then_inc(w2_scaled, 1)
            dve.wait_ge(b2_in, 32)
            link(V.tensor_scalar(b2_sb[:, 0, :], b2_sb[:, 0, :], picked_w[0:P, 0:1], None, ALU.mult))
            link(V.scalar_tensor_tensor(out=b2_sb[:, 0, :], in0=b2_sb[:, 1, :], scalar=picked_w[0:P, 1:2],
                                        in1=b2_sb[:, 0, :], op0=ALU.mult, op1=ALU.add))

            def take(t, b):
                here = out_z[:, ds(t, 1), :].rearrange("p a f -> p (a f)")
                V.tensor_scalar(here, c.x[:, ds(t, 1), :].rearrange("p a f -> p (a f)"), mean[:, ds(t, 1)],
                                rstd[:, ds(t, 1)], ALU.subtract, ALU.mult).then_inc(normal, 1)
                wait_slot(dve, normal, t * 2 + 1)
                V.tensor_tensor(here, here, b2_sb[:, 0, :], ALU.add).then_inc(normal, 1)
                dve.wait_ge(normal, t * 2 + 2)
                wait_slot(dve, down, t + 1)
                V.tensor_tensor(here, here, ps_y[b], ALU.add).then_inc(taken, 1)

            with dve.Fori(0, T // 2) as i:
                for b in range(2):
                    take(i * 2 + b, b)
            take(T - 1, 0)

        @block.scalar
        def _(act):
            act.wait_ge(w1_in, 64)

            def gelu(t, b):
                for f in range(F):
                    wait_slot(act, up, t * F + f + 1)
                    nc.scalar.activation(hidden[b][:, f, :], ps_h[f % 4], ACT.Gelu,
                                         bias=b1_sb[:, f // FC, f % FC:f % FC + 1]).then_inc(gelu_done, 1)

            with act.Fori(0, T // 2) as i:
                for b in range(2):
                    gelu(i * 2 + b, b)
            gelu(T - 1, 0)

        @block.tensor
        def _(pe):
            def rise(t, first=False):
                for f in range(F):
                    if not first or f >= 4:
                        wait_slot(pe, gelu_done, t * F if f < 4 else t * F + f - 3)
                    for j in range(KC):
                        last = nc.tensor.matmul(ps_h[f % 4], w1_sb[:, f // FC, j, (f % FC) * 128:(f % FC + 1) * 128],
                                                rows_t[:, j, ds(t * P, P)], start=(j == 0), stop=(j == KC - 1))
                    last.then_inc(up, 1)

            def fall(t, b):
                wait_slot(pe, taken, i_even(t, b))
                wait_slot(pe, gelu_done, (t + 1) * F)
                for f in range(F):
                    last = nc.tensor.matmul(ps_y[b], hidden[b][:, f, :], w2_sb[:, f, :], start=(f == 0), stop=(f == F - 1))
                last.then_inc(down, 1)

            def i_even(t, b):
                return t if b == 0 else t - 1

            pe.wait_ge(w1_in, 64)
            rise(0, first=True)
            pe.wait_ge(w2_scaled, TOPK)
            with pe.Fori(0, T // 2) as i:
                for b in range(2):
                    rise(i * 2 + b + 1)
                    fall(i * 2 + b, b)
            fall(T - 1, 0)


def stage_last(c, tag, z, mean, rstd, gamma, beta, out):
    nc = c.nc
    with ExitStack() as s:
        done, stored = (c.semaphore(f"{tag}_{n}") for n in ("done", "stored"))
        block = s.enter_context(nc.Block())

        @block.vector
        def _(dve):
            V = nc.vector
            with dve.Fori(0, T) as t:
                here = z[:, ds(t, 1), :].rearrange("p a f -> p (a f)")
                link = linker(dve, done, base=t * 4)
                link(V.tensor_scalar(here, here, mean[:, ds(t, 1)], rstd[:, ds(t, 1)], ALU.subtract, ALU.mult))
                dve.nop(nofuse=True)
                link(V.tensor_tensor(here, here, gamma[0:P, :], ALU.mult))
                dve.nop(nofuse=True)
                link(V.tensor_tensor(here, here, beta[0:P, :], ALU.add))
                dve.nop(nofuse=True)
                link(V.tensor_tensor(here, here, c.x[:, ds(t, 1), :].rearrange("p a f -> p (a f)"), ALU.add))
                dve.nop(nofuse=True)

        @block.sync
        def _(sp):
            out_v = out.rearrange("(t p) f -> p t f", p=P)
            for g in range(T // U):
                sp.wait_ge(done, 4 * U * (g + 1))
                sp.dma_start(out_v[:, g * U:(g + 1) * U, :], z[:, g * U:(g + 1) * U, :]).then_inc(stored, 16)
            sp.wait_ge(stored, 16 * T // U)


def stage_copy(c, tag, dst, src):
    nc = c.nc
    with ExitStack() as s:
        copied = c.semaphore(tag + "_copied")
        block = s.enter_context(nc.Block())

        @block.vector
        def _(dve):
            nc.vector.tensor_copy(dst, src).then_inc(copied, 1)


def flat(ap):
    return ap.rearrange("p a f -> p (a f)")


def layer0_graph(c, scratch, mean, rstd):
    nc, args = c.nc, c.args
    stage_norm_stats(c, "g0", c.x, mean, rstd)
    with ExitStack() as s:
        sb = lambda n, shape, dt=F32: s.enter_context(nc.sbuf_tensor(n, shape, dt))
        w, support = sb("g0_w", [128, 2, D]), sb("g0_support", [P, T, D])
        stage_load(c, "g0_w", [(w[:, :, :], args["g0_w"].rearrange("(j p) m -> p j m", p=128))])
        stage_project(c, "g0", c.x, D, w, D,
                      lambda t, ps: [lambda: nc.vector.tensor_copy(flat(support[:, ds(t, 1), :]), ps)],
                      norm=(mean, rstd), dram=(scratch["support"], support[:, :, :]))
    with ExitStack() as s:
        sb = lambda n, shape, dt=F32: s.enter_context(nc.sbuf_tensor(n, shape, dt))
        table, tiles_of = sb("g0_table", [S, SLOTS, 4]), sb("g0_tiles_of", [1, SLOTS], I32)
        with ExitStack() as s2:
            sb2 = lambda n, shape, dt=F32: s2.enter_context(nc.sbuf_tensor(n, shape, dt))
            rec, tile_of_edge = sb2("g0_rec", [P, EC, 4]), sb2("g0_tile", [P, EC])
            q, ends = sb2("g0_q", [P, EC]), sb2("g0_ends", [P, T])
            stage_edge_records(c, "g0r", args["src"], args["dst"], args["edge_weight"], rec, tile_of_edge)
            stage_rank_buckets(c, "g0k", tile_of_edge, EC, T, S, q, ends)
            stage_bucket_table(c, "g0t", ends, T, SLOTS, tiles_of)
            stage_scatter_records(c, "g0s", rec, q, scratch["rows0"], table)
        stage_aggregate(c, "g0a", table, tiles_of, scratch["support"], D, c.x, weighted=True)


def layer0_ffn(c, scratch, mean, rstd):
    nc, args = c.nc, c.args
    stage_norm_stats(c, "f0", c.x, mean, rstd)
    with ExitStack() as s:
        sb = lambda n, shape, dt=F32: s.enter_context(nc.sbuf_tensor(n, shape, dt))
        place, weights = sb("f0_place", [P, T, TOPK], I32), sb("f0_weights", [P, T, TOPK])
        experts_of = sb("f0_experts_of", [1, BLOCKS + 1], I32)
        with ExitStack() as s2:
            sb2 = lambda n, shape, dt=F32: s2.enter_context(nc.sbuf_tensor(n, shape, dt))
            xt, router, bias = sb2("f0_xt", [P, T, D]), sb2("f0_router", [128, 2, EXPERTS]), sb2("f0_bias", [128, EXPERTS])
            mean2, rstd2 = sb2("f0_mean2", [P, T]), sb2("f0_rstd2", [P, T])
            logits, probs, top_i = sb2("f0_logits", [P, T, EXPERTS]), sb2("f0_probs", [P, T, EXPERTS]), sb2("f0_top_i", [P, T, TOPK])
            q, ends = sb2("f0_q", [P, T * TOPK]), sb2("f0_ends", [P, EXPERTS])
            stage_load(c, "f0_router", [(router[:, :, :], args["f0_wr"].rearrange("(j p) m -> p j m", p=128)),
                                        (bias[:, :], row_to_all(args["f0_br"], 128))])
            stage_normalise(c, "f0n", c.x, mean, rstd, xt)
            stage_norm_stats(c, "f0b", xt, mean2, rstd2)
            stage_project(c, "f0", xt, D, router, EXPERTS,
                          lambda t, ps: [lambda: nc.vector.tensor_copy(flat(logits[:, ds(t, 1), :]), ps)])
            stage_route(c, "f0r", logits, bias, probs, top_i, weights)
            stage_rank_buckets(c, "f0k", flat(top_i[:, :, :]), T * TOPK, EXPERTS, B, q, ends)
            stage_bucket_table(c, "f0t", ends, EXPERTS, BLOCKS + 1, experts_of)
            stage_dispatch(c, "f0d", xt, mean2, rstd2, q[:, :], place, scratch["slots"])
        with ExitStack() as s2:
            sb2 = lambda n, shape, dt=F32: s2.enter_context(nc.sbuf_tensor(n, shape, dt))
            gain, shift = sb2("f0_gain", [128, EXPERTS * 2]), sb2("f0_shift", [128, EXPERTS * 2])
            bias1, bias2 = sb2("f0_bias1", [128, EXPERTS * H0 // 128]), sb2("f0_bias2", [128, EXPERTS, D])
            stage_load(c, "f0_params", [
                (gain[:, :], args["f0_g"]), (shift[:, :], args["f0_b"]), (bias1[:, :], args["f0_b1"]),
                (flat(bias2[:, :, :]), row_to_all(args["f0_b2"].rearrange("e d -> (e d)"), 128))])
            stage_expert_blocks(c, "f0e", scratch["slots"], scratch["results"], experts_of, args["f0_w1"], args["f0_w2"],
                                gain, shift, bias1, bias2)
        stage_combine(c, "f0c", scratch["results"], place, weights, c.x)


def layer1_graph(c, scratch, mean, rstd):
    nc, args = c.nc, c.args
    V = nc.vector
    stage_norm_stats(c, "g1", c.x, mean, rstd)
    with ExitStack() as s:
        sb = lambda n, shape, dt=F32: s.enter_context(nc.sbuf_tensor(n, shape, dt))
        table, tiles_of = sb("g1_table", [S, SLOTS, 4]), sb("g1_tiles_of", [1, SLOTS], I32)
        deg, dinv = sb("g1_deg", [P, T]), sb("g1_dinv", [P, T])
        fc = sb("g1_fc", [P, T, D])
        with ExitStack() as s2:
            sb2 = lambda n, shape, dt=F32: s2.enter_context(nc.sbuf_tensor(n, shape, dt))
            rec, tile_of_edge = sb2("g1_rec", [P, EC, 4]), sb2("g1_tile", [P, EC])
            q, ends = sb2("g1_q", [P, EC]), sb2("g1_ends", [P, T])
            stage_edge_records(c, "g1r", args["dst"], args["src"], args["edge_weight"], rec, tile_of_edge)
            stage_degree(c, "g1d", rec, tile_of_edge, deg)
            stage_degree_norm(c, "g1n", deg, dinv)
            stage_rank_buckets(c, "g1k", tile_of_edge, EC, T, S, q, ends)
            stage_bucket_table(c, "g1t", ends, T, SLOTS, tiles_of)
            stage_scatter_records(c, "g1s", rec, q, scratch["rows1"], table)
        w1, w2, w3 = sb("g1_w1", [128, 2, C1 + D]), sb("g1_w2", [128, 1, C2 + D]), sb("g1_w3", [C2, 1, D])
        vec = {n: sb("g1_" + n, [P, args["g1_" + n].shape[0]]) for n in ("b1", "g1", "be1", "b2", "g2", "be2", "bfc")}
        wfc = args["g1_wfc"]
        stage_load(c, "g1_w", [
            (w1[:, :, 0:C1], args["g1_w1"].rearrange("(j p) m -> p j m", p=128)),
            (w1[:, :, C1:], wfc[0:D, :].rearrange("(j p) m -> p j m", p=128)),
            (w2[:, 0, 0:C2], args["g1_w2"]), (w2[:, 0, C2:], wfc[D:D + C1, :]), (w3[:, 0, :], wfc[D + C1:, :])]
            + [(v[:, :], row_to_all(args["g1_" + n], P)) for n, v in vec.items()])
        h1, h2 = sb("g1_h1", [P, T, C1]), sb("g1_h2", [P, T, C2])
        stage_project(c, "g1a", c.x, D, w1, C1 + D, lambda t, ps: [
            lambda: V.tensor_scalar(flat(h1[:, ds(t, 1), :]), ps[:, 0:C1], dinv[:, ds(t, 1)], None, ALU.mult),
            lambda: V.tensor_copy(flat(fc[:, ds(t, 1), :]), ps[:, C1:])],
            norm=(mean, rstd), dram=(scratch["h1"], h1[:, :, :]))
        stage_aggregate(c, "g1b", table, tiles_of, scratch["h1"], C1, h1, weighted=False)
        stage_batch_norm(c, "g1c", h1, C1, dinv, vec["b1"], vec["g1"], vec["be1"])
        stage_project(c, "g1e", h1, C1, w2, C2 + D, lambda t, ps: [
            lambda: V.tensor_scalar(flat(h2[:, ds(t, 1), :]), ps[:, 0:C2], dinv[:, ds(t, 1)], None, ALU.mult),
            lambda: V.tensor_tensor(flat(fc[:, ds(t, 1), :]), flat(fc[:, ds(t, 1), :]), ps[:, C2:], ALU.add)],
            dram=(scratch["h2"], h2[:, :, :]))
        stage_aggregate(c, "g1f", table, tiles_of, scratch["h2"], C2, h2, weighted=False)
        stage_batch_norm(c, "g1g", h2, C2, dinv, vec["b2"], vec["g2"], vec["be2"])
        stage_project(c, "g1h", h2, C2, w3, D, lambda t, ps: [
            lambda: V.tensor_tensor(flat(fc[:, ds(t, 1), :]), flat(fc[:, ds(t, 1), :]), ps, ALU.add)])
        stage_fc_end(c, "g1i", fc, vec["bfc"], c.x)


def layer1_ffn(c, out, mean, rstd):
    nc, args = c.nc, c.args
    stage_norm_stats(c, "f1", c.x, mean, rstd)
    with ExitStack() as s:
        sb = lambda n, shape, dt=F32: s.enter_context(nc.sbuf_tensor(n, shape, dt))
        rows_t, z = sb("f1_rows_t", [128, 2, NODES]), sb("f1_z", [P, T, D])
        router, bias = sb("f1_router", [128, 2, EXPERTS]), sb("f1_bias", [128, EXPERTS])
        gamma, beta = sb("f1_gamma", [128, D]), sb("f1_beta", [128, D])
        picked, picked_w = sb("f1_picked", [1, TOPK], I32), sb("f1_picked_w", [128, TOPK])
        mean2, rstd2 = sb("f1_mean2", [P, T]), sb("f1_rstd2", [P, T])
        stage_load(c, "f1_w", [(router[:, :, :], args["f1_wr"].rearrange("(j p) m -> p j m", p=128)),
                               (bias[:, :], row_to_all(args["f1_br"], 128)),
                               (gamma[:, :], row_to_all(args["f1_gamma"], 128)),
                               (beta[:, :], row_to_all(args["f1_beta"], 128))])
        stage_project(c, "f1a", c.x, D, None, 0, None, norm=(mean, rstd), keep_t=rows_t)
        stage_pick_experts(c, "f1b", rows_t, router, bias, picked, picked_w)
        stage_shared_ffn(c, "f1c", rows_t, picked, picked_w, args["f1_w1"], args["f1_w2"], args["f1_b1"], args["f1_b2"],
                         mean, rstd, z)
        stage_norm_stats(c, "f1d", z, mean2, rstd2)
        stage_last(c, "f1e", z, mean2, rstd2, gamma, beta, out)


def part(nc, emit):
    with nc.cleanup_on_exit():
        emit()
    nc.all_engine_barrier()


def build(nc, args, out, scratch, upto=99):
    with ExitStack() as ctx:
        c = Core(nc, ctx, args)
        stage_constants(c)
        mean, rstd = c.keep("mean", [P, T]), c.keep("rstd", [P, T])
        part(nc, lambda: layer0_graph(c, scratch, mean, rstd))
        if upto >= 2:
            part(nc, lambda: layer0_ffn(c, scratch, mean, rstd))
        if upto >= 3:
            part(nc, lambda: layer1_graph(c, scratch, mean, rstd))
        if upto >= 4:
            layer1_ffn(c, out, mean, rstd)
            return
        with ExitStack() as s:
            out_stored = c.semaphore("out_stored")
            block = s.enter_context(nc.Block())

            @block.sync
            def _(sp):
                sp.dma_start(out.rearrange("(t p) f -> p t f", p=P), c.x[:, :, :]).then_inc(out_stored, 16)
                sp.wait_ge(out_stored, 16)


def lay_out(inputs):
    def a(name):
        return np.ascontiguousarray(inputs[name])

    def by_partition(w):
        e, k, n = w.shape
        return np.ascontiguousarray(w.reshape(e, k // 128, 128, n).transpose(0, 2, 1, 3))

    def columns(v):
        return np.ascontiguousarray(v.reshape(-1, 128).T)

    return {
        "x": a("x"), "src": a("src"), "dst": a("dst"), "edge_weight": a("edge_weight"), "g0_w": a("L0_gnn_weight"),
        "f0_wr": a("L0_ffn_Wr"), "f0_br": a("L0_ffn_br"), "f0_g": columns(a("L0_ffn_ln_g")), "f0_b": columns(a("L0_ffn_ln_b")),
        "f0_w1": by_partition(a("L0_ffn_W1")), "f0_b1": columns(a("L0_ffn_b1")),
        "f0_w2": by_partition(a("L0_ffn_W2")), "f0_b2": a("L0_ffn_b2"),
        "g1_w1": a("L1_gnn_W1"), "g1_b1": a("L1_gnn_b1"), "g1_g1": a("L1_gnn_g1"), "g1_be1": a("L1_gnn_be1"),
        "g1_w2": a("L1_gnn_W2"), "g1_b2": a("L1_gnn_b2"), "g1_g2": a("L1_gnn_g2"), "g1_be2": a("L1_gnn_be2"),
        "g1_wfc": a("L1_gnn_Wfc"), "g1_bfc": a("L1_gnn_bfc"),
        "f1_wr": a("L1_ffn_Wr"), "f1_br": a("L1_ffn_br"), "f1_w1": by_partition(a("L1_ffn_W1")),
        "f1_b1": np.ascontiguousarray(a("L1_ffn_b1").reshape(EXPERTS, H1 // 128, 128).transpose(0, 2, 1)),
        "f1_w2": by_partition(a("L1_ffn_W2")), "f1_b2": a("L1_ffn_b2"),
        "f1_gamma": a("L1_ffn_gamma"), "f1_beta": a("L1_ffn_beta"),
    }


def program(nc, args, out, upto=99):
    dram = lambda name, shape: nc.dram_tensor(name, shape, F32).ap()
    scratch = {
        "support": dram("support", [NODES, D]), "h1": dram("h1", [NODES, C1]), "h2": dram("h2", [NODES, C2]),
        "rows0": dram("rows0", [S * SLOTS, 4]), "rows1": dram("rows1", [S * SLOTS, 4]),
        "slots": dram("slots", [(BLOCKS + 1) * B, D]), "results": dram("results", [BLOCKS * B, D]),
    }
    build(nc, args, out, scratch, upto)


def kernel(**inputs):
    import concourse.bacc as bacc
    from concourse.bass_utils import run_bass_kernel_spmd

    nc = bacc.Bacc("TRN2", target_bir_lowering=False, num_devices=1)
    arrays = {"in_" + k: v for k, v in lay_out(inputs).items()}
    args = {k[3:]: nc.dram_tensor(k, v.shape, mybir.dt.from_np(v.dtype), kind="ExternalInput").ap()
            for k, v in arrays.items()}
    out = nc.dram_tensor("out_0_dram", (NODES, D), F32, kind="ExternalOutput").ap()
    program(nc, args, out)
    r = run_bass_kernel_spmd(nc, [arrays], core_ids=[0])
    return r.results[0]["out_0_dram"]
```

```python
from contextlib import ExitStack

import concourse.bass as bass
import numpy as np
from concourse import mybir
from concourse.alu_op_type import AluOpType as ALU

F32 = mybir.dt.float32
I32 = mybir.dt.int32
U32 = mybir.dt.uint32
BF16 = mybir.dt.bfloat16
ACT = mybir.ActivationFunctionType
AX = mybir.AxisListType

NODES, D = 3125, 256
P = 125
T = NODES // P
EDGES = 50000
EC = EDGES // P
S = 128
PAIRS = (EDGES + T * (2 * S - 1)) // (2 * S)
SLOTS = 2 * PAIRS
EXPERTS, TOPK = 8, 2
H0, H1 = 1024, 512
B = 256
BLOCKS = (NODES * TOPK + EXPERTS * (B - 1)) // B
C1, C2 = 128, 64
ROUND = 12582912.0
U = 5
LN_EPS = BN_EPS = 1e-5
ds = bass.ds


class Core:

    def __init__(self, nc, ctx, args):
        self.nc, self.ctx, self.args = nc, ctx, args

    def keep(self, name, shape, dt=F32):
        return self.ctx.enter_context(self.nc.sbuf_tensor(name, shape, dt))

    def semaphore(self, name):
        return self.nc.alloc_semaphore(name)


class Stage:

    def __init__(self):
        self.programs = {}

    def _put(self, engine):
        def put(program):
            self.programs[engine] = program
            return program
        return put

    @property
    def sync(self):
        return self._put("sync")

    @property
    def scalar(self):
        return self._put("scalar")

    @property
    def vector(self):
        return self._put("vector")

    @property
    def gpsimd(self):
        return self._put("gpsimd")

    @property
    def tensor(self):
        return self._put("tensor")


def run(c, *stages):
    with c.nc.Block() as block:
        @block.sync
        def _(sp):
            for stage in stages:
                if "sync" in stage.programs:
                    stage.programs["sync"](sp)

        @block.gpsimd
        def _(pool):
            for stage in stages:
                if "gpsimd" in stage.programs:
                    stage.programs["gpsimd"](pool)

        @block.vector
        def _(dve):
            for stage in stages:
                if "vector" in stage.programs:
                    stage.programs["vector"](dve)

        @block.scalar
        def _(act):
            for stage in stages:
                if "scalar" in stage.programs:
                    stage.programs["scalar"](act)

        @block.tensor
        def _(pe):
            for stage in stages:
                if "tensor" in stage.programs:
                    stage.programs["tensor"](pe)


def bank(c, stack, name):
    return stack.enter_context(c.nc.psum_tensor(name, [128, 512], F32))


def linker(engine, sem, base=0):
    count = [0]

    def link(instruction):
        count[0] += 1
        instruction.then_inc(sem, 1)
        engine.wait_ge(sem, base + count[0])

    return link


def repeat(engine, n, body, last=False):
    if last:
        body(0, True, False)
        with engine.Fori(1, n - 1) as i:
            body(i, False, False)
        body(n - 1, False, True)
    else:
        body(0, True)
        with engine.Fori(1, n) as i:
            body(i, False)


def wait_slot(engine, sem, value):
    engine.wait_ge(sem, value)
    if not isinstance(value, int):
        engine.nop(nofuse=True)


def row_to_all(ap, parts):
    return ap.rearrange("(a f) -> a f", a=1).broadcast_to([parts, ap.shape[0]])


def stage_constants(c, s):
    nc = c.nc
    stage = Stage()
    iota_i = s.enter_context(nc.sbuf_tensor("iota_i", [128, 512], I32))
    x_in, filled, selected, iota_made, iota_cast = (
        c.semaphore(n) for n in ("x_in", "filled", "selected", "iota_made", "iota_cast"))

    @stage.sync
    def _(sp):
        sp.dma_start(c.x[:, :, :], c.args["x"].rearrange("(t p) f -> p t f", p=P)).then_inc(x_in, 16)
        sp.wait_ge(x_in, 16)

    @stage.gpsimd
    def _(pool):
        nc.gpsimd.iota(iota_i[:, :], pattern=[[1, 512]], base=0, channel_multiplier=0).then_inc(iota_made, 1)
        nc.gpsimd.memset(c.ident[:, :], 0.0).then_inc(filled, 1)
        nc.gpsimd.memset(c.before[:, :], 1.0).then_inc(filled, 1)
        nc.gpsimd.memset(c.ones[:, :], 1.0).then_inc(filled, 1)
        pool.wait_ge(filled, 3)
        nc.gpsimd.affine_select(out=c.ident[:, :], in_=c.ident[:, :], compare_op=ALU.not_equal, fill=1.0, base=0,
                                pattern=[[-1, 128]], channel_multiplier=1).then_inc(selected, 1)
        nc.gpsimd.affine_select(out=c.before[:, :], in_=c.before[:, :], compare_op=ALU.is_gt, fill=0.0, base=0,
                                pattern=[[1, 128]], channel_multiplier=-1).then_inc(selected, 1)

    @stage.vector
    def _(dve):
        dve.wait_ge(iota_made, 1)
        nc.vector.tensor_copy(c.iota[:, :], iota_i[:, :]).then_inc(iota_cast, 1)

    return stage


def stage_norm_stats(c, s, tag, src, mean, rstd):
    nc = c.nc
    stage = Stage()
    sb = lambda n, shape: s.enter_context(nc.sbuf_tensor(f"{tag}_{n}", shape, F32))
    st, dm, var, std = sb("st", [P, T, 6]), sb("dm", [P, T]), sb("var", [P, T]), sb("std", [P, T])
    stats_done, chain, var_ready, std_ready = (
        c.semaphore(f"{tag}_{n}") for n in ("stats_done", "chain", "var_ready", "std_ready"))

    @stage.vector
    def _(dve):
        with dve.Fori(0, T // U) as i:
            for k in range(U):
                nc.vector.bn_stats(flat(st[:, ds(i * U + k, 1), :]), flat(src[:, ds(i * U + k, 1), :])).then_inc(stats_done, 1)
        dve.wait_ge(stats_done, T)
        link = linker(dve, chain)
        link(nc.vector.tensor_tensor(dm[:, :], st[:, :, 1], st[:, :, 4], ALU.subtract))
        link(nc.vector.tensor_tensor(mean[:, :], st[:, :, 1], st[:, :, 4], ALU.add))
        link(nc.vector.tensor_scalar(mean[:, :], mean[:, :], 0.5, None, ALU.mult))
        link(nc.vector.tensor_tensor(dm[:, :], dm[:, :], dm[:, :], ALU.mult))
        link(nc.vector.tensor_tensor(var[:, :], st[:, :, 2], st[:, :, 5], ALU.add))
        link(nc.vector.scalar_tensor_tensor(out=var[:, :], in0=dm[:, :], scalar=D / 4.0, in1=var[:, :],
                                            op0=ALU.mult, op1=ALU.add))
        nc.vector.tensor_scalar(var[:, :], var[:, :], 1.0 / D, LN_EPS, ALU.mult, ALU.add).then_inc(var_ready, 1)
        dve.wait_ge(std_ready, 1)
        link(nc.vector.reciprocal(rstd[:, :], std[:, :]))

    @stage.scalar
    def _(act):
        act.wait_ge(var_ready, 1)
        nc.scalar.activation(std[:, :], var[:, :], ACT.Sqrt).then_inc(std_ready, 1)

    return stage


def stage_project(c, s, tag, src, width, rhs, m, outs, norm=None, keep_t=None, dram=None):
    nc = c.nc
    stage = Stage()
    n = -(-width // 128)
    w = width // n
    LEAD = 2
    RING = (0, 1, 2, 0, 1)
    BACK = (2, 2, 5, 3, 3)
    rows = s.enter_context(nc.sbuf_tensor(tag + "_rows", [P, U, width], F32))
    rows_t = s.enter_context(nc.sbuf_tensor(tag + "_rows_t", [128, 3, n * P], F32))
    ps_t = [bank(c, s, f"{tag}_ps_t{b}")[0:w, 0:n * P] for b in range(3)]
    ps_o = [bank(c, s, f"{tag}_ps_o{b}")[0:P, 0:m] for b in range(3)] if m else None
    rows_ready, turned, copied, multiplied, written, taken, stored = (
        c.semaphore(f"{tag}_{x}") for x in ("rows_ready", "turned", "copied", "multiplied", "written", "taken", "stored"))

    def wait_free(engine, sem, i, k, first):
        if not (first and k < 3):
            wait_slot(engine, sem, i * U + k - BACK[k] + 1)

    @stage.vector
    def _(dve):
        def prepare(t, k, first):
            if not first:
                wait_slot(dve, turned, t - U + 1)
            if norm is None:
                nc.vector.tensor_copy(rows[:, k, :], flat(src[:, ds(t, 1), 0:width])).then_inc(rows_ready, 1)
            else:
                nc.vector.tensor_scalar(rows[:, k, :], flat(src[:, ds(t, 1), 0:width]), norm[0][:, ds(t, 1)],
                                        norm[1][:, ds(t, 1)], ALU.subtract, ALU.mult).then_inc(rows_ready, 1)

        def body(i, first, last):
            for k in range(U):
                if not (last and k + LEAD >= U):
                    prepare(i * U + k + LEAD, (k + LEAD) % U, first and k + LEAD < U)
                if m:
                    wait_slot(dve, multiplied, i * U + k + 1)
                    steps = outs(i * U + k, ps_o[RING[k]])
                    for step in steps[:-1]:
                        step().then_inc(written, 1)
                    steps[-1]().then_inc(taken, 1)

        for k in range(LEAD):
            prepare(k, k, True)
        repeat(dve, T // U, body, last=True)
        if m:
            dve.wait_ge(taken, T)

    @stage.scalar
    def _(act):
        def body(i, first):
            for k in range(U):
                if m:
                    wait_free(act, multiplied, i, k, first)
                wait_slot(act, turned, i * U + k + 1)
                if m:
                    nc.scalar.copy(rows_t[0:w, RING[k], :], ps_t[RING[k]]).then_inc(copied, 1)
                else:
                    nc.scalar.copy(keep_t[0:w, :, ds((i * U + k) * P, P)],
                                   ps_t[RING[k]].rearrange("p (j r) -> p j r", j=n)).then_inc(copied, 1)

        repeat(act, T // U, body)

    @stage.tensor
    def _(pe):
        def turn(i, k, t, first):
            wait_free(pe, copied, i, k, first)
            wait_slot(pe, rows_ready, t + 1)
            for j in range(n):
                last = nc.tensor.transpose(ps_t[RING[k]][:, j * P:(j + 1) * P], rows[:, k, j * w:(j + 1) * w], c.ident[0:P, 0:P])
            last.then_inc(turned, 1)

        def body(i, first, last):
            for k in range(U):
                if k + 1 < U:
                    turn(i, k + 1, i * U + k + 1, first)
                elif not last:
                    turn(i + 1, 0, (i + 1) * U, False)
                if m:
                    wait_free(pe, taken, i, k, first)
                    wait_slot(pe, copied, i * U + k + 1)
                    for j in range(n):
                        mm = nc.tensor.matmul(ps_o[RING[k]], rows_t[0:w, RING[k], j * P:(j + 1) * P], rhs[0:w, j, :],
                                              start=(j == 0), stop=(j == n - 1))
                    mm.then_inc(multiplied, 1)

        turn(0, 0, 0, True)
        repeat(pe, T // U, body, last=True)

    stage.kept = (copied, T)
    if dram is not None:
        @stage.sync
        def _(sp):
            sp.wait_ge(taken, T)
            sp.dma_start(dram[0].rearrange("(t p) f -> p t f", p=P), dram[1]).then_inc(stored, 16)
            sp.wait_ge(stored, 16)

    return stage


def stage_load_edges(c, s, tag):
    nc = c.nc
    stage = Stage()
    c.src_i, c.dst_i = (s.enter_context(nc.sbuf_tensor(f"{tag}_{n}", [P, EC], I32)) for n in ("src_i", "dst_i"))
    c.edge_w = s.enter_context(nc.sbuf_tensor(tag + "_edge_w", [P, EC], F32))
    loaded = c.semaphore(tag + "_loaded")

    @stage.sync
    def _(sp):
        for dst, src in ((c.src_i, "src"), (c.dst_i, "dst"), (c.edge_w, "edge_weight")):
            sp.dma_start(dst[:, :], c.args[src].rearrange("(p c) -> p c", p=P)).then_inc(loaded, 16)
        sp.wait_ge(loaded, 48)

    return stage


def stage_edge_records(c, s, tag, add_to, other, rec, bucket):
    nc = c.nc
    stage = Stage()
    to_f = s.enter_context(nc.sbuf_tensor(tag + "_to_f", [P, EC], F32))
    chain = c.semaphore(tag + "_chain")

    @stage.vector
    def _(dve):
        link = linker(dve, chain)
        link(nc.vector.memset(rec[:, :, 3], 0.0))
        link(nc.vector.tensor_copy(to_f[:, :], add_to[:, :]))
        link(nc.vector.tensor_scalar(bucket[:, :], to_f[:, :], 1.0 / P, -(P - 1) / (2.0 * P), ALU.mult, ALU.add))
        link(nc.vector.tensor_scalar(bucket[:, :], bucket[:, :], ROUND, ROUND, ALU.add, ALU.subtract))
        link(nc.vector.scalar_tensor_tensor(out=rec[:, :, 0], in0=bucket[:, :], scalar=-float(P), in1=to_f[:, :],
                                            op0=ALU.mult, op1=ALU.add))
        link(nc.vector.tensor_copy(rec[:, :, 1].bitcast(I32), other[:, :]))
        link(nc.vector.tensor_copy(rec[:, :, 2], c.edge_w[:, :]))

    return stage


def stage_rank_buckets(c, s, tag, bucket, cols, n_buckets, group, q, ends):
    nc = c.nc
    stage = Stage()
    W = 5 if n_buckets % 5 == 0 else 4
    assert n_buckets % W == 0
    sb = lambda n, shape: s.enter_context(nc.sbuf_tensor(f"{tag}_{n}", shape, F32))
    is_b, run_b = sb("is_b", [P, W, cols]), sb("run_b", [P, W, cols])
    count, groups, off = sb("count", [P, n_buckets]), sb("groups", [P, n_buckets]), sb("off", [P, n_buckets])
    stage.bank = bank(c, s, tag + "_ps")
    ps = stage.bank[0:P, 0:2 * n_buckets].rearrange("p (a b) -> p a b", a=2)
    counted, chain, summed, masked, scanned, ranked = (
        c.semaphore(f"{tag}_{n}") for n in ("counted", "chain", "summed", "masked", "scanned", "ranked"))

    @stage.vector
    def _(dve):
        def count_body(i, first):
            for k in range(W):
                b = i * W + k
                if not first:
                    wait_slot(dve, counted, b - W + 1)
                nc.vector.tensor_scalar(is_b[:, k, :], bucket[:, :], c.iota[0:P, ds(b, 1)], 0.0, ALU.is_equal, ALU.add,
                                        accum_out=count[:, ds(b, 1)]).then_inc(counted, 1)

        repeat(dve, n_buckets // W, count_body)
        dve.wait_ge(summed, 1)
        link = linker(dve, chain)
        link(nc.vector.tensor_scalar(groups[:, :], ps[:, 1, :], 1.0 / group, (group - 1) / (2.0 * group),
                                     ALU.mult, ALU.add))
        link(nc.vector.tensor_scalar(groups[:, :], groups[:, :], ROUND, ROUND, ALU.add, ALU.subtract))
        link(nc.vector.tensor_tensor_scan(ends[:, :], c.ones[0:P, 0:n_buckets], groups[:, :], 0.0, ALU.mult, ALU.add))
        link(nc.vector.tensor_tensor(off[:, :], ends[:, :], groups[:, :], ALU.subtract))
        link(nc.vector.scalar_tensor_tensor(out=off[:, :], in0=off[:, :], scalar=float(group), in1=ps[:, 0, :],
                                            op0=ALU.mult, op1=ALU.add))
        link(nc.vector.memset(q[:, :], 0.0))

        def rank_body(i, first):
            for k in range(W):
                if not first:
                    wait_slot(dve, ranked, i * W + k - W + 1)
                nc.vector.tensor_scalar(is_b[:, k, :], bucket[:, :], c.iota[0:P, ds(i * W + k, 1)], None,
                                        ALU.is_equal).then_inc(masked, 1)
            for k in range(W):
                wait_slot(dve, masked, i * W + k + 1)
                nc.vector.tensor_tensor_scan(run_b[:, k, :], c.ones[0:P, 0:1].broadcast_to([P, cols]), is_b[:, k, :],
                                             off[:, ds(i * W + k, 1)], ALU.mult, ALU.add).then_inc(scanned, 1)
            for k in range(W):
                wait_slot(dve, scanned, i * W + k + 1)
                if not (first and k == 0):
                    wait_slot(dve, ranked, i * W + k)
                nc.vector.copy_predicated(q[:, :], is_b[:, k, :].bitcast(I32), run_b[:, k, :]).then_inc(ranked, 1)

        repeat(dve, n_buckets // W, rank_body)
        dve.wait_ge(ranked, n_buckets)
        link(nc.vector.tensor_scalar(q[:, :], q[:, :], -1.0, None, ALU.add))

    stage.ends_ready = (chain, 5)

    @stage.tensor
    def _(pe):
        pe.wait_ge(counted, n_buckets)
        nc.tensor.matmul(ps[:, 0, :], c.before[0:P, 0:P], count[:, :], start=True, stop=True)
        nc.tensor.matmul(ps[:, 1, :], c.ones[0:P, 0:P], count[:, :], start=True, stop=True).then_inc(summed, 1)

    return stage


def stage_bucket_table(c, s, tag, rank, ends, n_buckets, n_groups, table):
    nc = c.nc
    stage = Stage()
    others = n_buckets - 1
    end_col = s.enter_context(nc.sbuf_tensor(tag + "_end_col", [others, 1], F32))
    ended = s.enter_context(nc.sbuf_tensor(tag + "_ended", [others, n_groups], F32))
    ps = rank.bank
    chain, turned, summed = (c.semaphore(f"{tag}_{n}") for n in ("chain", "turned", "summed"))

    @stage.vector
    def _(dve):
        link = linker(dve, chain)
        dve.wait_ge(turned, 1)
        link(nc.vector.tensor_copy(end_col[:, :], ps[0:others, 0:1]))
        link(nc.vector.tensor_scalar(ended[:, :], c.iota[0:others, 0:n_groups], end_col[:, 0:1], None, ALU.is_ge))
        dve.wait_ge(summed, 1)
        link(nc.vector.tensor_copy(table[:, :], ps[0:1, 0:n_groups]))

    @stage.tensor
    def _(pe):
        pe.wait_ge(*rank.ends_ready)
        nc.tensor.matmul(ps[0:others, 0:1], ends[0:1, 0:others], c.ones[0:1, 0:1], start=True, stop=True).then_inc(turned, 1)
        pe.wait_ge(chain, 2)
        nc.tensor.matmul(ps[0:1, 0:n_groups], c.ones[0:others, 0:1], ended[:, :], start=True, stop=True).then_inc(summed, 1)

    return stage


def stage_places(c, s, tag, q, place_i):
    nc = c.nc
    stage = Stage()
    slot, place = (s.enter_context(nc.sbuf_tensor(f"{tag}_{n}", [P, EC], F32)) for n in ("slot", "place"))
    chain = c.semaphore(tag + "_chain")

    @stage.vector
    def _(dve):
        link = linker(dve, chain)
        link(nc.vector.tensor_scalar(slot[:, :], q[:, :], 1.0 / S, -(S - 1) / (2.0 * S), ALU.mult, ALU.add))
        link(nc.vector.tensor_scalar(slot[:, :], slot[:, :], ROUND, ROUND, ALU.add, ALU.subtract))
        link(nc.vector.scalar_tensor_tensor(out=place[:, :], in0=slot[:, :], scalar=-float(S), in1=q[:, :],
                                            op0=ALU.mult, op1=ALU.add))
        link(nc.vector.scalar_tensor_tensor(out=place[:, :], in0=place[:, :], scalar=float(SLOTS), in1=slot[:, :],
                                            op0=ALU.mult, op1=ALU.add))
        link(nc.vector.tensor_copy(place_i[:, :], place[:, :]))

    return stage


def stage_fill(c, s, tag, rows_list, slots):
    nc = c.nc
    stage = Stage()
    none = s.enter_context(nc.sbuf_tensor(tag + "_none", [S, SLOTS, 4], F32))
    zero = s.enter_context(nc.sbuf_tensor(tag + "_zero", [128, B * D // 128], F32))
    made, filled = c.semaphore(tag + "_made"), c.semaphore(tag + "_filled")
    slots_v = slots.rearrange("(a p r) f -> a p (r f)", a=BLOCKS + 1, p=128)

    @stage.vector
    def _(dve):
        nc.vector.memset(none[:, :, :], 0.0).then_inc(made, 1)
        nc.vector.memset(zero[:, :], 0.0).then_inc(made, 1)
        dve.wait_ge(made, 2)
        nc.vector.memset(none[:, :, 0], -1.0).then_inc(made, 1)

    @stage.sync
    def _(sp):
        sp.wait_ge(made, 3)
        for rows in rows_list:
            sp.dma_start(rows.rearrange("(r j) f -> r j f", r=S), none[:, :, :]).then_inc(filled, 16)
        for a in range(BLOCKS + 1):
            sp.dma_start(slots_v[a], zero[:, :]).then_inc(filled, 16)
        sp.wait_ge(filled, 16 * (len(rows_list) + BLOCKS + 1))

    return stage


def stage_scatter_records(c, s, tag, rec, place_i, rows, table_sb):
    nc = c.nc
    stage = Stage()
    W = 8
    idx = s.enter_context(nc.sbuf_tensor(tag + "_idx", [P, 2, W], I32))
    put = s.enter_context(nc.sbuf_tensor(tag + "_put", [P, 2, W, 4], F32))
    staged, read = c.semaphore(tag + "_staged"), c.semaphore(tag + "_read")
    scattered = [c.semaphore(f"{tag}_scattered{h}") for h in range(2)]

    @stage.gpsimd
    def _(pool):
        def body(i, first):
            for h in range(2):
                if not first:
                    wait_slot(pool, scattered[h], i * (16 * W))
                at = i * (2 * W) + h * W
                nc.gpsimd.tensor_copy(idx[:, h, :], place_i[:, ds(at, W)]).then_inc(staged, 1)
                nc.gpsimd.tensor_copy(put[:, h, :, :], rec[:, ds(at, W), :]).then_inc(staged, 1)
                wait_slot(pool, staged, i * 4 + 2 * h + 2)
                for k in range(W):
                    nc.gpsimd.indirect_dma_start(
                        out=rows, out_offset=bass.IndirectOffsetOnAxis(ap=idx[:, h, k:k + 1], axis=0),
                        in_=put[:, h, k, :], in_offset=None).then_inc(scattered[h], 16)

        repeat(pool, EC // (2 * W), body)

    @stage.sync
    def _(sp):
        for h in range(2):
            sp.wait_ge(scattered[h], 16 * EC // 2)
        sp.dma_start(table_sb[:, :, :], rows.rearrange("(r j) f -> r j f", r=S)).then_inc(read, 16)
        sp.wait_ge(read, 16)

    return stage


def stage_aggregate(c, s, tag, table_sb, tiles_of, values, width, acc, weighted):
    nc = c.nc
    stage = Stage()
    G = 20
    H = G // 2
    NB = H // 2
    assert SLOTS % G == 0
    sb = lambda n, shape, dt=F32: s.enter_context(nc.sbuf_tensor(f"{tag}_{n}", shape, dt))
    idx, got, hot = sb("idx", [S, 2, H], I32), sb("got", [S, G, width]), sb("hot", [S, G, P])
    ps = [bank(c, s, f"{tag}_ps{b}")[0:P, 0:width] for b in range(NB)]
    staged, matched, hot_ready, summed, added = (
        c.semaphore(f"{tag}_{n}") for n in ("staged", "matched", "hot_ready", "summed", "added"))
    gathered = [c.semaphore(f"{tag}_gathered{k}") for k in range(G)]

    @stage.scalar
    def _(act):
        def body(i, first):
            for h in range(2):
                if not first:
                    wait_slot(act, summed, (i * 2 + h - 1) * NB)
                nc.scalar.copy(idx[:, h, :], table_sb[:, ds(i * G + h * H, H), 1].bitcast(I32)).then_inc(staged, 1)

        repeat(act, SLOTS // G, body)

    @stage.gpsimd
    def _(pool):
        def body(i, first):
            for h in range(2):
                wait_slot(pool, staged, i * 2 + h + 1)
                for k in range(H):
                    nc.gpsimd.indirect_dma_start(
                        out=got[:, h * H + k, :], out_offset=None, in_=values,
                        in_offset=bass.IndirectOffsetOnAxis(ap=idx[:, h, k:k + 1], axis=0),
                    ).then_inc(gathered[h * H + k], 16)

        repeat(pool, SLOTS // G, body)

    @stage.vector
    def _(dve):
        def make_hot(i, h, first):
            if not first:
                wait_slot(dve, summed, (i * 2 + h - 1) * NB)
            here, at = hot[:, h * H:(h + 1) * H, :], ds(i * G + h * H, H)
            wide = lambda field: table_sb[:, at, field].unsqueeze(2).broadcast_to([S, H, P])
            match = nc.vector.tensor_tensor(here, c.iota[0:S, 0:P].unsqueeze(1).broadcast_to([S, H, P]), wide(0),
                                            ALU.is_equal)
            if weighted:
                match.then_inc(matched, 1)
                wait_slot(dve, matched, i * 2 + h + 1)
                nc.vector.tensor_tensor(here, here, wide(2), ALU.mult).then_inc(hot_ready, 1)
            else:
                match.then_inc(hot_ready, 1)

        def add(pair, b, first=False):
            tile = dve.value_load(tiles_of[0:1, ds(pair, 1)], min_val=0, max_val=T - 1)
            if not first:
                wait_slot(dve, added, pair)
            wait_slot(dve, summed, pair + 1)
            here = flat(acc[:, ds(tile, 1), :])
            nc.vector.tensor_tensor(here, here, ps[b], ALU.add).then_inc(added, 1)

        def body(i, first):
            for h in range(2):
                make_hot(i, h, first)
                if not (first and h == 0):
                    for b in range(NB):
                        add((i * 2 + h - 1) * NB + b, b, first and b == 0)

        repeat(dve, SLOTS // G, body)
        for b in range(NB):
            add(PAIRS - NB + b, b)
        dve.wait_ge(added, PAIRS)

    @stage.tensor
    def _(pe):
        def body(i, first):
            for h in range(2):
                wait_slot(pe, hot_ready, i * 2 + h + 1)
                for b in range(NB):
                    if not (first and h == 0):
                        wait_slot(pe, added, (i * 2 + h - 1) * NB + b + 1)
                    for e in range(2):
                        k = h * H + b * 2 + e
                        pe.wait_ge(gathered[k], i * 16 + 16)
                        mm = nc.tensor.matmul(ps[b], hot[:, k, :], got[:, k, :], start=(e == 0), stop=(e == 1))
                    mm.then_inc(summed, 1)

        repeat(pe, SLOTS // G, body)

    return stage


def stage_normalise(c, s, tag, src, mean, rstd, dst):
    nc = c.nc
    stage = Stage()
    done = c.semaphore(tag + "_done")

    @stage.vector
    def _(dve):
        with dve.Fori(0, T // U) as i:
            for k in range(U):
                t = i * U + k
                nc.vector.tensor_scalar(flat(dst[:, ds(t, 1), :]), flat(src[:, ds(t, 1), :]), mean[:, ds(t, 1)],
                                        rstd[:, ds(t, 1)], ALU.subtract, ALU.mult).then_inc(done, 1)
        dve.wait_ge(done, T)

    return stage


def stage_load(c, s, tag, pairs):
    stage = Stage()
    loaded = c.semaphore(tag + "_loaded")

    @stage.sync
    def _(sp):
        for dst, src in pairs:
            sp.dma_start(dst, src).then_inc(loaded, 16)
        sp.wait_ge(loaded, 16 * len(pairs))

    return stage


def stage_route(c, s, tag, logits, bias, probs, top_i, weights):
    nc = c.nc
    E = EXPERTS
    stage = Stage()
    sb = lambda n, shape, dt=F32: s.enter_context(nc.sbuf_tensor(f"{tag}_{n}", shape, dt))
    most, total, both = sb("most", [P, T]), sb("total", [P, T]), sb("both", [P, T])
    top_p = sb("top_p", [P, T, 8])
    raw = sb("raw", [P, T, 8], U32)
    chain, shifted, exped, top = (c.semaphore(f"{tag}_{n}") for n in ("chain", "shifted", "exped", "top"))

    @stage.vector
    def _(dve):
        link = linker(dve, chain)
        link(nc.vector.tensor_tensor(logits[:, :, :], logits[:, :, :],
                                     bias[0:P, :].unsqueeze(1).broadcast_to([P, T, E]), ALU.add))
        link(nc.vector.tensor_reduce(most[:, :], logits[:, :, :], AX.X, ALU.max))
        nc.vector.tensor_tensor(logits[:, :, :], logits[:, :, :], most[:, :].unsqueeze(2).broadcast_to([P, T, E]),
                                ALU.subtract).then_inc(shifted, 1)
        dve.wait_ge(exped, 1)
        link(nc.vector.tensor_reduce(total[:, :], probs[:, :, :], AX.X, ALU.add))
        link(nc.vector.reciprocal(total[:, :], total[:, :]))
        link(nc.vector.tensor_tensor(probs[:, :, :], probs[:, :, :],
                                     total[:, :].unsqueeze(2).broadcast_to([P, T, E]), ALU.mult))
        for t in range(T):
            nc.vector.max(top_p[:, t, :], probs[:, t, :]).then_inc(top, 1)
        dve.wait_ge(top, T)
        for t in range(T):
            nc.vector.max_index(raw[:, t, :], top_p[:, t, :], probs[:, t, :]).then_inc(top, 1)
        link(nc.vector.tensor_tensor(both[:, :], top_p[:, :, 0], top_p[:, :, 1], ALU.add))
        link(nc.vector.reciprocal(both[:, :], both[:, :]))
        link(nc.vector.tensor_tensor(weights[:, :, :], top_p[:, :, 0:TOPK],
                                     both[:, :].unsqueeze(2).broadcast_to([P, T, TOPK]), ALU.mult))
        dve.wait_ge(top, 2 * T)
        link(nc.vector.tensor_copy(top_i[:, :, :], raw[:, :, 0:TOPK]))

    @stage.scalar
    def _(act):
        act.wait_ge(shifted, 1)
        nc.scalar.activation(probs[:, :, :], logits[:, :, :], ACT.Exp).then_inc(exped, 1)

    return stage


def stage_dispatch(c, s, tag, src, mean, rstd, q, place, slots):
    nc = c.nc
    stage = Stage()
    rows = s.enter_context(nc.sbuf_tensor(tag + "_rows", [P, U, D], F32))
    idx = s.enter_context(nc.sbuf_tensor(tag + "_idx", [P, U, TOPK], I32))
    idx_ready, rows_ready, cast = (c.semaphore(f"{tag}_{n}") for n in ("idx_ready", "rows_ready", "cast"))
    placed = [c.semaphore(f"{tag}_placed{k}") for k in range(U)]

    @stage.vector
    def _(dve):
        nc.vector.tensor_copy(place[:, :, :], q.rearrange("p (t e) -> p t e", e=TOPK)).then_inc(cast, 1)
        dve.wait_ge(cast, 1)

        def body(i, first):
            for k in range(U):
                t = i * U + k
                if not first:
                    wait_slot(dve, placed[k], i * (16 * TOPK))
                nc.vector.tensor_copy(idx[:, k, :], flat(place[:, ds(t, 1), :])).then_inc(idx_ready, 1)
                nc.vector.tensor_scalar(rows[:, k, :], flat(src[:, ds(t, 1), :]), mean[:, ds(t, 1)], rstd[:, ds(t, 1)],
                                        ALU.subtract, ALU.mult).then_inc(rows_ready, 1)

        repeat(dve, T // U, body)

    @stage.gpsimd
    def _(pool):
        with pool.Fori(0, T // U) as i:
            for k in range(U):
                pool.wait_ge(idx_ready, i * U + k + 1)
                wait_slot(pool, rows_ready, i * U + k + 1)
                for e in range(TOPK):
                    nc.gpsimd.indirect_dma_start(
                        out=slots, out_offset=bass.IndirectOffsetOnAxis(ap=idx[:, k, e:e + 1], axis=0),
                        in_=rows[:, k, :], in_offset=None).then_inc(placed[k], 16)
        for k in range(U):
            pool.wait_ge(placed[k], 16 * TOPK * T // U)

    return stage


def stage_expert_blocks(c, s, tag, slots, results, experts_of, w1, w2, gain, shift, bias1, bias2):
    nc = c.nc
    HC = H0 // 128
    KC = D // 128
    Q = B // 128
    assert BLOCKS % 2 == 0
    stage = Stage()
    sb = lambda n, shape, dt=F32: s.enter_context(nc.sbuf_tensor(f"{tag}_{n}", shape, dt))
    w1_sb = [sb(f"w1_{b}", [128, KC, H0]) for b in range(2)]
    w2_sb = [sb(f"w2_{b}", [128, HC, D]) for b in range(2)]
    rows = [sb(f"rows_{b}", [128, Q, D]) for b in range(2)]
    rows_t = [sb(f"rows_t_{b}", [128, KC, B]) for b in range(2)]
    hidden = sb("hidden", [128, HC, B])
    y = [sb(f"y_{b}", [128, Q, D]) for b in range(2)]
    ps_t = bank(c, s, f"{tag}_ps_t")[:, 0:KC * B].rearrange("p (j n) -> p j n", j=KC)
    ps_h = [bank(c, s, f"{tag}_ps_h{b}")[:, 0:B] for b in range(4)]
    ps_y = [bank(c, s, f"{tag}_ps_y{b}")[:, 0:D] for b in range(Q)]
    sem = lambda n: c.semaphore(f"{tag}_{n}")
    turned, scaled, up, gelu_done, down, y_ready = (
        sem(n) for n in ("turned", "scaled", "up", "gelu_done", "down", "y_ready"))
    rows_in, w1_in, w2_in, y_out = ([sem(f"{n}{b}") for b in range(2)] for n in ("rows_in", "w1_in", "w2_in", "y_out"))
    slots_v = slots.rearrange("(n q p) f -> n p q f", q=Q, p=128)
    results_v = results.rearrange("(n q p) f -> n p q f", q=Q, p=128)

    @stage.sync
    def _(sp):
        def load_weights(n, b):
            e = sp.value_load(experts_of[0:1, ds(n, 1)], min_val=0, max_val=EXPERTS - 1)
            sp.dma_start(w1_sb[b][:, :, :], w1[ds(e, 1)].rearrange("a p j h -> (a p) j h")).then_inc(w1_in[b], 16)
            sp.dma_start(w2_sb[b][:, :, :], w2[ds(e, 1)].rearrange("a p j h -> (a p) j h")).then_inc(w2_in[b], 16)

        def load_rows(n, b):
            sp.dma_start(rows[b][:, :, :], slots_v[ds(n, 1)].rearrange("a p q f -> (a p) q f")).then_inc(rows_in[b], 16)

        def store(n, b):
            sp.dma_start(results_v[ds(n, 1)].rearrange("a p q f -> (a p) q f"), y[b][:, :, :]).then_inc(y_out[b], 16)

        for b in range(2):
            load_rows(b, b)
            load_weights(b, b)
        with sp.Fori(0, BLOCKS // 2 - 1) as i:
            for b in range(2):
                n = i * 2 + b + 2
                wait_slot(sp, turned, n - 1)
                load_rows(n, b)
                wait_slot(sp, down, (n - 1) * Q)
                load_weights(n, b)
                wait_slot(sp, y_ready, (n - 1) * Q)
                store(n - 2, b)
        sp.wait_ge(turned, BLOCKS - 1)
        load_rows(BLOCKS, 0)
        for b in range(2):
            sp.wait_ge(y_ready, (BLOCKS - 1 + b) * Q)
            store(BLOCKS - 2 + b, b)
        for b in range(2):
            sp.wait_ge(y_out[b], 16 * BLOCKS // 2)

    @stage.vector
    def _(dve):
        def scale_rows(n, b):
            e = dve.value_load(experts_of[0:1, ds(n, 1)], min_val=0, max_val=EXPERTS - 1)
            wait_slot(dve, turned, n + 1)
            for j in range(KC):
                last = nc.vector.tensor_scalar(rows_t[b][:, j, :], ps_t[:, j, :], gain[:, ds(e * KC + j, 1)],
                                               shift[:, ds(e * KC + j, 1)], ALU.mult, ALU.add)
            last.then_inc(scaled, 1)

        def body(i, first):
            for b in range(2):
                n = i * 2 + b
                scale_rows(n + 1, 1 - b)
                e = dve.value_load(experts_of[0:1, ds(n, 1)], min_val=0, max_val=EXPERTS - 1)
                if not first:
                    wait_slot(dve, y_out[b], i * 16)
                for q in range(Q):
                    wait_slot(dve, down, n * Q + q + 1)
                    nc.vector.tensor_tensor(y[b][:, q, :], ps_y[q], flat(bias2[:, ds(e, 1), :]), ALU.add).then_inc(y_ready, 1)

        scale_rows(0, 0)
        repeat(dve, BLOCKS // 2, body)

    @stage.scalar
    def _(act):
        with act.Fori(0, BLOCKS // 2) as i:
            for b in range(2):
                n = i * 2 + b
                e = act.value_load(experts_of[0:1, ds(n, 1)], min_val=0, max_val=EXPERTS - 1)
                for h in range(HC):
                    wait_slot(act, up, n * HC + h + 1)
                    nc.scalar.activation(hidden[:, h, :], ps_h[h % 4], ACT.Gelu,
                                         bias=bias1[:, ds(e * HC + h, 1)]).then_inc(gelu_done, 1)

    @stage.tensor
    def _(pe):
        def turn_rows(b, arrived):
            wait_slot(pe, rows_in[b], arrived)
            for q in range(Q):
                for j in range(KC):
                    last = nc.tensor.transpose(ps_t[:, j, q * 128:(q + 1) * 128],
                                               rows[b][:, q, j * 128:(j + 1) * 128], c.ident[:, :])
            last.then_inc(turned, 1)

        def body(i, first):
            for b in range(2):
                n = i * 2 + b
                pe.wait_ge(w1_in[b], i * 16 + 16)
                wait_slot(pe, scaled, n + 1)
                for h in range(HC):
                    if not (first and b == 0 and h < 4):
                        wait_slot(pe, gelu_done, n * HC + h - 3)
                    for j in range(KC):
                        last = nc.tensor.matmul(ps_h[h % 4], w1_sb[b][:, j, h * 128:(h + 1) * 128], rows_t[b][:, j, :],
                                                start=(j == 0), stop=(j == KC - 1))
                    last.then_inc(up, 1)
                turn_rows(1 - b, i * 16 + 16 + 16 * b)
                pe.wait_ge(w2_in[b], i * 16 + 16)
                if not (first and b == 0):
                    pe.wait_ge(y_ready, n * Q)
                wait_slot(pe, gelu_done, (n + 1) * HC)
                for q in range(Q):
                    for h in range(HC):
                        last = nc.tensor.matmul(ps_y[q], hidden[:, h, q * 128:(q + 1) * 128], w2_sb[b][:, h, :],
                                                start=(h == 0), stop=(h == HC - 1))
                    last.then_inc(down, 1)

        turn_rows(0, 16)
        repeat(pe, BLOCKS // 2, body)

    return stage


def stage_combine(c, s, tag, results, place, weights, acc):
    nc = c.nc
    stage = Stage()
    got = s.enter_context(nc.sbuf_tensor(tag + "_got", [P, U, TOPK, D], F32))
    idx = s.enter_context(nc.sbuf_tensor(tag + "_idx", [P, U, TOPK], I32))
    staged, added = c.semaphore(tag + "_staged"), c.semaphore(tag + "_added")
    gathered = [c.semaphore(f"{tag}_gathered{k}") for k in range(U)]

    @stage.scalar
    def _(act):
        def body(i, first):
            for k in range(U):
                t = i * U + k
                if not first:
                    wait_slot(act, added, (t - U + 1) * TOPK)
                nc.scalar.copy(idx[:, k, :], flat(place[:, ds(t, 1), :])).then_inc(staged, 1)

        repeat(act, T // U, body)

    @stage.gpsimd
    def _(pool):
        with pool.Fori(0, T // U) as i:
            for k in range(U):
                wait_slot(pool, staged, i * U + k + 1)
                for e in range(TOPK):
                    nc.gpsimd.indirect_dma_start(
                        out=got[:, k, e, :], out_offset=None, in_=results,
                        in_offset=bass.IndirectOffsetOnAxis(ap=idx[:, k, e:e + 1], axis=0)).then_inc(gathered[k], 16)

    @stage.vector
    def _(dve):
        with dve.Fori(0, T // U) as i:
            for k in range(U):
                t = i * U + k
                here = flat(acc[:, ds(t, 1), :])
                wait_slot(dve, gathered[k], (i + 1) * (16 * TOPK))
                for e in range(TOPK):
                    if e:
                        wait_slot(dve, added, t * TOPK + e)
                    nc.vector.scalar_tensor_tensor(
                        out=here, in0=got[:, k, e, :], scalar=weights[:, ds(t, 1), e], in1=here,
                        op0=ALU.mult, op1=ALU.add).then_inc(added, 1)
        dve.wait_ge(added, T * TOPK)

    return stage


def stage_degree(c, s, tag, rec, tile_of, deg):
    nc = c.nc
    W = 10
    stage = Stage()
    sb = lambda n, shape, dt=BF16: s.enter_context(nc.sbuf_tensor(f"{tag}_{n}", shape, dt))
    of_row, of_tile = sb("of_row", [P, 2, W, P]), sb("of_tile", [P, 2, W, T])
    none = sb("none", [P, P])
    ps = bank(c, s, f"{tag}_ps")[0:P, 0:T]
    zeroed, made, used, whole = (c.semaphore(f"{tag}_{n}") for n in ("zeroed", "made", "used", "whole"))

    @stage.vector
    def _(dve):
        nc.vector.memset(none[:, :], 0.0).then_inc(zeroed, 1)

        def body(i, first):
            for h in range(2):
                at = i * (2 * W) + h * W
                if not first:
                    wait_slot(dve, used, i * 2 - 1 + h)
                nc.vector.tensor_tensor(of_row[:, h, :, :], rec[:, ds(at, W), 0].unsqueeze(2).broadcast_to([P, W, P]),
                                        c.iota[0:P, 0:P].unsqueeze(1).broadcast_to([P, W, P]), ALU.is_equal)
                nc.vector.tensor_tensor(of_tile[:, h, :, :], tile_of[:, ds(at, W)].unsqueeze(2).broadcast_to([P, W, T]),
                                        c.iota[0:P, 0:T].unsqueeze(1).broadcast_to([P, W, T]),
                                        ALU.is_equal).then_inc(made, 1)

        repeat(dve, EC // (2 * W), body)
        dve.wait_ge(whole, 1)
        nc.vector.tensor_copy(deg[:, :], ps).then_inc(zeroed, 1)
        dve.wait_ge(zeroed, 2)

    @stage.tensor
    def _(pe):
        pe.wait_ge(zeroed, 1)
        nc.tensor.matmul(ps, none[:, 0:P], none[:, 0:T], start=True, stop=False)
        with pe.Fori(0, EC // (2 * W)) as i:
            for h in range(2):
                wait_slot(pe, made, i * 2 + h + 1)
                for k in range(W):
                    last = nc.tensor.matmul(ps, of_row[:, h, k, :], of_tile[:, h, k, :], start=False, stop=False)
                last.then_inc(used, 1)
        nc.tensor.matmul(ps, none[:, 0:P], none[:, 0:T], start=False, stop=True).then_inc(whole, 1)

    return stage


def stage_degree_norm(c, s, tag, deg, dinv):
    nc = c.nc
    stage = Stage()
    root = s.enter_context(nc.sbuf_tensor(tag + "_root", [P, T], F32))
    chain, rooted = (c.semaphore(f"{tag}_{n}") for n in ("chain", "rooted"))

    @stage.vector
    def _(dve):
        nc.vector.tensor_scalar(deg[:, :], deg[:, :], 1.0, 1.0, ALU.add, ALU.max).then_inc(chain, 1)
        dve.wait_ge(rooted, 1)
        nc.vector.reciprocal(dinv[:, :], root[:, :]).then_inc(chain, 1)
        dve.wait_ge(chain, 2)

    @stage.scalar
    def _(act):
        act.wait_ge(chain, 1)
        nc.scalar.activation(root[:, :], deg[:, :], ACT.Sqrt).then_inc(rooted, 1)

    return stage


def stage_batch_norm(c, s, tag, acc, width, dinv, bias, gain, shift):
    nc = c.nc
    stage = Stage()
    sb = lambda n, shape: s.enter_context(nc.sbuf_tensor(f"{tag}_{n}", shape, F32))
    square, part = sb("square", [P, T, width]), sb("part", [P, width])
    mean, var, std = sb("mean", [P, width]), sb("var", [P, width]), sb("std", [P, width])
    ps = bank(c, s, f"{tag}_ps")[0:P, 0:width]
    chain, part_ready, summed, var_ready, std_ready = (
        c.semaphore(f"{tag}_{n}") for n in ("chain", "part_ready", "summed", "var_ready", "std_ready"))
    rows = lambda v: v[0:P, 0:width].unsqueeze(1).broadcast_to([P, T, width])

    @stage.vector
    def _(dve):
        V = nc.vector
        link = linker(dve, chain)
        link(V.tensor_tensor(acc[:, :, :], acc[:, :, :], dinv[:, :].unsqueeze(2).broadcast_to([P, T, width]), ALU.mult))
        link(V.tensor_tensor(acc[:, :, :], acc[:, :, :], rows(bias), ALU.add))
        V.tensor_reduce(part[:, :], acc[:, :, :].rearrange("p t f -> p f t"), AX.X, ALU.add).then_inc(part_ready, 1)
        dve.wait_ge(summed, 1)
        link(V.tensor_scalar(mean[:, :], ps, 1.0 / NODES, None, ALU.mult))
        link(V.tensor_tensor(acc[:, :, :], acc[:, :, :], rows(mean), ALU.subtract))
        link(V.tensor_tensor(square[:, :, :], acc[:, :, :], acc[:, :, :], ALU.mult))
        V.tensor_reduce(part[:, :], square[:, :, :].rearrange("p t f -> p f t"), AX.X, ALU.add).then_inc(part_ready, 1)
        dve.wait_ge(summed, 2)
        V.tensor_scalar(var[:, :], ps, 1.0 / NODES, BN_EPS, ALU.mult, ALU.add).then_inc(var_ready, 1)
        dve.wait_ge(std_ready, 1)
        link(V.reciprocal(var[:, :], std[:, :]))
        link(V.tensor_tensor(var[:, :], var[:, :], gain[0:P, :], ALU.mult))
        link(V.tensor_tensor(acc[:, :, :], acc[:, :, :], rows(var), ALU.mult))
        link(V.tensor_tensor(acc[:, :, :], acc[:, :, :], rows(shift), ALU.add))
        link(V.tensor_scalar(acc[:, :, :], acc[:, :, :], 0.0, None, ALU.max))

    @stage.scalar
    def _(act):
        act.wait_ge(var_ready, 1)
        nc.scalar.activation(std[:, :], var[:, :], ACT.Sqrt).then_inc(std_ready, 1)

    @stage.tensor
    def _(pe):
        for n in range(2):
            pe.wait_ge(part_ready, n + 1)
            nc.tensor.matmul(ps, c.ones[0:P, 0:P], part[:, :], start=True, stop=True).then_inc(summed, 1)

    return stage


def stage_fc_end(c, s, tag, fc, bias, acc):
    nc = c.nc
    stage = Stage()
    chain = c.semaphore(tag + "_chain")

    @stage.vector
    def _(dve):
        link = linker(dve, chain)
        link(nc.vector.tensor_tensor(fc[:, :, :], fc[:, :, :], bias[0:P, :].unsqueeze(1).broadcast_to([P, T, D]), ALU.add))
        link(nc.vector.scalar_tensor_tensor(out=acc[:, :, :], in0=fc[:, :, :], scalar=0.0, in1=acc[:, :, :],
                                            op0=ALU.max, op1=ALU.add))

    return stage


def stage_pick_experts(c, s, tag, rows_ready, rows_t, router, bias, picked, picked_w):
    nc = c.nc
    E = EXPERTS
    capacity = float(-(-NODES * 125 // (100 * E)))
    stage = Stage()
    sb = lambda n, shape, dt=F32: s.enter_context(nc.sbuf_tensor(f"{tag}_{n}", shape, dt))
    mean = sb("mean", [128, 2])
    z, p, load, one, top, top_w = (sb("z", [1, E]), sb("p", [1, E]), sb("load", [1, E]), sb("one", [1, 1]),
                                   sb("top", [1, 8]), sb("top_w", [1, TOPK]))
    top_i = sb("top_i", [1, 8], U32)
    ps_l, ps_w = bank(c, s, f"{tag}_ps_l")[0:1, 0:E], bank(c, s, f"{tag}_ps_w")[:, 0:TOPK]
    chain, mean_ready, product, to_exp, exped, weights_ready = (
        c.semaphore(f"{tag}_{n}")
        for n in ("chain", "mean_ready", "product", "to_exp", "exped", "weights_ready"))

    @stage.vector
    def _(dve):
        V = nc.vector
        link = linker(dve, chain)
        rounds = [0]

        def softmax(src, out, n, signal=None):
            rounds[0] += 1
            link(V.tensor_reduce(one[:, :], src[0:1, 0:n], AX.X, ALU.max))
            V.tensor_scalar(z[0:1, 0:n], src[0:1, 0:n], one[0:1, 0:1], None, ALU.subtract).then_inc(to_exp, 1)
            dve.wait_ge(exped, rounds[0])
            link(V.tensor_reduce(one[:, :], p[0:1, 0:n], AX.X, ALU.add))
            link(V.reciprocal(one[:, :], one[:, :]))
            scaled = V.tensor_scalar(out[0:1, 0:n], p[0:1, 0:n], one[0:1, 0:1], None, ALU.mult)
            if signal is None:
                link(scaled)
            else:
                scaled.then_inc(signal, 1)

        dve.wait_ge(*rows_ready)
        link(V.tensor_reduce(mean[:, :], rows_t[:, :, :], AX.X, ALU.add))
        V.tensor_scalar(mean[:, :], mean[:, :], 1.0 / NODES, None, ALU.mult).then_inc(mean_ready, 1)
        dve.wait_ge(product, 1)
        link(V.tensor_tensor(p[:, :], ps_l, bias[0:1, :], ALU.add))
        softmax(p, p, E)
        link(V.tensor_scalar(load[:, :], p[:, :], float(NODES), None, ALU.mult))
        link(V.reciprocal(load[:, :], load[:, :]))
        link(V.tensor_scalar(load[:, :], load[:, :], capacity, 1.0, ALU.mult, ALU.min))
        link(V.tensor_tensor(p[:, :], p[:, :], load[:, :], ALU.mult))
        softmax(p, p, E)
        link(V.max(top[:, :], p[:, :]))
        link(V.max_index(top_i[:, :], top[:, :], p[:, :]))
        link(V.tensor_copy(picked[:, :], top_i[0:1, 0:TOPK]))
        softmax(top, top_w, TOPK, signal=weights_ready)
        dve.wait_ge(product, 2)
        link(V.tensor_copy(picked_w[:, :], ps_w))

    @stage.scalar
    def _(act):
        for n, width in enumerate((E, E, TOPK)):
            act.wait_ge(to_exp, n + 1)
            nc.scalar.activation(p[0:1, 0:width], z[0:1, 0:width], ACT.Exp).then_inc(exped, 1)

    @stage.tensor
    def _(pe):
        pe.wait_ge(mean_ready, 1)
        for j in range(2):
            last = nc.tensor.matmul(ps_l, mean[:, j:j + 1], router[:, j, :], start=(j == 0), stop=(j == 1))
        last.then_inc(product, 1)
        pe.wait_ge(weights_ready, 1)
        nc.tensor.matmul(ps_w, c.ones[0:1, :], top_w[:, :], start=True, stop=True).then_inc(product, 1)

    return stage


def stage_shared_ffn(c, s, tag, rows_t, picked, picked_w, w1, w2, b1, b2, mean, rstd, out_z):
    nc = c.nc
    FC, KC = H1 // 128, D // 128
    F = TOPK * FC
    stage = Stage()
    sb = lambda n, shape, dt=F32: s.enter_context(nc.sbuf_tensor(f"{tag}_{n}", shape, dt))
    w1_sb, w2_sb = sb("w1", [128, TOPK, KC, H1]), sb("w2", [128, F, D])
    b1_sb, b2_sb = sb("b1", [128, TOPK, FC]), sb("b2", [P, TOPK, D])
    hidden = [sb(f"hidden{b}", [128, F, P]) for b in range(2)]
    ps_h = [bank(c, s, f"{tag}_ps_h{b}")[:, 0:P] for b in range(4)]
    ps_y = [bank(c, s, f"{tag}_ps_y{b}")[0:P, 0:D] for b in range(2)]
    sem = lambda n: c.semaphore(f"{tag}_{n}")
    w1_in, w2_in, b2_in, chain, w2_scaled, up, gelu_done, down, taken, normal = (
        sem(n) for n in ("w1_in", "w2_in", "b2_in", "chain", "w2_scaled", "up", "gelu_done", "down", "taken", "normal"))

    @stage.sync
    def _(sp):
        for k in range(TOPK):
            e = sp.value_load(picked[0:1, k:k + 1], min_val=0, max_val=EXPERTS - 1)
            sp.dma_start(w1_sb[:, k, :, :], w1[ds(e, 1)].rearrange("a p j h -> (a p) j h")).then_inc(w1_in, 16)
            sp.dma_start(b1_sb[:, k, :], b1[ds(e, 1)].rearrange("a p j -> (a p) j")).then_inc(w1_in, 16)
            sp.dma_start(w2_sb[:, k * FC:(k + 1) * FC, :], w2[ds(e, 1)].rearrange("a p j h -> (a p) j h")).then_inc(w2_in, 16)
            sp.dma_start(b2_sb[:, k, :], b2[ds(e, 1), :].broadcast_to([P, D])).then_inc(b2_in, 16)

    @stage.vector
    def _(dve):
        V = nc.vector
        link = linker(dve, chain)
        dve.wait_ge(w2_in, 32)
        for k in range(TOPK):
            V.tensor_scalar(w2_sb[:, k * FC:(k + 1) * FC, :], w2_sb[:, k * FC:(k + 1) * FC, :],
                            picked_w[:, k:k + 1], None, ALU.mult).then_inc(w2_scaled, 1)
        dve.wait_ge(b2_in, 32)
        link(V.tensor_scalar(b2_sb[:, 0, :], b2_sb[:, 0, :], picked_w[0:P, 0:1], None, ALU.mult))
        link(V.scalar_tensor_tensor(out=b2_sb[:, 0, :], in0=b2_sb[:, 1, :], scalar=picked_w[0:P, 1:2],
                                    in1=b2_sb[:, 0, :], op0=ALU.mult, op1=ALU.add))

        def take(t, b):
            here = out_z[:, ds(t, 1), :].rearrange("p a f -> p (a f)")
            V.tensor_scalar(here, c.x[:, ds(t, 1), :].rearrange("p a f -> p (a f)"), mean[:, ds(t, 1)],
                            rstd[:, ds(t, 1)], ALU.subtract, ALU.mult).then_inc(normal, 1)
            wait_slot(dve, normal, t * 2 + 1)
            V.tensor_tensor(here, here, b2_sb[:, 0, :], ALU.add).then_inc(normal, 1)
            dve.wait_ge(normal, t * 2 + 2)
            wait_slot(dve, down, t + 1)
            V.tensor_tensor(here, here, ps_y[b], ALU.add).then_inc(taken, 1)

        with dve.Fori(0, T // 2) as i:
            for b in range(2):
                take(i * 2 + b, b)
        take(T - 1, 0)
        dve.wait_ge(taken, T)

    @stage.scalar
    def _(act):
        act.wait_ge(w1_in, 64)

        def gelu(t, b):
            for f in range(F):
                wait_slot(act, up, t * F + f + 1)
                nc.scalar.activation(hidden[b][:, f, :], ps_h[f % 4], ACT.Gelu,
                                     bias=b1_sb[:, f // FC, f % FC:f % FC + 1]).then_inc(gelu_done, 1)

        with act.Fori(0, T // 2) as i:
            for b in range(2):
                gelu(i * 2 + b, b)
        gelu(T - 1, 0)

    @stage.tensor
    def _(pe):
        def rise(t, first=False):
            for f in range(F):
                if not (first and f < 4):
                    wait_slot(pe, gelu_done, t * F + f - 3)
                for j in range(KC):
                    last = nc.tensor.matmul(ps_h[f % 4], w1_sb[:, f // FC, j, (f % FC) * 128:(f % FC + 1) * 128],
                                            rows_t[:, j, ds(t * P, P)], start=(j == 0), stop=(j == KC - 1))
                last.then_inc(up, 1)

        def fall(t, b, first=False):
            if not first:
                wait_slot(pe, taken, t - 1)
            wait_slot(pe, gelu_done, (t + 1) * F)
            for f in range(F):
                last = nc.tensor.matmul(ps_y[b], hidden[b][:, f, :], w2_sb[:, f, :], start=(f == 0), stop=(f == F - 1))
            last.then_inc(down, 1)

        def body(i, first):
            for b in range(2):
                rise(i * 2 + b + 1)
                fall(i * 2 + b, b, first)

        pe.wait_ge(w1_in, 64)
        rise(0, first=True)
        pe.wait_ge(w2_scaled, TOPK)
        repeat(pe, T // 2, body)
        fall(T - 1, 0)

    return stage


def stage_last(c, s, tag, z, mean, rstd, gamma, beta, out):
    nc = c.nc
    stage = Stage()
    chain, stored = c.semaphore(tag + "_chain"), c.semaphore(tag + "_stored")
    out_v = out.rearrange("(t p) f -> p t f", p=P)

    @stage.vector
    def _(dve):
        V = nc.vector
        link = linker(dve, chain)
        all_rows = lambda v: v[0:P, :].unsqueeze(1).broadcast_to([P, U, D])
        for g in range(T // U):
            part_z, part_x = z[:, g * U:(g + 1) * U, :], c.x[:, g * U:(g + 1) * U, :]
            wide = lambda v: v[:, g * U:(g + 1) * U].unsqueeze(2).broadcast_to([P, U, D])
            link(V.tensor_tensor(part_z, part_z, wide(mean), ALU.subtract))
            link(V.tensor_tensor(part_z, part_z, wide(rstd), ALU.mult))
            link(V.tensor_tensor(part_z, part_z, all_rows(gamma), ALU.mult))
            link(V.tensor_tensor(part_z, part_z, all_rows(beta), ALU.add))
            link(V.tensor_tensor(part_z, part_z, part_x, ALU.add))

    @stage.sync
    def _(sp):
        for g in range(T // U):
            sp.wait_ge(chain, 5 * (g + 1))
            sp.dma_start(out_v[:, g * U:(g + 1) * U, :], z[:, g * U:(g + 1) * U, :]).then_inc(stored, 16)
        sp.wait_ge(stored, 16 * T // U)

    return stage


def flat(ap):
    return ap.rearrange("p a f -> p (a f)")


def allocator(nc, stack):
    return lambda name, shape, dt=F32: stack.enter_context(nc.sbuf_tensor(name, shape, dt))


def halves(w):
    return w.rearrange("(j p) m -> p j m", p=128)


def layer0_graph(c, scratch, mean, rstd, g1):
    nc, args = c.nc, c.args
    V = nc.vector
    with ExitStack() as s:
        sb = allocator(nc, s)
        w = sb("g0_w", [128, 2, D])
        table, tiles_of = sb("g0_table", [S, SLOTS, 4]), sb("g0_tiles_of", [1, PAIRS], I32)
        with ExitStack() as s1:
            sb1 = allocator(nc, s1)
            rec, tile_of_edge, place_i = sb1("g0_rec", [P, EC, 4]), sb1("g0_tile", [P, EC]), sb1("g0_place_i", [P, EC], I32)
            q, ends = sb1("g0_q", [P, EC]), sb1("g0_ends", [P, T])
            edges = stage_load_edges(c, s1, "edges")
            with ExitStack() as s2:
                run(c, stage_constants(c, s2), edges, stage_load(c, s2, "g0_w", [(w[:, :, :], halves(args["g0_w"]))]))
                run(c, stage_fill(c, s2, "fill", [scratch["rows0"], scratch["rows1"]], scratch["slots"]),
                    stage_edge_records(c, s2, "g0r", c.src_i, c.dst_i, rec, tile_of_edge),
                    rank := stage_rank_buckets(c, s2, "g0k", tile_of_edge, EC, T, 2 * S, q, ends),
                    stage_places(c, s2, "g0p", q, place_i),
                    stage_bucket_table(c, s2, "g0t", rank, ends, T, PAIRS, tiles_of))
            with ExitStack() as s2:
                sb2 = allocator(nc, s2)
                support = sb2("g0_support", [P, T, D])
                g1_tile, g1_q, g1_ends = sb2("g1_tile", [P, EC]), sb2("g1_q", [P, EC]), sb2("g1_ends", [P, T])
                run(c, stage_norm_stats(c, s2, "g0", c.x, mean, rstd),
                    stage_project(c, s2, "g0x", c.x, D, w, D,
                                  lambda t, ps: [lambda: V.tensor_copy(flat(support[:, ds(t, 1), :]), ps)],
                                  norm=(mean, rstd), dram=(scratch["support"], support[:, :, :])),
                    stage_edge_records(c, s2, "g1r", c.dst_i, c.src_i, g1["rec"], g1_tile),
                    stage_degree(c, s2, "g1d", g1["rec"], g1_tile, g1["dinv"]),
                    stage_degree_norm(c, s2, "g1n", g1["dinv"], g1["dinv"]),
                    rank := stage_rank_buckets(c, s2, "g1k", g1_tile, EC, T, 2 * S, g1_q, g1_ends),
                    stage_places(c, s2, "g1p", g1_q, g1["place_i"]),
                    stage_bucket_table(c, s2, "g1t", rank, g1_ends, T, PAIRS, g1["tiles_of"]),
                    stage_scatter_records(c, s2, "g0s", rec, place_i, scratch["rows0"], table))
        with ExitStack() as s1:
            run(c, stage_aggregate(c, s1, "g0a", table, tiles_of, scratch["support"], D, c.x, weighted=True))


def layer0_ffn(c, scratch, mean, rstd, g1):
    nc, args = c.nc, c.args
    with ExitStack() as s:
        sb = allocator(nc, s)
        place, weights = sb("f0_place", [P, T, TOPK], I32), sb("f0_weights", [P, T, TOPK])
        experts_of = sb("f0_experts_of", [1, BLOCKS + 1], I32)
        with ExitStack() as s2:
            sb2 = allocator(nc, s2)
            xt, router, bias = sb2("f0_xt", [P, T, D]), sb2("f0_router", [128, 2, EXPERTS]), sb2("f0_bias", [128, EXPERTS])
            mean2, rstd2 = sb2("f0_mean2", [P, T]), sb2("f0_rstd2", [P, T])
            logits, probs, top_i = sb2("f0_logits", [P, T, EXPERTS]), sb2("f0_probs", [P, T, EXPERTS]), sb2("f0_top_i", [P, T, TOPK])
            q, ends = sb2("f0_q", [P, T * TOPK]), sb2("f0_ends", [P, EXPERTS])
            run(c, stage_load(c, s2, "f0_router", [(router[:, :, :], halves(args["f0_wr"])),
                                                   (bias[:, :], row_to_all(args["f0_br"], 128))]),
                stage_norm_stats(c, s2, "f0", c.x, mean, rstd),
                stage_normalise(c, s2, "f0n", c.x, mean, rstd, xt))
            run(c, stage_norm_stats(c, s2, "f0b", xt, mean2, rstd2),
                stage_project(c, s2, "f0x", xt, D, router, EXPERTS,
                              lambda t, ps: [lambda: nc.vector.tensor_copy(flat(logits[:, ds(t, 1), :]), ps)]),
                stage_route(c, s2, "f0r", logits, bias, probs, top_i, weights),
                rank := stage_rank_buckets(c, s2, "f0k", flat(top_i[:, :, :]), T * TOPK, EXPERTS, B, q, ends),
                stage_bucket_table(c, s2, "f0t", rank, ends, EXPERTS, BLOCKS + 1, experts_of),
                stage_dispatch(c, s2, "f0d", xt, mean2, rstd2, q[:, :], place, scratch["slots"]))
        with ExitStack() as s2:
            sb2 = allocator(nc, s2)
            gain, shift = sb2("f0_gain", [128, EXPERTS * 2]), sb2("f0_shift", [128, EXPERTS * 2])
            bias1, bias2 = sb2("f0_bias1", [128, EXPERTS * H0 // 128]), sb2("f0_bias2", [128, EXPERTS, D])
            run(c, stage_load(c, s2, "f0_params", [
                (gain[:, :], args["f0_g"]), (shift[:, :], args["f0_b"]), (bias1[:, :], args["f0_b1"]),
                (flat(bias2[:, :, :]), row_to_all(args["f0_b2"].rearrange("e d -> (e d)"), 128))]))
            run(c, stage_expert_blocks(c, s2, "f0e", scratch["slots"], scratch["results"], experts_of, args["f0_w1"],
                                       args["f0_w2"], gain, shift, bias1, bias2),
                stage_scatter_records(c, s2, "g1s", g1["rec"], g1["place_i"], scratch["rows1"], g1["table"]))
        with ExitStack() as s2:
            run(c, stage_combine(c, s2, "f0c", scratch["results"], place, weights, c.x))


def layer1_graph(c, scratch, mean, rstd, g1):
    nc, args = c.nc, c.args
    V = nc.vector
    with ExitStack() as s:
        sb = allocator(nc, s)
        table, tiles_of, dinv = g1["table"], g1["tiles_of"], g1["dinv"]
        fc = sb("g1_fc", [P, T, D])
        w1, w2, w3 = sb("g1_w1", [128, 2, C1 + D]), sb("g1_w2", [128, 1, C2 + D]), sb("g1_w3", [C2, 1, D])
        vec = {n: sb("g1_" + n, [P, args["g1_" + n].shape[0]]) for n in ("b1", "g1", "be1", "b2", "g2", "be2", "bfc")}
        h1, h2 = sb("g1_h1", [P, T, C1]), sb("g1_h2", [P, T, C2])
        wfc = args["g1_wfc"]
        with ExitStack() as s2:
            run(c, stage_load(c, s2, "g1_w", [
                (w1[:, :, 0:C1], halves(args["g1_w1"])), (w1[:, :, C1:], halves(wfc[0:D, :])),
                (w2[:, 0, 0:C2], args["g1_w2"]), (w2[:, 0, C2:], wfc[D:D + C1, :]), (w3[:, 0, :], wfc[D + C1:, :])]
                + [(v[:, :], row_to_all(args["g1_" + n], P)) for n, v in vec.items()]),
                stage_norm_stats(c, s2, "g1", c.x, mean, rstd))
            run(c, stage_project(c, s2, "g1a", c.x, D, w1, C1 + D, lambda t, ps: [
                lambda: V.tensor_scalar(flat(h1[:, ds(t, 1), :]), ps[:, 0:C1], dinv[:, ds(t, 1)], None, ALU.mult),
                lambda: V.tensor_copy(flat(fc[:, ds(t, 1), :]), ps[:, C1:])],
                norm=(mean, rstd), dram=(scratch["h1"], h1[:, :, :])))
        with ExitStack() as s2:
            run(c, stage_aggregate(c, s2, "g1b", table, tiles_of, scratch["h1"], C1, h1, weighted=False),
                stage_batch_norm(c, s2, "g1c", h1, C1, dinv, vec["b1"], vec["g1"], vec["be1"]))
        with ExitStack() as s2:
            run(c, stage_project(c, s2, "g1e", h1, C1, w2, C2 + D, lambda t, ps: [
                lambda: V.tensor_scalar(flat(h2[:, ds(t, 1), :]), ps[:, 0:C2], dinv[:, ds(t, 1)], None, ALU.mult),
                lambda: V.tensor_tensor(flat(fc[:, ds(t, 1), :]), flat(fc[:, ds(t, 1), :]), ps[:, C2:], ALU.add)],
                dram=(scratch["h2"], h2[:, :, :])))
        with ExitStack() as s2:
            run(c, stage_aggregate(c, s2, "g1f", table, tiles_of, scratch["h2"], C2, h2, weighted=False),
                stage_batch_norm(c, s2, "g1g", h2, C2, dinv, vec["b2"], vec["g2"], vec["be2"]))
        with ExitStack() as s2:
            run(c, stage_project(c, s2, "g1h", h2, C2, w3, D, lambda t, ps: [
                lambda: V.tensor_tensor(flat(fc[:, ds(t, 1), :]), flat(fc[:, ds(t, 1), :]), ps, ALU.add)]),
                stage_fc_end(c, s2, "g1i", fc, vec["bfc"], c.x))


def layer1_ffn(c, out, mean, rstd):
    nc, args = c.nc, c.args
    with ExitStack() as s:
        sb = allocator(nc, s)
        rows_t, z = sb("f1_rows_t", [128, 2, NODES]), sb("f1_z", [P, T, D])
        router, bias = sb("f1_router", [128, 2, EXPERTS]), sb("f1_bias", [128, EXPERTS])
        gamma, beta = sb("f1_gamma", [128, D]), sb("f1_beta", [128, D])
        picked, picked_w = sb("f1_picked", [1, TOPK], I32), sb("f1_picked_w", [128, TOPK])
        mean2, rstd2 = sb("f1_mean2", [P, T]), sb("f1_rstd2", [P, T])
        with ExitStack() as s2:
            run(c, stage_load(c, s2, "f1_w", [(router[:, :, :], halves(args["f1_wr"])),
                                              (bias[:, :], row_to_all(args["f1_br"], 128)),
                                              (gamma[:, :], row_to_all(args["f1_gamma"], 128)),
                                              (beta[:, :], row_to_all(args["f1_beta"], 128))]),
                stage_norm_stats(c, s2, "f1", c.x, mean, rstd))
            run(c, turn := stage_project(c, s2, "f1a", c.x, D, None, 0, None, norm=(mean, rstd), keep_t=rows_t),
                stage_pick_experts(c, s2, "f1b", turn.kept, rows_t, router, bias, picked, picked_w))
        with ExitStack() as s2:
            run(c, stage_shared_ffn(c, s2, "f1c", rows_t, picked, picked_w, args["f1_w1"], args["f1_w2"], args["f1_b1"],
                                    args["f1_b2"], mean, rstd, z),
                stage_norm_stats(c, s2, "f1d", z, mean2, rstd2),
                stage_last(c, s2, "f1e", z, mean2, rstd2, gamma, beta, out))


def part(nc, emit):
    with nc.cleanup_on_exit():
        emit()
    nc.all_engine_barrier()


def build(nc, args, out, scratch, upto=99):
    with ExitStack() as ctx:
        c = Core(nc, ctx, args)
        c.iota, c.ident = c.keep("iota", [128, 512]), c.keep("ident", [128, 128])
        c.ones, c.before = c.keep("ones", [128, 128]), c.keep("before", [128, 128])
        c.x = c.keep("x_now", [P, T, D])
        mean, rstd = c.keep("mean", [P, T]), c.keep("rstd", [P, T])
        g1 = {"rec": c.keep("g1_rec", [P, EC, 4]), "place_i": c.keep("g1_place_i", [P, EC], I32),
              "dinv": c.keep("g1_dinv", [P, T]), "tiles_of": c.keep("g1_tiles_of", [1, PAIRS], I32),
              "table": c.keep("g1_table", [S, SLOTS, 4])}
        part(nc, lambda: layer0_graph(c, scratch, mean, rstd, g1))
        if upto >= 2:
            part(nc, lambda: layer0_ffn(c, scratch, mean, rstd, g1))
        if upto >= 3:
            part(nc, lambda: layer1_graph(c, scratch, mean, rstd, g1))
        if upto >= 4:
            layer1_ffn(c, out, mean, rstd)
            return
        with nc.Block() as block:
            out_stored = c.semaphore("out_stored")

            @block.sync
            def _(sp):
                sp.dma_start(out.rearrange("(t p) f -> p t f", p=P), c.x[:, :, :]).then_inc(out_stored, 16)
                sp.wait_ge(out_stored, 16)


def lay_out(inputs):
    def a(name):
        return np.ascontiguousarray(inputs[name])

    def by_partition(w):
        e, k, n = w.shape
        return np.ascontiguousarray(w.reshape(e, k // 128, 128, n).transpose(0, 2, 1, 3))

    def columns(v):
        return np.ascontiguousarray(v.reshape(-1, 128).T)

    return {
        "x": a("x"), "src": a("src"), "dst": a("dst"), "edge_weight": a("edge_weight"), "g0_w": a("L0_gnn_weight"),
        "f0_wr": a("L0_ffn_Wr"), "f0_br": a("L0_ffn_br"), "f0_g": columns(a("L0_ffn_ln_g")), "f0_b": columns(a("L0_ffn_ln_b")),
        "f0_w1": by_partition(a("L0_ffn_W1")), "f0_b1": columns(a("L0_ffn_b1")),
        "f0_w2": by_partition(a("L0_ffn_W2")), "f0_b2": a("L0_ffn_b2"),
        "g1_w1": a("L1_gnn_W1"), "g1_b1": a("L1_gnn_b1"), "g1_g1": a("L1_gnn_g1"), "g1_be1": a("L1_gnn_be1"),
        "g1_w2": a("L1_gnn_W2"), "g1_b2": a("L1_gnn_b2"), "g1_g2": a("L1_gnn_g2"), "g1_be2": a("L1_gnn_be2"),
        "g1_wfc": a("L1_gnn_Wfc"), "g1_bfc": a("L1_gnn_bfc"),
        "f1_wr": a("L1_ffn_Wr"), "f1_br": a("L1_ffn_br"), "f1_w1": by_partition(a("L1_ffn_W1")),
        "f1_b1": np.ascontiguousarray(a("L1_ffn_b1").reshape(EXPERTS, H1 // 128, 128).transpose(0, 2, 1)),
        "f1_w2": by_partition(a("L1_ffn_W2")), "f1_b2": a("L1_ffn_b2"),
        "f1_gamma": a("L1_ffn_gamma"), "f1_beta": a("L1_ffn_beta"),
    }


def program(nc, args, out, upto=99):
    dram = lambda name, shape: nc.dram_tensor(name, shape, F32).ap()
    scratch = {
        "support": dram("support", [NODES, D]), "h1": dram("h1", [NODES, C1]), "h2": dram("h2", [NODES, C2]),
        "rows0": dram("rows0", [S * SLOTS, 4]), "rows1": dram("rows1", [S * SLOTS, 4]),
        "slots": dram("slots", [(BLOCKS + 1) * B, D]), "results": dram("results", [BLOCKS * B, D]),
    }
    build(nc, args, out, scratch, upto)


def kernel(**inputs):
    import concourse.bacc as bacc
    from concourse.bass_utils import run_bass_kernel_spmd

    nc = bacc.Bacc("TRN2", target_bir_lowering=False, num_devices=1)
    arrays = {"in_" + k: v for k, v in lay_out(inputs).items()}
    args = {k[3:]: nc.dram_tensor(k, v.shape, mybir.dt.from_np(v.dtype), kind="ExternalInput").ap()
            for k, v in arrays.items()}
    out = nc.dram_tensor("out_0_dram", (NODES, D), F32, kind="ExternalOutput").ap()
    program(nc, args, out)
    r = run_bass_kernel_spmd(nc, [arrays], core_ids=[0])
    return r.results[0]["out_0_dram"]
```

```python
from contextlib import ExitStack

import concourse.bass as bass
import numpy as np
from concourse import mybir
from concourse.alu_op_type import AluOpType as ALU

F32 = mybir.dt.float32
I32 = mybir.dt.int32
U32 = mybir.dt.uint32
BF16, F16 = mybir.dt.bfloat16, mybir.dt.float16
ACT = mybir.ActivationFunctionType
AX = mybir.AxisListType

NODES, D = 3125, 256
P = 125
T = NODES // P
EDGES = 50000
EC = EDGES // P
S = 128
PAIRS = (EDGES + T * (2 * S - 1)) // (2 * S)
SLOTS = 2 * PAIRS
AGGREGATE = 20
AGGREGATE_STEPS = SLOTS // AGGREGATE
assert SLOTS % AGGREGATE == 0
AGGREGATE1_STEPS = -(-((EDGES + T * (S - 1)) // S) // AGGREGATE)
SLOTS1 = AGGREGATE1_STEPS * AGGREGATE
assert SLOTS1 <= SLOTS
BY_PRODUCTS = 160
PARTS = 6
EXPERTS, TOPK = 8, 2
H0, H1 = 1024, 512
B = 256
BLOCKS = (NODES * TOPK + EXPERTS * (B - 1)) // B
C1, C2 = 128, 64
ROUND = 12582912.0
U = 5
LN_EPS = BN_EPS = 1e-5
ds = bass.ds


class Core:

    def __init__(self, nc, ctx, args):
        self.nc, self.ctx, self.args = nc, ctx, args

    def keep(self, name, shape, dt=F32):
        return self.ctx.enter_context(self.nc.sbuf_tensor(name, shape, dt))

    def load_params(self):
        args, self.param, self.param_loads = self.args, {}, []

        def param(name, shape, *loads):
            self.param[name] = self.keep(name, shape)
            self.param_loads += [(dst(self.param[name]), src) for dst, src in loads]

        whole = lambda t: t[:, :]
        wfc = args["g1_wfc"]
        for ffn in ("f0", "f1"):
            param(ffn + "_router", [128, 2, EXPERTS], (lambda t: t[:, :, :], halves(args[ffn + "_wr"])))
            param(ffn + "_bias", [128, EXPERTS], (whole, row_to_all(args[ffn + "_br"], 128)))
        for n, src in (("gain", "f0_g"), ("shift", "f0_b"), ("bias1", "f0_b1")):
            param("f0_" + n, list(args[src].shape), (whole, args[src]))
        param("f0_bias2", [128, EXPERTS, D],
              (lambda t: flat(t[:, :, :]), row_to_all(args["f0_b2"].rearrange("e d -> (e d)"), 128)))
        param("w1", [128, 2, C1], (lambda t: t[:, :, :], halves(args["g1_w1"])))
        param("w2", [128, 1, C2], (lambda t: t[:, 0, :], args["g1_w2"]))
        param("wfc", [128, (D + C1) // 128, D], (lambda t: t[:, :, :], halves(wfc[0:D + C1, :])))
        param("wfc_end", [C2, 1, D], (lambda t: t[:, 0, :], wfc[D + C1:, :]))
        for n in ("b1", "g1", "be1", "b2", "g2", "be2", "bfc"):
            param(n, [P, args["g1_" + n].shape[0]], (whole, row_to_all(args["g1_" + n], P)))
        for n in ("gamma", "beta"):
            param(n, [128, D], (whole, row_to_all(args["f1_" + n], 128)))

    def semaphore(self, name):
        return self.nc.alloc_semaphore(name)


class Stage:

    def __init__(self):
        self.programs = {}

    def _put(self, engine):
        def put(program):
            self.programs[engine] = program
            return program
        return put

    @property
    def sync(self):
        return self._put("sync")

    @property
    def scalar(self):
        return self._put("scalar")

    @property
    def vector(self):
        return self._put("vector")

    @property
    def gpsimd(self):
        return self._put("gpsimd")

    @property
    def tensor(self):
        return self._put("tensor")


def run(c, *stages):
    with c.nc.Block() as block:
        @block.sync
        def _(sp):
            for stage in stages:
                if "sync" in stage.programs:
                    stage.programs["sync"](sp)

        @block.gpsimd
        def _(pool):
            for stage in stages:
                if "gpsimd" in stage.programs:
                    stage.programs["gpsimd"](pool)

        @block.vector
        def _(dve):
            for stage in stages:
                if "vector" in stage.programs:
                    stage.programs["vector"](dve)

        @block.scalar
        def _(act):
            for stage in stages:
                if "scalar" in stage.programs:
                    stage.programs["scalar"](act)

        @block.tensor
        def _(pe):
            for stage in stages:
                if "tensor" in stage.programs:
                    stage.programs["tensor"](pe)


def linker(engine, sem, base=0):
    count = [0]

    def link(instruction):
        count[0] += 1
        instruction.then_inc(sem, 1)
        wait_slot(engine, sem, base + count[0])

    return link


def repeat(engine, n, body, last=False):
    if last:
        body(0, True, False)
        with engine.Fori(1, n - 1) as i:
            body(i, False, False)
        body(n - 1, False, True)
    else:
        body(0, True)
        with engine.Fori(1, n) as i:
            body(i, False)


def wait_slot(engine, sem, value):
    engine.wait_ge(sem, value)
    if not isinstance(value, int):
        engine.nop(nofuse=True)


def row_to_all(ap, parts):
    return ap.rearrange("(a f) -> a f", a=1).broadcast_to([parts, ap.shape[0]])


def stage_constants(c, s):
    nc = c.nc
    stage = Stage()
    iota_i = s.enter_context(nc.sbuf_tensor("iota_i", [128, 512], I32))
    x_in, filled, selected, iota_made, iota_cast = (
        c.semaphore(n) for n in ("x_in", "filled", "selected", "iota_made", "iota_cast"))

    @stage.sync
    def _(sp):
        sp.dma_start(c.x[:, :, :], c.args["x"].rearrange("(t p) f -> p t f", p=P)).then_inc(x_in, 16)
        sp.wait_ge(x_in, 16)

    @stage.gpsimd
    def _(pool):
        nc.gpsimd.iota(iota_i[:, :], pattern=[[1, 512]], base=0, channel_multiplier=0).then_inc(iota_made, 1)
        nc.gpsimd.memset(c.ident[:, :], 0.0).then_inc(filled, 1)
        nc.gpsimd.memset(c.before[:, :], 1.0).then_inc(filled, 1)
        nc.gpsimd.memset(c.ones[:, :], 1.0).then_inc(filled, 1)
        pool.wait_ge(filled, 3)
        nc.gpsimd.affine_select(out=c.ident[:, :], in_=c.ident[:, :], compare_op=ALU.not_equal, fill=1.0, base=0,
                                pattern=[[-1, 128]], channel_multiplier=1).then_inc(selected, 1)
        nc.gpsimd.affine_select(out=c.before[:, :], in_=c.before[:, :], compare_op=ALU.is_gt, fill=0.0, base=0,
                                pattern=[[1, 128]], channel_multiplier=-1).then_inc(selected, 1)

    @stage.vector
    def _(dve):
        dve.wait_ge(iota_made, 1)
        nc.vector.tensor_copy(c.iota[:, :], iota_i[:, :]).then_inc(iota_cast, 1)

    return stage


def stage_norm_stats(c, s, tag, src, mean, rstd):
    nc = c.nc
    stage = Stage()
    sb = lambda n, shape: s.enter_context(nc.sbuf_tensor(f"{tag}_{n}", shape, F32))
    st, dm, var, std = sb("st", [P, T, 6]), sb("dm", [P, T]), sb("var", [P, T]), sb("std", [P, T])
    stats_done, chain, var_ready, std_ready = (
        c.semaphore(f"{tag}_{n}") for n in ("stats_done", "chain", "var_ready", "std_ready"))

    @stage.vector
    def _(dve):
        for t in range(T):
            nc.vector.bn_stats(st[:, t, :], src[:, t, :]).then_inc(stats_done, 1)
        dve.wait_ge(stats_done, T)
        link = linker(dve, chain)
        link(nc.vector.tensor_tensor(dm[:, :], st[:, :, 1], st[:, :, 4], ALU.subtract))
        link(nc.vector.tensor_tensor(mean[:, :], st[:, :, 1], st[:, :, 4], ALU.add))
        link(nc.vector.tensor_scalar(mean[:, :], mean[:, :], 0.5, None, ALU.mult))
        link(nc.vector.tensor_tensor(dm[:, :], dm[:, :], dm[:, :], ALU.mult))
        link(nc.vector.tensor_tensor(var[:, :], st[:, :, 2], st[:, :, 5], ALU.add))
        link(nc.vector.scalar_tensor_tensor(out=var[:, :], in0=dm[:, :], scalar=D / 4.0, in1=var[:, :],
                                            op0=ALU.mult, op1=ALU.add))
        nc.vector.tensor_scalar(var[:, :], var[:, :], 1.0 / D, LN_EPS, ALU.mult, ALU.add).then_inc(var_ready, 1)
        dve.wait_ge(std_ready, 1)
        link(nc.vector.reciprocal(rstd[:, :], std[:, :]))

    @stage.scalar
    def _(act):
        act.wait_ge(var_ready, 1)
        nc.scalar.activation(std[:, :], var[:, :], ACT.Sqrt).then_inc(std_ready, 1)

    return stage


def stage_project(c, s, tag, src, width, rhs, m, outs, norm=None, keep_t=None, dram=None,
                  source_ready=None, relu=False, preparer="vector", out_engine="vector"):
    nc = c.nc
    stage = Stage()
    n = -(-width // 128)
    w = width // n
    LEAD = 2
    RING = (0, 1, 2, 0, 1)
    BACK = (2, 2, 5, 3, 3)
    rows = s.enter_context(nc.sbuf_tensor(tag + "_rows", [P, U, width], F32))
    rows_t = s.enter_context(nc.sbuf_tensor(tag + "_rows_t", [128, 3, n * P], F32))
    ps_t = [c.banks[b][0:w, 0:n * P] for b in range(3)]
    ps_o = [c.banks[3 + b][0:P, 0:m] for b in range(3)] if m else None
    rows_ready, turned, copied, kept, multiplied, written, taken, stored = (
        c.semaphore(f"{tag}_{x}")
        for x in ("rows_ready", "turned", "copied", "kept", "multiplied", "written", "taken", "stored"))
    last_read = copied if keep_t is None else kept

    def wait_free(engine, sem, i, k, first):
        if not (first and k < 3):
            wait_slot(engine, sem, i * U + k - BACK[k] + 1)

    def prepare(engine, maths, t, k, first):
        if not first:
            wait_slot(engine, turned, t - U + 1)
        here, at = flat(src[:, ds(t, 1), 0:width]), ds(t, 1)
        if relu:
            maths.tensor_scalar(rows[:, k, :], here, 0.0, None, ALU.max).then_inc(rows_ready, 1)
        elif norm is None:
            maths.tensor_copy(rows[:, k, :], here).then_inc(rows_ready, 1)
        else:
            maths.tensor_scalar(rows[:, k, :], here, norm[0][:, at], norm[1][:, at],
                                ALU.subtract, ALU.mult).then_inc(rows_ready, 1)

    def take_out(engine, i, k):
        wait_slot(engine, multiplied, i * U + k + 1)
        steps = outs(i * U + k, ps_o[RING[k]])
        for step in steps[:-1]:
            step().then_inc(written, 1)
        steps[-1]().then_inc(taken, 1)

    if preparer == "gpsimd":
        @stage.gpsimd
        def _(pool):
            for t in range(T):
                pool.wait_ge(*source_ready(t))
                prepare(pool, nc.gpsimd, t, t % U, t < U)

    @stage.vector
    def _(dve):
        def body(i, first, last):
            for k in range(U):
                if preparer == "vector" and not (last and k + LEAD >= U):
                    prepare(dve, nc.vector, i * U + k + LEAD, (k + LEAD) % U, first and k + LEAD < U)
                if m and out_engine == "vector":
                    take_out(dve, i, k)

        if preparer == "vector":
            for k in range(LEAD):
                prepare(dve, nc.vector, k, k, True)
        if preparer == "vector" or out_engine == "vector":
            repeat(dve, T // U, body, last=True)
        if m:
            dve.wait_ge(taken, T)

    @stage.scalar
    def _(act):
        def body(i, first):
            for k in range(U):
                if m:
                    wait_free(act, multiplied, i, k, first)
                wait_slot(act, turned, i * U + k + 1)
                if m:
                    nc.scalar.copy(rows_t[0:w, RING[k], :], ps_t[RING[k]]).then_inc(copied, 1)
                if keep_t is not None:
                    nc.scalar.copy(keep_t[0:w, :, ds((i * U + k) * P, P)],
                                   ps_t[RING[k]].rearrange("p (j r) -> p j r", j=n)).then_inc(kept, 1)
                if m and out_engine == "scalar" and not (first and k == 0):
                    take_out(act, i if k else i - 1, (k - 1) % U)

        repeat(act, T // U, body)
        if m and out_engine == "scalar":
            take_out(act, T // U - 1, U - 1)

    @stage.tensor
    def _(pe):
        def turn(i, k, t, first):
            wait_free(pe, last_read, i, k, first)
            wait_slot(pe, rows_ready, t + 1)
            for j in range(n):
                last = nc.tensor.transpose(ps_t[RING[k]][:, j * P:(j + 1) * P],
                                           rows[:, k, j * w:(j + 1) * w], c.ident[0:P, 0:P])
            last.then_inc(turned, 1)

        def body(i, first, last):
            for k in range(U):
                if k + 1 < U:
                    turn(i, k + 1, i * U + k + 1, first)
                elif not last:
                    turn(i + 1, 0, (i + 1) * U, False)
                if m:
                    wait_free(pe, taken, i, k, first)
                    wait_slot(pe, copied, i * U + k + 1)
                    for j in range(n):
                        mm = nc.tensor.matmul(ps_o[RING[k]], rows_t[0:w, RING[k], j * P:(j + 1) * P], rhs[0:w, j, :],
                                              start=(j == 0), stop=(j == n - 1))
                    mm.then_inc(multiplied, 1)

        turn(0, 0, 0, True)
        repeat(pe, T // U, body, last=True)

    stage.kept = (kept, T)
    if dram is not None:
        @stage.sync
        def _(sp):
            sp.wait_ge(taken, T)
            sp.dma_start(dram[0].rearrange("(t p) f -> p t f", p=P), dram[1]).then_inc(stored, 16)
            sp.wait_ge(stored, 16)

    return stage


def stage_load_edges(c, s, tag):
    nc = c.nc
    stage = Stage()
    c.src_i, c.dst_i = (s.enter_context(nc.sbuf_tensor(f"{tag}_{n}", [P, EC], I32)) for n in ("src_i", "dst_i"))
    c.edge_w = s.enter_context(nc.sbuf_tensor(tag + "_edge_w", [P, EC], F32))
    loaded = c.semaphore(tag + "_loaded")

    @stage.sync
    def _(sp):
        for dst, src in ((c.src_i, "src"), (c.dst_i, "dst"), (c.edge_w, "edge_weight")):
            sp.dma_start(dst[:, :], c.args[src].rearrange("(p c) -> p c", p=P)).then_inc(loaded, 16)
        sp.wait_ge(loaded, 48)

    return stage


def stage_edge_records(c, s, tag, add_to, other, rec, bucket):
    nc = c.nc
    stage = Stage()
    to_f = s.enter_context(nc.sbuf_tensor(tag + "_to_f", [P, EC], F32))
    chain = c.semaphore(tag + "_chain")

    @stage.vector
    def _(dve):
        link = linker(dve, chain)
        link(nc.vector.memset(rec[:, :, 3], 0.0))
        link(nc.vector.tensor_copy(to_f[:, :], add_to[:, :]))
        link(nc.vector.tensor_scalar(bucket[:, :], to_f[:, :], 1.0 / P, -(P - 1) / (2.0 * P), ALU.mult, ALU.add))
        link(nc.vector.tensor_scalar(bucket[:, :], bucket[:, :], ROUND, ROUND, ALU.add, ALU.subtract))
        link(nc.vector.scalar_tensor_tensor(out=rec[:, :, 0], in0=bucket[:, :], scalar=-float(P), in1=to_f[:, :],
                                            op0=ALU.mult, op1=ALU.add))
        link(nc.vector.tensor_scalar(rec[:, :, 0], rec[:, :, 0], 1.0, None, ALU.add))
        link(nc.vector.tensor_copy(rec[:, :, 1], other[:, :]))
        link(nc.vector.tensor_copy(rec[:, :, 2], c.edge_w[:, :]))

    return stage


def stage_rank_buckets(c, s, tag, bucket, cols, n_buckets, group, q, ends):
    nc = c.nc
    stage = Stage()
    W = 5 if n_buckets % 5 == 0 else 4
    assert n_buckets % W == 0
    sb = lambda n, shape: s.enter_context(nc.sbuf_tensor(f"{tag}_{n}", shape, F32))
    is_b, run_b, q_odd = sb("is_b", [P, W, cols]), sb("run_b", [P, W, cols]), sb("q_odd", [P, cols])
    count, groups, off = sb("count", [P, n_buckets]), sb("groups", [P, n_buckets]), sb("off", [P, n_buckets])
    stage.bank = c.banks[7]
    ps = stage.bank[0:P, 0:2 * n_buckets].rearrange("p (a b) -> p a b", a=2)
    counted, chain, summed, masked, scanned, ranked = (
        c.semaphore(f"{tag}_{n}") for n in ("counted", "chain", "summed", "masked", "scanned", "ranked"))

    @stage.vector
    def _(dve):
        def count_body(i, first):
            for k in range(W):
                b = i * W + k
                if not first:
                    wait_slot(dve, counted, b - W + 1)
                nc.vector.tensor_scalar(is_b[:, k, :], bucket[:, :], c.iota[0:P, ds(b, 1)], 0.0, ALU.is_equal, ALU.add,
                                        accum_out=count[:, ds(b, 1)]).then_inc(counted, 1)

        repeat(dve, n_buckets // W, count_body)
        dve.wait_ge(summed, 1)
        link = linker(dve, chain)
        link(nc.vector.tensor_scalar(groups[:, :], ps[:, 1, :], 1.0 / group, (group - 1) / (2.0 * group),
                                     ALU.mult, ALU.add))
        link(nc.vector.tensor_scalar(groups[:, :], groups[:, :], ROUND, ROUND, ALU.add, ALU.subtract))
        link(nc.vector.tensor_tensor_scan(ends[:, :], c.ones[0:P, 0:n_buckets], groups[:, :], 0.0, ALU.mult, ALU.add))
        link(nc.vector.tensor_tensor(off[:, :], ends[:, :], groups[:, :], ALU.subtract))
        link(nc.vector.scalar_tensor_tensor(out=off[:, :], in0=off[:, :], scalar=float(group), in1=ps[:, 0, :],
                                            op0=ALU.mult, op1=ALU.add))
        nc.vector.memset(q_odd[:, :], 0.0)
        link(nc.vector.memset(q[:, :], 0.0))

        def rank_body(i, first):
            for k in range(W):
                if not first:
                    wait_slot(dve, ranked, i * W + k - W + 1)
                nc.vector.tensor_scalar(is_b[:, k, :], bucket[:, :], c.iota[0:P, ds(i * W + k, 1)], None,
                                        ALU.is_equal).then_inc(masked, 1)
            for k in range(W):
                wait_slot(dve, masked, i * W + k + 1)
                nc.vector.tensor_tensor_scan(run_b[:, k, :], c.ones[0:P, 0:1].broadcast_to([P, cols]), is_b[:, k, :],
                                             off[:, ds(i * W + k, 1)], ALU.mult, ALU.add).then_inc(scanned, 1)
            for k in range(W):
                wait_slot(dve, scanned, i * W + k + 1)
                if k != 1 and not (first and k == 0):
                    wait_slot(dve, ranked, i * W + max(k - 1, 0))
                nc.vector.copy_predicated((q, q_odd)[k % 2][:, :], is_b[:, k, :].bitcast(I32),
                                          run_b[:, k, :]).then_inc(ranked, 1)

        repeat(dve, n_buckets // W, rank_body)
        dve.wait_ge(ranked, n_buckets)
        link(nc.vector.scalar_tensor_tensor(out=q[:, :], in0=q[:, :], scalar=-1.0,
                                            in1=q_odd[:, :], op0=ALU.add, op1=ALU.add))

    stage.ends_ready = (chain, 5)

    @stage.tensor
    def _(pe):
        pe.wait_ge(counted, n_buckets)
        nc.tensor.matmul(ps[:, 0, :], c.before[0:P, 0:P], count[:, :], start=True, stop=True)
        nc.tensor.matmul(ps[:, 1, :], c.ones[0:P, 0:P], count[:, :], start=True, stop=True).then_inc(summed, 1)

    return stage


def stage_bucket_table(c, s, tag, rank, ends, n_buckets, n_groups, table):
    nc = c.nc
    stage = Stage()
    others = n_buckets - 1
    end_col = s.enter_context(nc.sbuf_tensor(tag + "_end_col", [others, 1], F32))
    ended = s.enter_context(nc.sbuf_tensor(tag + "_ended", [others, n_groups], F32))
    ps = rank.bank
    chain, turned, summed = (c.semaphore(f"{tag}_{n}") for n in ("chain", "turned", "summed"))

    @stage.vector
    def _(dve):
        link = linker(dve, chain)
        dve.wait_ge(turned, 1)
        link(nc.vector.tensor_copy(end_col[:, :], ps[0:others, 0:1]))
        link(nc.vector.tensor_scalar(ended[:, :], c.iota[0:others, 0:n_groups], end_col[:, 0:1], None, ALU.is_ge))
        dve.wait_ge(summed, 1)
        link(nc.vector.tensor_copy(table[:, :], ps[0:1, 0:n_groups]))

    @stage.tensor
    def _(pe):
        pe.wait_ge(*rank.ends_ready)
        nc.tensor.matmul(ps[0:others, 0:1], ends[0:1, 0:others], c.ones[0:1, 0:1], start=True, stop=True).then_inc(turned, 1)
        pe.wait_ge(chain, 2)
        nc.tensor.matmul(ps[0:1, 0:n_groups], c.ones[0:others, 0:1], ended[:, :], start=True, stop=True).then_inc(summed, 1)

    return stage


def stage_places(c, s, tag, q, place_i, slots=SLOTS, rec=None, fields=None):
    nc = c.nc
    stage = Stage()
    slot, place = (s.enter_context(nc.sbuf_tensor(f"{tag}_{n}", [P, EC], F32)) for n in ("slot", "place"))
    chain = c.semaphore(tag + "_chain")

    @stage.vector
    def _(dve):
        link = linker(dve, chain)
        link(nc.vector.tensor_scalar(slot[:, :], q[:, :], 1.0 / S, -(S - 1) / (2.0 * S), ALU.mult, ALU.add))
        link(nc.vector.tensor_scalar(slot[:, :], slot[:, :], ROUND, ROUND, ALU.add, ALU.subtract))
        link(nc.vector.scalar_tensor_tensor(out=place[:, :], in0=slot[:, :], scalar=-float(S), in1=q[:, :],
                                            op0=ALU.mult, op1=ALU.add))
        if fields is not None:
            n = BY_PRODUCTS
            other, weight = rec[:, 0:n, 1], rec[:, 0:n, 2]
            upper, lower, w_a, w_b, w_c = (fields[:, :, 3 + k] for k in range(5))
            top_half = lambda out, v: link(nc.vector.tensor_scalar(out.bitcast(I32), v.bitcast(I32), -65536, None,
                                                                   ALU.bitwise_and))
            link(nc.vector.tensor_copy(fields[:, :, 0], place[:, 0:n]))
            link(nc.vector.tensor_copy(fields[:, :, 1], slot[:, 0:n]))
            link(nc.vector.tensor_copy(fields[:, :, 2], rec[:, 0:n, 0]))
            link(nc.vector.tensor_scalar(upper, other, 1.0 / 64, -63.0 / 128, ALU.mult, ALU.add))
            link(nc.vector.tensor_scalar(upper, upper, ROUND, ROUND, ALU.add, ALU.subtract))
            link(nc.vector.tensor_scalar(upper, upper, 64.0, None, ALU.mult))
            link(nc.vector.tensor_tensor(lower, other, upper, ALU.subtract))
            top_half(w_a, weight)
            link(nc.vector.tensor_tensor(w_c, weight, w_a, ALU.subtract))
            top_half(w_b, w_c)
            link(nc.vector.tensor_tensor(w_c, w_c, w_b, ALU.subtract))
        link(nc.vector.scalar_tensor_tensor(out=place[:, :], in0=place[:, :], scalar=float(slots), in1=slot[:, :],
                                            op0=ALU.mult, op1=ALU.add))
        link(nc.vector.tensor_copy(place_i[:, :], place[:, :]))

    return stage


def stage_fill(c, s, tag, rows_list, slots):
    nc = c.nc
    stage = Stage()
    none = s.enter_context(nc.sbuf_tensor(tag + "_none", [S, SLOTS, 4], F32))
    zero = s.enter_context(nc.sbuf_tensor(tag + "_zero", [128, B * D // 128], F32))
    made, filled = c.semaphore(tag + "_made"), c.semaphore(tag + "_filled")
    slots_v = slots.rearrange("(a p r) f -> a p (r f)", a=BLOCKS + 1, p=128)

    @stage.vector
    def _(dve):
        nc.vector.memset(none[:, :, :], 0.0).then_inc(made, 1)
        nc.vector.memset(zero[:, :], 0.0).then_inc(made, 1)

    @stage.sync
    def _(sp):
        sp.wait_ge(made, 2)
        for rows in rows_list:
            sp.dma_start(rows.rearrange("(r j) f -> r j f", r=S), none[:, 0:rows.shape[0] // S, :]).then_inc(filled, 16)
        for a in range(BLOCKS + 1):
            sp.dma_start(slots_v[a], zero[:, :]).then_inc(filled, 16)
        sp.wait_ge(filled, 16 * (len(rows_list) + BLOCKS + 1))

    return stage


def stage_place_by_products(c, s, tag, fields, lists):
    nc = c.nc
    stage = Stage()
    W, R = 8, 4
    K = PARTS
    MIXED = K // 2
    sb = lambda n, shape, dt=F32: s.enter_context(nc.sbuf_tensor(f"{tag}_{n}", shape, dt))
    now = sb("now", [P, 2, W, 2 + K])
    one_hot = sb("one_hot", [P, R, S], BF16)
    of_slot, of_row = sb("of_slot", [P, R, SLOTS], BF16), sb("of_row", [P, R, K, S], BF16)
    none, numbers = sb("none", [P, SLOTS], BF16), sb("numbers", [P, SLOTS], F16)
    ps = [c.banks[k][:, 0:SLOTS] for k in range(K)]
    staged, zeroed, hot_ready, made, scaled, used, whole, taken = (
        c.semaphore(f"{tag}_{n}") for n in ("staged", "zeroed", "hot_ready", "made", "scaled", "used", "whole", "taken"))

    @stage.scalar
    def _(act):
        def stage_half(i, h):
            nc.scalar.copy(now[:, h, :, :], fields[:, ds(i * (2 * W) + h * W, W), :]).then_inc(staged, 1)

        def body(i, first, last):
            for h in range(2):
                for k in range(W):
                    n, b = h * W + k, k % R
                    if k == W // 2 and not (last and h == 1):
                        if not (first and h == 0):
                            wait_slot(act, used, (i * 2 + h) * W)
                        if h == 0:
                            stage_half(i, 1)
                        else:
                            stage_half(i + 1, 0)
                    wait_slot(act, hot_ready, i * (2 * W) + n + 1)
                    for f in range(MIXED, K):
                        mul = nc.scalar.activation(of_row[:, b, f, :], one_hot[:, b, :], ACT.Copy,
                                                   scale=now[:, h, k, 2 + f:3 + f])
                    mul.then_inc(scaled, 1)

        stage_half(0, 0)
        repeat(act, BY_PRODUCTS // (2 * W), body, last=True)
        act.wait_ge(whole, 1)
        for k in range(K):
            nc.scalar.copy(lists[:, k, :], ps[k]).then_inc(taken, 1)
        act.wait_ge(taken, K)

    @stage.vector
    def _(dve):
        nc.vector.memset(none[:, :], 0.0).then_inc(zeroed, 1)
        nc.vector.tensor_copy(numbers[:, :], c.iota[0:P, 0:SLOTS]).then_inc(zeroed, 1)
        dve.wait_ge(zeroed, 2)

        def body(i, first):
            for h in range(2):
                wait_slot(dve, staged, i * 2 + h + 1)
                for k in range(W):
                    n, b = h * W + k, k % R
                    if not (first and n < R):
                        wait_slot(dve, used, i * (2 * W) + (n + 1 - R))
                    nc.vector.tensor_scalar(one_hot[:, b, :], numbers[:, 0:S], now[:, h, k, 0:1], None,
                                            ALU.is_equal).then_inc(hot_ready, 1)
                    nc.vector.tensor_scalar(of_slot[:, b, :], numbers[:, :], now[:, h, k, 1:2], None, ALU.is_equal)
                    for f in range(MIXED):
                        last = nc.vector.tensor_scalar(of_row[:, b, f, :], numbers[:, 0:S], now[:, h, k, 0:1],
                                                       now[:, h, k, 2 + f:3 + f], ALU.is_equal, ALU.mult)
                    last.then_inc(made, 1)

        repeat(dve, BY_PRODUCTS // (2 * W), body)

    @stage.tensor
    def _(pe):
        pe.wait_ge(zeroed, 2)
        for k in range(K):
            nc.tensor.matmul(ps[k], none[:, 0:S], none[:, :], start=True, stop=False)

        def body(i, first):
            for k in range(2 * W):
                b = k % R
                wait_slot(pe, made, i * (2 * W) + k + 1)
                wait_slot(pe, scaled, i * (2 * W) + k + 1)
                for f in range(K):
                    mm = nc.tensor.matmul(ps[f], of_row[:, b, f, :], of_slot[:, b, :], start=False, stop=False)
                mm.then_inc(used, 1)

        repeat(pe, BY_PRODUCTS // (2 * W), body)
        for k in range(K):
            mm = nc.tensor.matmul(ps[k], none[:, 0:S], none[:, :], start=False, stop=True)
        mm.then_inc(whole, 1)

    return stage


def stage_merge(c, s, tag, lists, table_sb):
    nc = c.nc
    stage = Stage()
    chain = c.semaphore(tag + "_chain")
    stage.merged = (chain, 2)

    @stage.vector
    def _(dve):
        link = linker(dve, chain)
        link(nc.vector.tensor_tensor(lists[:, 1, :], lists[:, 1, :], lists[:, 2, :], ALU.add))
        link(nc.vector.tensor_tensor(table_sb[:, :, 1], table_sb[:, :, 1], lists[:, 1, :], ALU.add))
        link(nc.vector.tensor_tensor(table_sb[:, :, 0], table_sb[:, :, 0], lists[:, 0, :], ALU.add))
        link(nc.vector.tensor_tensor(lists[:, 4, :], lists[:, 4, :], lists[:, 5, :], ALU.add))
        link(nc.vector.tensor_tensor(lists[:, 3, :], lists[:, 3, :], lists[:, 4, :], ALU.add))
        link(nc.vector.tensor_tensor(table_sb[:, :, 2], table_sb[:, :, 2], lists[:, 3, :], ALU.add))

    return stage


def stage_scatter_records(c, s, tag, rec, place_i, rows, table_sb, start=0):
    nc = c.nc
    stage = Stage()
    W = 8
    idx = s.enter_context(nc.sbuf_tensor(tag + "_idx", [P, 2, W], I32))
    put = s.enter_context(nc.sbuf_tensor(tag + "_put", [P, 2, W, 4], F32))
    staged, read = c.semaphore(tag + "_staged"), c.semaphore(tag + "_read")
    scattered = [c.semaphore(f"{tag}_scattered{h}") for h in range(2)]

    @stage.gpsimd
    def _(pool):
        def body(i, first):
            for h in range(2):
                if not first:
                    wait_slot(pool, scattered[h], i * (16 * W))
                at = i * (2 * W) + (h * W + start)
                nc.gpsimd.tensor_copy(idx[:, h, :], place_i[:, ds(at, W)]).then_inc(staged, 1)
                nc.gpsimd.tensor_copy(put[:, h, :, :], rec[:, ds(at, W), :]).then_inc(staged, 1)
                wait_slot(pool, staged, i * 4 + 2 * h + 2)
                for k in range(W):
                    nc.gpsimd.indirect_dma_start(
                        out=rows, out_offset=bass.IndirectOffsetOnAxis(ap=idx[:, h, k:k + 1], axis=0),
                        in_=put[:, h, k, :], in_offset=None).then_inc(scattered[h], 16)

        repeat(pool, (EC - start) // (2 * W), body)

    @stage.sync
    def _(sp):
        for h in range(2):
            sp.wait_ge(scattered[h], 16 * (EC - start) // 2)
        sp.dma_start(table_sb[:, :, :], rows.rearrange("(r j) f -> r j f", r=S)).then_inc(read, 16)
        sp.wait_ge(read, 16)

    return stage


class Aside:

    def __init__(self, steps):
        self.steps = steps

    def vector_begin(self, dve):
        pass

    def vector_piece(self, dve, i, first):
        pass

    def vector_end(self, dve):
        pass

    def scalar_piece(self, act, i, first):
        pass

    def scalar_end(self, act):
        pass

    def tensor_begin(self, pe):
        pass

    def tensor_piece(self, pe, i, first):
        pass

    def tensor_end(self, pe):
        pass


class CountDegrees(Aside):

    COLS = 16

    def __init__(self, c, s, tag, steps, rec, tile_of, deg):
        super().__init__(steps)
        nc = self.nc = c.nc
        self.c, self.rec, self.tile_of, self.deg = c, rec, tile_of, deg
        self.early = EC // self.COLS - steps
        assert self.early * self.COLS + steps * self.COLS == EC and self.early >= 2
        sb = lambda n, shape: s.enter_context(nc.sbuf_tensor(f"{tag}_{n}", shape, BF16))
        self.of_row, self.of_tile = sb("of_row", [P, self.COLS, P]), sb("of_tile", [P, self.COLS, T])
        self.none = sb("none", [P, P])
        self.ps = c.banks[7][0:P, 0:T]
        self.zeroed, self.made, self.used, self.whole, self.counted = (
            c.semaphore(f"{tag}_{n}") for n in ("zeroed", "made", "used", "whole", "counted"))

    def make(self, dve, piece, first=False):
        at = ds(piece * self.COLS, self.COLS)
        if not first:
            wait_slot(dve, self.used, piece)
        wide = lambda v, m: v.unsqueeze(2).broadcast_to([P, self.COLS, m])
        numbers = lambda a, m: self.c.iota[0:P, a:a + m].unsqueeze(1).broadcast_to([P, self.COLS, m])
        self.nc.vector.tensor_tensor(self.of_row[:, :, :], wide(self.rec[:, at, 0], P), numbers(1, P), ALU.is_equal)
        self.nc.vector.tensor_tensor(self.of_tile[:, :, :], wide(self.tile_of[:, at], T), numbers(0, T),
                                     ALU.is_equal).then_inc(self.made, 1)

    def sum(self, pe, piece):
        wait_slot(pe, self.made, piece + 1)
        for k in range(self.COLS):
            mm = self.nc.tensor.matmul(self.ps, self.of_row[:, k, :], self.of_tile[:, k, :], start=False, stop=False)
        mm.then_inc(self.used, 1)

    def vector_begin(self, dve):
        self.nc.vector.memset(self.none[:, :], 0.0).then_inc(self.zeroed, 1)
        for piece in range(self.early):
            self.make(dve, piece, piece == 0)

    def vector_piece(self, dve, i, first):
        self.make(dve, i + self.early)

    def vector_end(self, dve):
        dve.wait_ge(self.whole, 1)
        self.nc.vector.tensor_copy(self.deg[:, :], self.ps).then_inc(self.counted, 1)
        dve.wait_ge(self.counted, 1)

    def tensor_begin(self, pe):
        pe.wait_ge(self.zeroed, 1)
        self.nc.tensor.matmul(self.ps, self.none[:, 0:P], self.none[:, 0:T], start=True, stop=False)
        for piece in range(self.early):
            self.sum(pe, piece)

    def tensor_piece(self, pe, i, first):
        self.sum(pe, i + self.early)

    def tensor_end(self, pe):
        self.nc.tensor.matmul(self.ps, self.none[:, 0:P], self.none[:, 0:T], start=False, stop=True).then_inc(self.whole, 1)


class MultiplyTiles(Aside):

    def __init__(self, c, s, tag, steps, turned, w, bias, out):
        super().__init__(steps)
        self.more = T - steps
        nc = self.nc = c.nc
        self.c, self.turned, self.w, self.bias, self.out = c, turned, w, bias, out
        self.rows_t = s.enter_context(nc.sbuf_tensor(tag + "_rows_t", list(turned.shape[:2]) + [P], F32))
        self.ps = c.banks[5][0:P, 0:D]
        self.copied, self.multiplied, self.taken = (c.semaphore(f"{tag}_{n}") for n in ("copied", "multiplied", "taken"))

    def copy_and_take(self, act, tile, first):
        if not first:
            wait_slot(act, self.multiplied, tile)
            self.nc.scalar.copy(flat(self.out[:, ds(tile - 1, 1), :]), self.ps).then_inc(self.taken, 1)
        self.nc.scalar.copy(self.rows_t[:, :, :], self.turned[:, :, ds(tile * P, P)]).then_inc(self.copied, 1)

    def multiply(self, pe, tile, first):
        chunks = self.rows_t.shape[1]
        if not first:
            wait_slot(pe, self.taken, tile)
        wait_slot(pe, self.copied, tile + 1)
        for j in range(chunks):
            self.nc.tensor.matmul(self.ps, self.rows_t[:, j, :], self.w[:, j, :], start=(j == 0), stop=False)
        self.nc.tensor.matmul(self.ps, self.c.ones[0:1, 0:P], self.bias[0:1, :], start=False,
                              stop=True).then_inc(self.multiplied, 1)

    def scalar_piece(self, act, i, first):
        if first:
            for tile in range(self.more):
                self.copy_and_take(act, tile, tile == 0)
        self.copy_and_take(act, i + self.more, False)

    def scalar_end(self, act):
        act.wait_ge(self.multiplied, T)
        self.nc.scalar.copy(self.out[:, T - 1, :], self.ps).then_inc(self.taken, 1)
        act.wait_ge(self.taken, T)

    def tensor_begin(self, pe):
        for tile in range(self.more):
            self.multiply(pe, tile, tile == 0)

    def tensor_piece(self, pe, i, first):
        self.multiply(pe, i + self.more, False)


def stage_aggregate(c, s, tag, table_sb, tiles_of, values, width, acc, table_ready, aside=Aside(0)):
    nc = c.nc
    stage = Stage()
    G = AGGREGATE
    H = G // 2
    NB = H // 2
    sb = lambda n, shape, dt=F32: s.enter_context(nc.sbuf_tensor(f"{tag}_{n}", shape, dt))
    idx, got, hot = sb("idx", [S, 2, H], I32), sb("got", [S, G, width]), sb("hot", [S, G, P])
    ps = [c.banks[b][0:P, 0:width] for b in range(NB)]
    staged, matched, hot_ready, summed, added = (
        c.semaphore(f"{tag}_{n}") for n in ("staged", "matched", "hot_ready", "summed", "added"))
    gathered = [c.semaphore(f"{tag}_gathered{k}") for k in range(G)]

    @stage.scalar
    def _(act):
        act.wait_ge(*table_ready)

        def body(i, first):
            for h in range(2):
                if not first:
                    wait_slot(act, summed, (i * 2 + h - 1) * NB)
                nc.scalar.copy(idx[:, h, :], table_sb[:, ds(i * G + h * H, H), 1]).then_inc(staged, 1)
            aside.scalar_piece(act, i, first)

        repeat(act, AGGREGATE_STEPS, body)
        aside.scalar_end(act)

    @stage.gpsimd
    def _(pool):
        def body(i, first):
            for h in range(2):
                wait_slot(pool, staged, i * 2 + h + 1)
                for k in range(H):
                    nc.gpsimd.indirect_dma_start(
                        out=got[:, h * H + k, :], out_offset=None, in_=values,
                        in_offset=bass.IndirectOffsetOnAxis(ap=idx[:, h, k:k + 1], axis=0),
                    ).then_inc(gathered[h * H + k], 16)

        repeat(pool, AGGREGATE_STEPS, body)

    @stage.vector
    def _(dve):
        def make_hot(i, h, first):
            if not first:
                wait_slot(dve, summed, (i * 2 + h - 1) * NB)
            here, at = hot[:, h * H:(h + 1) * H, :], ds(i * G + h * H, H)
            wide = lambda field: table_sb[:, at, field].unsqueeze(2).broadcast_to([S, H, P])
            match = nc.vector.tensor_tensor(here, c.iota[0:S, 1:P + 1].unsqueeze(1).broadcast_to([S, H, P]), wide(0),
                                            ALU.is_equal)
            match.then_inc(matched, 1)
            wait_slot(dve, matched, i * 2 + h + 1)
            nc.vector.tensor_tensor(here, here, wide(2), ALU.mult).then_inc(hot_ready, 1)

        def add(pair, b, first=False):
            tile = dve.value_load(tiles_of[0:1, ds(pair, 1)], min_val=0, max_val=T - 1)
            if not first:
                wait_slot(dve, added, pair)
            wait_slot(dve, summed, pair + 1)
            here = flat(acc[:, ds(tile, 1), :])
            nc.vector.tensor_tensor(here, here, ps[b], ALU.add).then_inc(added, 1)

        def body(i, first):
            for h in range(2):
                make_hot(i, h, first)
                if not (first and h == 0):
                    for b in range(NB):
                        add((i * 2 + h - 1) * NB + b, b, first and b == 0)
            aside.vector_piece(dve, i, first)

        aside.vector_begin(dve)
        repeat(dve, AGGREGATE_STEPS, body)
        for b in range(NB):
            add(PAIRS - NB + b, b)
        dve.wait_ge(added, PAIRS)
        aside.vector_end(dve)

    @stage.tensor
    def _(pe):
        def body(i, first):
            for h in range(2):
                wait_slot(pe, hot_ready, i * 2 + h + 1)
                for b in range(NB):
                    if not (first and h == 0):
                        wait_slot(pe, added, (i * 2 + h - 1) * NB + b + 1)
                    for e in range(2):
                        k = h * H + b * 2 + e
                        pe.wait_ge(gathered[k], i * 16 + 16)
                        mm = nc.tensor.matmul(ps[b], hot[:, k, :], got[:, k, :], start=(e == 0), stop=(e == 1))
                    mm.then_inc(summed, 1)
            aside.tensor_piece(pe, i, first)

        aside.tensor_begin(pe)
        repeat(pe, AGGREGATE_STEPS, body)
        aside.tensor_end(pe)

    return stage


def stage_aggregate_narrow(c, s, tag, table_sb, tiles_of, values, width, acc, aside=Aside(0)):
    nc = c.nc
    stage = Stage()
    G = AGGREGATE
    H = G // 2
    TB = 512 // width
    BANKS = -(-T // TB)
    sb = lambda n, shape, dt=F32: s.enter_context(nc.sbuf_tensor(f"{tag}_{n}", shape, dt))
    idx, got, hot = sb("idx", [S, 2, H], I32), sb("got", [S, G, width]), sb("hot", [S, G, P])
    none = sb("none", [1, 512], BF16)
    zeroed, staged, hot_ready, summed, whole, added = (
        c.semaphore(f"{tag}_{n}") for n in ("zeroed", "staged", "hot_ready", "summed", "whole", "added"))
    gathered = [c.semaphore(f"{tag}_gathered{k}") for k in range(G)]

    @stage.scalar
    def _(act):
        def body(i, first):
            for h in range(2):
                if not first:
                    wait_slot(act, summed, (i * 2 + h - 1) * H)
                nc.scalar.copy(idx[:, h, :], table_sb[:, ds(i * G + h * H, H), 1]).then_inc(staged, 1)
            aside.scalar_piece(act, i, first)

        repeat(act, AGGREGATE1_STEPS, body)
        aside.scalar_end(act)

    @stage.gpsimd
    def _(pool):
        def body(i, first):
            for h in range(2):
                wait_slot(pool, staged, i * 2 + h + 1)
                for k in range(H):
                    nc.gpsimd.indirect_dma_start(
                        out=got[:, h * H + k, :], out_offset=None, in_=values,
                        in_offset=bass.IndirectOffsetOnAxis(ap=idx[:, h, k:k + 1], axis=0),
                    ).then_inc(gathered[h * H + k], 16)

        repeat(pool, AGGREGATE1_STEPS, body)

    @stage.vector
    def _(dve):
        def body(i, first):
            for h in range(2):
                if not first:
                    wait_slot(dve, summed, (i * 2 + h - 1) * H)
                row = table_sb[:, ds(i * G + h * H, H), 0].unsqueeze(2).broadcast_to([S, H, P])
                nc.vector.tensor_tensor(hot[:, h * H:(h + 1) * H, :], c.iota[0:S, 1:P + 1].unsqueeze(1).broadcast_to([S, H, P]),
                                        row, ALU.is_equal).then_inc(hot_ready, 1)

        nc.vector.memset(none[:, :], 0.0).then_inc(zeroed, 1)
        repeat(dve, AGGREGATE1_STEPS, body)
        for b in range(BANKS):
            dve.wait_ge(whole, b + 1)
            here = acc[:, b * TB:min(T, (b + 1) * TB), :]
            nc.vector.tensor_tensor(here, here, c.banks[b][0:P, 0:here.shape[1] * width].rearrange(
                "p (t f) -> p t f", f=width), ALU.add).then_inc(added, 1)
        dve.wait_ge(added, BANKS)

    @stage.tensor
    def _(pe):
        def body(i, first):
            for h in range(2):
                wait_slot(pe, hot_ready, i * 2 + h + 1)
                for k in range(h * H, (h + 1) * H):
                    tile = pe.value_load(tiles_of[0:1, ds(i * G + k, 1)], min_val=0, max_val=T - 1)
                    pe.wait_ge(gathered[k], i * 16 + 16)
                    nc.tensor.matmul(c.psum[0:P, ds(tile * width, width)], hot[:, k, :], got[:, k, :],
                                     start=False, stop=False).then_inc(summed, 1)
            aside.tensor_piece(pe, i, first)

        pe.wait_ge(zeroed, 1)
        for b in range(BANKS):
            nc.tensor.matmul(c.banks[b][0:P, :], none[:, 0:P], none[:, :], start=True, stop=False)
        aside.tensor_begin(pe)
        repeat(pe, AGGREGATE1_STEPS, body)
        for b in range(BANKS):
            nc.tensor.matmul(c.banks[b][0:P, :], none[:, 0:P], none[:, :], start=False, stop=True).then_inc(whole, 1)
        aside.tensor_end(pe)

    return stage


def stage_normalise(c, s, tag, src, mean, rstd, dst):
    nc = c.nc
    stage = Stage()
    done = c.semaphore(tag + "_done")

    @stage.vector
    def _(dve):
        for t in range(T):
            nc.vector.tensor_scalar(dst[:, t, :], src[:, t, :], mean[:, t:t + 1], rstd[:, t:t + 1],
                                    ALU.subtract, ALU.mult).then_inc(done, 1)
        dve.wait_ge(done, T)

    stage.ready = lambda t: (done, t + 1)

    return stage


def stage_load(c, s, tag, pairs):
    stage = Stage()
    loaded = c.semaphore(tag + "_loaded")

    @stage.sync
    def _(sp):
        for dst, src in pairs:
            sp.dma_start(dst, src).then_inc(loaded, 16)
        sp.wait_ge(loaded, 16 * len(pairs))

    return stage


def stage_route(c, s, tag, logits, bias, probs, top_i, weights):
    nc = c.nc
    E = EXPERTS
    stage = Stage()
    sb = lambda n, shape, dt=F32: s.enter_context(nc.sbuf_tensor(f"{tag}_{n}", shape, dt))
    most, total, both = sb("most", [P, T]), sb("total", [P, T]), sb("both", [P, T])
    top_p = sb("top_p", [P, T, 8])
    raw = sb("raw", [P, T, 8], U32)
    chain, shifted, exped, top = (c.semaphore(f"{tag}_{n}") for n in ("chain", "shifted", "exped", "top"))

    @stage.vector
    def _(dve):
        link = linker(dve, chain)
        link(nc.vector.tensor_tensor(logits[:, :, :], logits[:, :, :],
                                     bias[0:P, :].unsqueeze(1).broadcast_to([P, T, E]), ALU.add))
        link(nc.vector.tensor_reduce(most[:, :], logits[:, :, :], AX.X, ALU.max))
        nc.vector.tensor_tensor(logits[:, :, :], logits[:, :, :], most[:, :].unsqueeze(2).broadcast_to([P, T, E]),
                                ALU.subtract).then_inc(shifted, 1)
        dve.wait_ge(exped, 1)
        link(nc.vector.tensor_reduce(total[:, :], probs[:, :, :], AX.X, ALU.add))
        link(nc.vector.reciprocal(total[:, :], total[:, :]))
        link(nc.vector.tensor_tensor(probs[:, :, :], probs[:, :, :],
                                     total[:, :].unsqueeze(2).broadcast_to([P, T, E]), ALU.mult))
        for t in range(T):
            nc.vector.max(top_p[:, t, :], probs[:, t, :]).then_inc(top, 1)
        dve.wait_ge(top, T)
        for t in range(T):
            nc.vector.max_index(raw[:, t, :], top_p[:, t, :], probs[:, t, :]).then_inc(top, 1)
        link(nc.vector.tensor_tensor(both[:, :], top_p[:, :, 0], top_p[:, :, 1], ALU.add))
        link(nc.vector.reciprocal(both[:, :], both[:, :]))
        link(nc.vector.tensor_tensor(weights[:, :, :], top_p[:, :, 0:TOPK],
                                     both[:, :].unsqueeze(2).broadcast_to([P, T, TOPK]), ALU.mult))
        dve.wait_ge(top, 2 * T)
        link(nc.vector.tensor_copy(top_i[:, :, :], raw[:, :, 0:TOPK]))

    @stage.scalar
    def _(act):
        act.wait_ge(shifted, 1)
        nc.scalar.activation(probs[:, :, :], logits[:, :, :], ACT.Exp).then_inc(exped, 1)

    return stage


def stage_dispatch(c, s, tag, src, mean, rstd, q, place, slots):
    nc = c.nc
    stage = Stage()
    rows = s.enter_context(nc.sbuf_tensor(tag + "_rows", [P, U, D], F32))
    idx = s.enter_context(nc.sbuf_tensor(tag + "_idx", [P, U, TOPK], I32))
    idx_ready, rows_ready, cast = (c.semaphore(f"{tag}_{n}") for n in ("idx_ready", "rows_ready", "cast"))
    placed = [c.semaphore(f"{tag}_placed{k}") for k in range(U)]

    @stage.vector
    def _(dve):
        nc.vector.tensor_copy(place[:, :, :], q.rearrange("p (t e) -> p t e", e=TOPK)).then_inc(cast, 1)
        dve.wait_ge(cast, 1)

        def body(i, first):
            for k in range(U):
                t = i * U + k
                if not first:
                    wait_slot(dve, placed[k], i * (16 * TOPK))
                nc.vector.tensor_copy(idx[:, k, :], flat(place[:, ds(t, 1), :])).then_inc(idx_ready, 1)
                nc.vector.tensor_scalar(rows[:, k, :], flat(src[:, ds(t, 1), :]), mean[:, ds(t, 1)], rstd[:, ds(t, 1)],
                                        ALU.subtract, ALU.mult).then_inc(rows_ready, 1)

        repeat(dve, T // U, body)

    @stage.gpsimd
    def _(pool):
        with pool.Fori(0, T // U) as i:
            for k in range(U):
                pool.wait_ge(idx_ready, i * U + k + 1)
                wait_slot(pool, rows_ready, i * U + k + 1)
                for e in range(TOPK):
                    nc.gpsimd.indirect_dma_start(
                        out=slots, out_offset=bass.IndirectOffsetOnAxis(ap=idx[:, k, e:e + 1], axis=0),
                        in_=rows[:, k, :], in_offset=None).then_inc(placed[k], 16)
        for k in range(U):
            pool.wait_ge(placed[k], 16 * TOPK * T // U)

    return stage


def stage_expert_blocks(c, s, tag, slots, results, experts_of, w1, w2, gain, shift, bias1, bias2):
    nc = c.nc
    HC = H0 // 128
    KC = D // 128
    Q = B // 128
    assert BLOCKS % 2 == 0
    stage = Stage()
    sb = lambda n, shape, dt=F32: s.enter_context(nc.sbuf_tensor(f"{tag}_{n}", shape, dt))
    w1_sb = [sb(f"w1_{b}", [128, KC, H0]) for b in range(2)]
    w2_sb = [sb(f"w2_{b}", [128, HC, D]) for b in range(2)]
    rows = [sb(f"rows_{b}", [128, Q, D]) for b in range(2)]
    rows_t = [sb(f"rows_t_{b}", [128, KC, B]) for b in range(2)]
    hidden = sb("hidden", [128, HC, B])
    y = [sb(f"y_{b}", [128, Q, D]) for b in range(2)]
    ps_h = [c.banks[b][:, 0:B] for b in range(4)]
    ps_y = [c.banks[4 + q][:, 0:D] for q in range(Q)]
    ps_t = c.banks[6][:, 0:KC * B].rearrange("p (j n) -> p j n", j=KC)
    sem = lambda n: c.semaphore(f"{tag}_{n}")
    turned, scaled, up, gelu_done, down, y_ready = (
        sem(n) for n in ("turned", "scaled", "up", "gelu_done", "down", "y_ready"))
    rows_in, w1_in, w2_in, y_out = ([sem(f"{n}{b}") for b in range(2)] for n in ("rows_in", "w1_in", "w2_in", "y_out"))
    slots_v = slots.rearrange("(n q p) f -> n p q f", q=Q, p=128)
    results_v = results.rearrange("(n q p) f -> n p q f", q=Q, p=128)

    @stage.sync
    def _(sp):
        def load_weights(n, b):
            e = sp.value_load(experts_of[0:1, ds(n, 1)], min_val=0, max_val=EXPERTS - 1)
            sp.dma_start(w1_sb[b][:, :, :], w1[ds(e, 1)].rearrange("a p j h -> (a p) j h")).then_inc(w1_in[b], 16)
            sp.dma_start(w2_sb[b][:, :, :], w2[ds(e, 1)].rearrange("a p j h -> (a p) j h")).then_inc(w2_in[b], 16)

        def load_rows(n, b):
            sp.dma_start(rows[b][:, :, :], slots_v[ds(n, 1)].rearrange("a p q f -> (a p) q f")).then_inc(rows_in[b], 16)

        def store(n, b):
            sp.dma_start(results_v[ds(n, 1)].rearrange("a p q f -> (a p) q f"), y[b][:, :, :]).then_inc(y_out[b], 16)

        for b in range(2):
            load_rows(b, b)
            load_weights(b, b)
        with sp.Fori(0, BLOCKS // 2 - 1) as i:
            for b in range(2):
                n = i * 2 + b + 2
                wait_slot(sp, turned, n - 1)
                load_rows(n, b)
                wait_slot(sp, down, (n - 1) * Q)
                load_weights(n, b)
                wait_slot(sp, y_ready, (n - 1) * Q)
                store(n - 2, b)
        sp.wait_ge(turned, BLOCKS - 1)
        load_rows(BLOCKS, 0)
        for b in range(2):
            sp.wait_ge(y_ready, (BLOCKS - 1 + b) * Q)
            store(BLOCKS - 2 + b, b)
        for b in range(2):
            sp.wait_ge(y_out[b], 16 * BLOCKS // 2)

    @stage.vector
    def _(dve):
        def scale_rows(n, b):
            e = dve.value_load(experts_of[0:1, ds(n, 1)], min_val=0, max_val=EXPERTS - 1)
            wait_slot(dve, turned, n + 1)
            for j in range(KC):
                last = nc.vector.tensor_scalar(rows_t[b][:, j, :], ps_t[:, j, :], gain[:, ds(e * KC + j, 1)],
                                               shift[:, ds(e * KC + j, 1)], ALU.mult, ALU.add)
            last.then_inc(scaled, 1)

        def body(i, first):
            for b in range(2):
                n = i * 2 + b
                scale_rows(n + 1, 1 - b)
                e = dve.value_load(experts_of[0:1, ds(n, 1)], min_val=0, max_val=EXPERTS - 1)
                if not first:
                    wait_slot(dve, y_out[b], i * 16)
                for q in range(Q):
                    wait_slot(dve, down, n * Q + q + 1)
                    nc.vector.tensor_tensor(y[b][:, q, :], ps_y[q],
                                            flat(bias2[:, ds(e, 1), :]), ALU.add).then_inc(y_ready, 1)

        scale_rows(0, 0)
        repeat(dve, BLOCKS // 2, body)

    @stage.scalar
    def _(act):
        with act.Fori(0, BLOCKS // 2) as i:
            for b in range(2):
                n = i * 2 + b
                e = act.value_load(experts_of[0:1, ds(n, 1)], min_val=0, max_val=EXPERTS - 1)
                for h in range(HC):
                    wait_slot(act, up, n * HC + h + 1)
                    nc.scalar.activation(hidden[:, h, :], ps_h[h % 4], ACT.Gelu,
                                         bias=bias1[:, ds(e * HC + h, 1)]).then_inc(gelu_done, 1)

    @stage.tensor
    def _(pe):
        def turn_rows(b, arrived):
            wait_slot(pe, rows_in[b], arrived)
            for q in range(Q):
                for j in range(KC):
                    last = nc.tensor.transpose(ps_t[:, j, q * 128:(q + 1) * 128],
                                               rows[b][:, q, j * 128:(j + 1) * 128], c.ident[:, :])
            last.then_inc(turned, 1)

        def body(i, first):
            for b in range(2):
                n = i * 2 + b
                pe.wait_ge(w1_in[b], i * 16 + 16)
                wait_slot(pe, scaled, n + 1)
                for h in range(HC):
                    if not (first and b == 0 and h < 4):
                        wait_slot(pe, gelu_done, n * HC + h - 3)
                    for j in range(KC):
                        last = nc.tensor.matmul(ps_h[h % 4], w1_sb[b][:, j, h * 128:(h + 1) * 128], rows_t[b][:, j, :],
                                                start=(j == 0), stop=(j == KC - 1))
                    last.then_inc(up, 1)
                turn_rows(1 - b, i * 16 + 16 + 16 * b)
                pe.wait_ge(w2_in[b], i * 16 + 16)
                if not (first and b == 0):
                    pe.wait_ge(y_ready, n * Q)
                wait_slot(pe, gelu_done, n * HC + (HC - 2))
                for q in range(Q):
                    for h in range(HC):
                        if q == 0 and h >= HC - 2:
                            wait_slot(pe, gelu_done, n * HC + (h + 1))
                        last = nc.tensor.matmul(ps_y[q], hidden[:, h, q * 128:(q + 1) * 128], w2_sb[b][:, h, :],
                                                start=(h == 0), stop=(h == HC - 1))
                    last.then_inc(down, 1)

        turn_rows(0, 16)
        repeat(pe, BLOCKS // 2, body)

    return stage


def stage_combine(c, s, tag, results, place, weights, acc):
    nc = c.nc
    stage = Stage()
    got = s.enter_context(nc.sbuf_tensor(tag + "_got", [P, U, TOPK, D], F32))
    idx = s.enter_context(nc.sbuf_tensor(tag + "_idx", [P, U, TOPK], I32))
    staged, added = c.semaphore(tag + "_staged"), c.semaphore(tag + "_added")
    gathered = [c.semaphore(f"{tag}_gathered{k}") for k in range(U)]

    @stage.scalar
    def _(act):
        def body(i, first):
            for k in range(U):
                t = i * U + k
                if not first:
                    wait_slot(act, added, (t - U + 1) * TOPK)
                nc.scalar.copy(idx[:, k, :], flat(place[:, ds(t, 1), :])).then_inc(staged, 1)

        repeat(act, T // U, body)

    @stage.gpsimd
    def _(pool):
        with pool.Fori(0, T // U) as i:
            for k in range(U):
                wait_slot(pool, staged, i * U + k + 1)
                for e in range(TOPK):
                    nc.gpsimd.indirect_dma_start(
                        out=got[:, k, e, :], out_offset=None, in_=results,
                        in_offset=bass.IndirectOffsetOnAxis(ap=idx[:, k, e:e + 1], axis=0)).then_inc(gathered[k], 16)

    @stage.vector
    def _(dve):
        with dve.Fori(0, T // U) as i:
            for k in range(U):
                t = i * U + k
                here = flat(acc[:, ds(t, 1), :])
                wait_slot(dve, gathered[k], (i + 1) * (16 * TOPK))
                for e in range(TOPK):
                    if e:
                        wait_slot(dve, added, t * TOPK + e)
                    nc.vector.scalar_tensor_tensor(
                        out=here, in0=got[:, k, e, :], scalar=weights[:, ds(t, 1), e], in1=here,
                        op0=ALU.mult, op1=ALU.add).then_inc(added, 1)
        dve.wait_ge(added, T * TOPK)

    return stage


def stage_degree_norm(c, s, tag, deg, dinv):
    nc = c.nc
    stage = Stage()
    root = s.enter_context(nc.sbuf_tensor(tag + "_root", [P, T], F32))
    chain, rooted = (c.semaphore(f"{tag}_{n}") for n in ("chain", "rooted"))

    @stage.vector
    def _(dve):
        nc.vector.tensor_scalar(deg[:, :], deg[:, :], 1.0, 1.0, ALU.add, ALU.max).then_inc(chain, 1)
        dve.wait_ge(rooted, 1)
        nc.vector.reciprocal(dinv[:, :], root[:, :]).then_inc(chain, 1)
        dve.wait_ge(chain, 2)

    @stage.scalar
    def _(act):
        act.wait_ge(chain, 1)
        nc.scalar.activation(root[:, :], deg[:, :], ACT.Sqrt).then_inc(rooted, 1)

    return stage


def stage_batch_norm(c, s, tag, acc, width, dinv, bias, gain, shift):
    nc = c.nc
    stage = Stage()
    sb = lambda n, shape: s.enter_context(nc.sbuf_tensor(f"{tag}_{n}", shape, F32))
    square, part = sb("square", [P, T, width]), sb("part", [P, width])
    mean, var, std = sb("mean", [P, width]), sb("var", [P, width]), sb("std", [P, width])
    ps = c.banks[6][0:P, 0:width]
    chain, part_ready, centred, squared, summed, var_ready, std_ready, finished = (
        c.semaphore(f"{tag}_{n}")
        for n in ("chain", "part_ready", "centred", "squared", "summed", "var_ready", "std_ready", "finished"))
    GROUPS = T // U
    group = lambda v, g: v[:, g * U:(g + 1) * U, :]
    rows = lambda v, tiles: v[0:P, 0:width].unsqueeze(1).broadcast_to([P, tiles, width])
    stage.ready = lambda t: (finished, 2 * (t // U + 1))

    @stage.vector
    def _(dve):
        V = nc.vector
        link = linker(dve, chain)
        link(V.tensor_tensor(acc[:, :, :], acc[:, :, :], dinv[:, :].unsqueeze(2).broadcast_to([P, T, width]), ALU.mult))
        link(V.tensor_tensor(acc[:, :, :], acc[:, :, :], rows(bias, T), ALU.add))
        V.tensor_reduce(part[:, :], acc[:, :, :].rearrange("p t f -> p f t"), AX.X, ALU.add).then_inc(part_ready, 1)
        dve.wait_ge(summed, 1)
        link(V.tensor_scalar(mean[:, :], ps, 1.0 / NODES, None, ALU.mult))
        for g in range(GROUPS):
            V.tensor_tensor(group(acc, g), group(acc, g), rows(mean, U), ALU.subtract).then_inc(centred, 1)
        dve.wait_ge(squared, GROUPS)
        V.tensor_reduce(part[:, :], square[:, :, :].rearrange("p t f -> p f t"), AX.X, ALU.add).then_inc(part_ready, 1)
        dve.wait_ge(summed, 2)
        V.tensor_scalar(var[:, :], ps, 1.0 / NODES, BN_EPS, ALU.mult, ALU.add).then_inc(var_ready, 1)
        dve.wait_ge(std_ready, 1)
        link(V.reciprocal(var[:, :], std[:, :]))
        link(V.tensor_tensor(var[:, :], var[:, :], gain[0:P, :], ALU.mult))
        link = linker(dve, finished)
        for g in range(GROUPS):
            link(V.tensor_tensor(group(acc, g), group(acc, g), rows(var, U), ALU.mult))
            link(V.tensor_tensor(group(acc, g), group(acc, g), rows(shift, U), ALU.add))

    @stage.scalar
    def _(act):
        for g in range(GROUPS):
            act.wait_ge(centred, g + 1)
            nc.scalar.activation(group(square, g), group(acc, g), ACT.Square).then_inc(squared, 1)
        act.wait_ge(var_ready, 1)
        nc.scalar.activation(std[:, :], var[:, :], ACT.Sqrt).then_inc(std_ready, 1)

    @stage.tensor
    def _(pe):
        for n in range(2):
            pe.wait_ge(part_ready, n + 1)
            nc.tensor.matmul(ps, c.ones[0:P, 0:P], part[:, :], start=True, stop=True).then_inc(summed, 1)

    return stage


def stage_fc_end(c, s, tag, fc, acc):
    nc = c.nc
    stage = Stage()
    chain = c.semaphore(tag + "_chain")

    @stage.vector
    def _(dve):
        link = linker(dve, chain)
        link(nc.vector.scalar_tensor_tensor(out=acc[:, :, :], in0=fc[:, :, :], scalar=0.0, in1=acc[:, :, :],
                                            op0=ALU.max, op1=ALU.add))

    return stage


def stage_pick_experts(c, s, tag, rows_ready, rows_t, router, bias, picked, picked_w):
    nc = c.nc
    E = EXPERTS
    capacity = float(-(-NODES * 125 // (100 * E)))
    stage = Stage()
    sb = lambda n, shape, dt=F32: s.enter_context(nc.sbuf_tensor(f"{tag}_{n}", shape, dt))
    mean = sb("mean", [128, 2])
    z, p, load, one, top, top_w = (sb("z", [1, E]), sb("p", [1, E]), sb("load", [1, E]), sb("one", [1, 1]),
                                   sb("top", [1, 8]), sb("top_w", [1, TOPK]))
    top_i = sb("top_i", [1, 8], U32)
    ps_l, ps_w = c.banks[6][0:1, 0:E], c.banks[7][:, 0:TOPK]
    chain, mean_ready, product, to_exp, exped, weights_ready = (
        c.semaphore(f"{tag}_{n}")
        for n in ("chain", "mean_ready", "product", "to_exp", "exped", "weights_ready"))

    @stage.vector
    def _(dve):
        V = nc.vector
        link = linker(dve, chain)
        rounds = [0]

        def softmax(src, out, n, signal=None):
            rounds[0] += 1
            link(V.tensor_reduce(one[:, :], src[0:1, 0:n], AX.X, ALU.max))
            V.tensor_scalar(z[0:1, 0:n], src[0:1, 0:n], one[0:1, 0:1], None, ALU.subtract).then_inc(to_exp, 1)
            dve.wait_ge(exped, rounds[0])
            link(V.tensor_reduce(one[:, :], p[0:1, 0:n], AX.X, ALU.add))
            link(V.reciprocal(one[:, :], one[:, :]))
            scaled = V.tensor_scalar(out[0:1, 0:n], p[0:1, 0:n], one[0:1, 0:1], None, ALU.mult)
            if signal is None:
                link(scaled)
            else:
                scaled.then_inc(signal, 1)

        dve.wait_ge(*rows_ready)
        link(V.tensor_reduce(mean[:, :], rows_t[:, :, :], AX.X, ALU.add))
        V.tensor_scalar(mean[:, :], mean[:, :], 1.0 / NODES, None, ALU.mult).then_inc(mean_ready, 1)
        dve.wait_ge(product, 1)
        link(V.tensor_tensor(p[:, :], ps_l, bias[0:1, :], ALU.add))
        softmax(p, p, E)
        link(V.tensor_scalar(load[:, :], p[:, :], float(NODES), None, ALU.mult))
        link(V.reciprocal(load[:, :], load[:, :]))
        link(V.tensor_scalar(load[:, :], load[:, :], capacity, 1.0, ALU.mult, ALU.min))
        link(V.tensor_tensor(p[:, :], p[:, :], load[:, :], ALU.mult))
        softmax(p, p, E)
        link(V.max(top[:, :], p[:, :]))
        link(V.max_index(top_i[:, :], top[:, :], p[:, :]))
        link(V.tensor_copy(picked[:, :], top_i[0:1, 0:TOPK]))
        softmax(top, top_w, TOPK, signal=weights_ready)
        dve.wait_ge(product, 2)
        link(V.tensor_copy(picked_w[:, :], ps_w))

    @stage.scalar
    def _(act):
        for n, width in enumerate((E, E, TOPK)):
            act.wait_ge(to_exp, n + 1)
            nc.scalar.activation(p[0:1, 0:width], z[0:1, 0:width], ACT.Exp).then_inc(exped, 1)

    @stage.tensor
    def _(pe):
        pe.wait_ge(mean_ready, 1)
        for j in range(2):
            last = nc.tensor.matmul(ps_l, mean[:, j:j + 1], router[:, j, :], start=(j == 0), stop=(j == 1))
        last.then_inc(product, 1)
        pe.wait_ge(weights_ready, 1)
        nc.tensor.matmul(ps_w, c.ones[0:1, :], top_w[:, :], start=True, stop=True).then_inc(product, 1)

    return stage


def stage_shared_ffn(c, s, tag, rows_t, picked, picked_w, w1, w2, b1, b2, mean, rstd, gamma, beta, out):
    nc = c.nc
    FC, KC = H1 // 128, D // 128
    F = TOPK * FC
    RING = (0, 1, 2, 0, 1)
    BACK = (2, 2, 5, 3, 3)
    stage = Stage()
    sb = lambda n, shape, dt=F32: s.enter_context(nc.sbuf_tensor(f"{tag}_{n}", shape, dt))
    w1_sb, w2_sb = sb("w1", [128, TOPK, KC, H1]), sb("w2", [128, F, D])
    b1_sb, b2_sb = sb("b1", [128, TOPK, FC]), sb("b2", [P, TOPK, D])
    hidden = [sb(f"hidden{k}", [128, F, P]) for k in range(U)]
    z, st = sb("z", [P, 2, U, D]), sb("st", [P, U, 6])
    dm, z_mean, var, std, z_rstd = (sb(n, [P, U]) for n in ("dm", "z_mean", "var", "std", "z_rstd"))
    ps_h = [c.banks[b][:, 0:P] for b in range(4)]
    ps_y = [c.banks[4 + b][0:P, 0:D] for b in range(3)]
    sem = lambda n: c.semaphore(f"{tag}_{n}")
    w1_in, w2_in, b2_in, w2_scaled, up, gelu_done, down, taken = (
        sem(n) for n in ("w1_in", "w2_in", "b2_in", "w2_scaled", "up", "gelu_done", "down", "taken"))
    b2_made, normal, stats, reduced, var_ready, std_ready, finished = (
        sem(n) for n in ("b2_made", "normal", "stats", "reduced", "var_ready", "std_ready", "finished"))
    stored = [sem(f"stored{b}") for b in range(2)]
    out_v = out.rearrange("(t p) f -> p t f", p=P)
    REDUCE, FINISH = 5, 5

    @stage.sync
    def _(sp):
        for k in range(TOPK):
            e = sp.value_load(picked[0:1, k:k + 1], min_val=0, max_val=EXPERTS - 1)
            sp.dma_start(w1_sb[:, k, :, :], w1[ds(e, 1)].rearrange("a p j h -> (a p) j h")).then_inc(w1_in, 16)
            sp.dma_start(b1_sb[:, k, :], b1[ds(e, 1)].rearrange("a p j -> (a p) j")).then_inc(w1_in, 16)
            sp.dma_start(w2_sb[:, k * FC:(k + 1) * FC, :],
                         w2[ds(e, 1)].rearrange("a p j h -> (a p) j h")).then_inc(w2_in, 16)
            sp.dma_start(b2_sb[:, k, :], b2[ds(e, 1), :].broadcast_to([P, D])).then_inc(b2_in, 16)
        for g in range(T // U):
            sp.wait_ge(finished, (g + 1) * FINISH)
            sp.dma_start(out_v[:, g * U:(g + 1) * U, :], z[:, g % 2, :, :]).then_inc(stored[g % 2], 16)
        for b in range(2):
            sp.wait_ge(stored[b], 16 * (T // U // 2 + (1 - b) * (T // U % 2)))

    @stage.vector
    def _(dve):
        V = nc.vector
        dve.wait_ge(w2_in, 32)
        for k in range(TOPK):
            V.tensor_scalar(w2_sb[:, k * FC:(k + 1) * FC, :], w2_sb[:, k * FC:(k + 1) * FC, :],
                            picked_w[:, k:k + 1], None, ALU.mult).then_inc(w2_scaled, 1)
        dve.wait_ge(b2_in, 32)
        link = linker(dve, b2_made)
        link(V.tensor_scalar(b2_sb[:, 0, :], b2_sb[:, 0, :], picked_w[0:P, 0:1], None, ALU.mult))
        link(V.scalar_tensor_tensor(out=b2_sb[:, 0, :], in0=b2_sb[:, 1, :], scalar=picked_w[0:P, 1:2],
                                    in1=b2_sb[:, 0, :], op0=ALU.mult, op1=ALU.add))

        def take(g, k):
            t = g * U + k
            here = z[:, g % 2, k, :]
            V.tensor_scalar(here, c.x[:, t, :], mean[:, t:t + 1], rstd[:, t:t + 1],
                            ALU.subtract, ALU.mult).then_inc(normal, 1)
            dve.wait_ge(normal, t * 2 + 1)
            V.tensor_tensor(c.x[:, t, :], c.x[:, t, :], beta[0:P, :], ALU.add)
            V.tensor_tensor(here, here, b2_sb[:, 0, :], ALU.add).then_inc(normal, 1)
            dve.wait_ge(normal, t * 2 + 2)
            dve.wait_ge(down, t + 1)
            V.tensor_tensor(here, here, ps_y[RING[k]], ALU.add).then_inc(taken, 1)

        def reduce(g):
            dve.wait_ge(taken, (g + 1) * U)
            for k in range(U):
                V.bn_stats(st[:, k, :], z[:, g % 2, k, :]).then_inc(stats, 1)
            dve.wait_ge(stats, (g + 1) * U)
            link = linker(dve, reduced, g * REDUCE)
            link(V.tensor_tensor(dm[:, :], st[:, :, 1], st[:, :, 4], ALU.subtract))
            link(V.tensor_tensor(dm[:, :], dm[:, :], dm[:, :], ALU.mult))
            link(V.tensor_tensor(var[:, :], st[:, :, 2], st[:, :, 5], ALU.add))
            link(V.scalar_tensor_tensor(out=var[:, :], in0=dm[:, :], scalar=D / 4.0, in1=var[:, :],
                                        op0=ALU.mult, op1=ALU.add))
            V.tensor_scalar(var[:, :], var[:, :], 1.0 / D, LN_EPS, ALU.mult, ALU.add).then_inc(var_ready, 1)
            link(V.tensor_tensor(z_mean[:, :], st[:, :, 1], st[:, :, 4], ALU.add))
            V.tensor_scalar(z_mean[:, :], z_mean[:, :], 0.5, None, ALU.mult).then_inc(var_ready, 1)

        def finish(g):
            here, x_here = z[:, g % 2, :, :], c.x[:, g * U:(g + 1) * U, :]
            wide = lambda v: v[:, :].unsqueeze(2).broadcast_to([P, U, D])
            dve.wait_ge(var_ready, 2 * g + 2)
            link = linker(dve, finished, g * FINISH)
            link(V.tensor_tensor(here, here, wide(z_mean), ALU.subtract))
            dve.wait_ge(std_ready, g + 1)
            link(V.reciprocal(z_rstd[:, :], std[:, :]))
            link(V.tensor_tensor(here, here, wide(z_rstd), ALU.mult))
            link(V.tensor_tensor(here, here, gamma[0:P, :].unsqueeze(1).broadcast_to([P, U, D]), ALU.mult))
            link(V.tensor_tensor(here, here, x_here, ALU.add))

        for g in range(T // U):
            if g > 1:
                dve.wait_ge(stored[g % 2], 16 * (g // 2))
            for k in range(U):
                if g and k == 3:
                    finish(g - 1)
                take(g, k)
            reduce(g)
        finish(T // U - 1)

    @stage.scalar
    def _(act):
        act.wait_ge(w1_in, 64)

        def body(g, first):
            for k in range(U):
                for f in range(F):
                    wait_slot(act, up, (g * U + k) * F + f + 1)
                    nc.scalar.activation(hidden[k][:, f, :], ps_h[f % 4], ACT.Gelu,
                                         bias=b1_sb[:, f // FC, f % FC:f % FC + 1]).then_inc(gelu_done, 1)
                if k == 2 and not first:
                    wait_slot(act, var_ready, g * 2)
                    nc.scalar.activation(std[:, :], var[:, :], ACT.Sqrt).then_inc(std_ready, 1)

        repeat(act, T // U, body)
        act.wait_ge(var_ready, T // U * 2)
        nc.scalar.activation(std[:, :], var[:, :], ACT.Sqrt).then_inc(std_ready, 1)

    @stage.tensor
    def _(pe):
        def rise(t, first=False):
            for f in range(F):
                if not (first and f < 4):
                    wait_slot(pe, gelu_done, t * F + f - 3)
                for j in range(KC):
                    mm = nc.tensor.matmul(ps_h[f % 4], w1_sb[:, f // FC, j, (f % FC) * 128:(f % FC + 1) * 128],
                                          rows_t[:, j, ds(t * P, P)], start=(j == 0), stop=(j == KC - 1))
                mm.then_inc(up, 1)

        def fall(i, k, first):
            if not (first and k < 3):
                wait_slot(pe, taken, i * U + k - BACK[k] + 1)
            wait_slot(pe, gelu_done, (i * U + k + 1) * F)
            for f in range(F):
                mm = nc.tensor.matmul(ps_y[RING[k]], hidden[k][:, f, :], w2_sb[:, f, :], start=(f == 0), stop=(f == F - 1))
            mm.then_inc(down, 1)

        def body(i, first, last):
            for k in range(U):
                if not (last and k == U - 1):
                    rise(i * U + k + 1)
                fall(i, k, first)

        pe.wait_ge(w1_in, 64)
        rise(0, first=True)
        pe.wait_ge(w2_scaled, TOPK)
        repeat(pe, T // U, body, last=True)

    return stage


def flat(ap):
    return ap.rearrange("p a f -> p (a f)")


def allocator(nc, stack):
    return lambda name, shape, dt=F32: stack.enter_context(nc.sbuf_tensor(name, shape, dt))


def halves(w):
    return w.rearrange("(j p) m -> p j m", p=128)


def layer0_graph(c, scratch, mean, rstd, g1):
    nc, args = c.nc, c.args
    V = nc.vector
    with ExitStack() as s:
        sb = allocator(nc, s)
        w = sb("g0_w", [128, 2, D])
        lists = sb("g0_lists", [S, PARTS, SLOTS])
        table, tiles_of = sb("g0_table", [S, SLOTS, 4]), sb("g0_tiles_of", [1, PAIRS], I32)
        with ExitStack() as s1:
            sb1 = allocator(nc, s1)
            rec, tile_of_edge = sb1("g0_rec", [P, EC, 4]), sb1("g0_tile", [P, EC])
            place_i = sb1("g0_place_i", [P, EC], I32)
            q, ends = sb1("g0_q", [P, EC]), sb1("g0_ends", [P, T])
            fields = sb1("g0_fields", [P, BY_PRODUCTS, 2 + PARTS])
            edges = stage_load_edges(c, s1, "edges")
            with ExitStack() as s2:
                run(c, stage_constants(c, s2), edges, stage_load(c, s2, "g0_w", [(w[:, :, :], halves(args["g0_w"]))]))
                run(c, stage_load(c, s2, "params", c.param_loads),
                    stage_fill(c, s2, "fill", [scratch["rows0"], scratch["rows1"]], scratch["slots"]),
                    stage_edge_records(c, s2, "g0r", c.src_i, c.dst_i, rec, tile_of_edge),
                    rank := stage_rank_buckets(c, s2, "g0k", tile_of_edge, EC, T, 2 * S, q, ends),
                    stage_places(c, s2, "g0p", q, place_i, rec=rec, fields=fields),
                    stage_bucket_table(c, s2, "g0t", rank, ends, T, PAIRS, tiles_of))
            with ExitStack() as s2:
                sb2 = allocator(nc, s2)
                support = sb2("g0_support", [P, T, D])
                g1_tile, g1_q, g1_ends = g1["tile"], sb2("g1_q", [P, EC]), sb2("g1_ends", [P, T])
                run(c, stage_place_by_products(c, s2, "g0b", fields, lists),
                    stage_norm_stats(c, s2, "g0", c.x, mean, rstd),
                    stage_project(c, s2, "g0x", c.x, D, w, D,
                                  lambda t, ps: [lambda: V.tensor_copy(flat(support[:, ds(t, 1), :]), ps)],
                                  norm=(mean, rstd), dram=(scratch["support"], support[:, :, :])),
                    stage_edge_records(c, s2, "g1r", c.dst_i, c.src_i, g1["rec"], g1_tile),
                    rank := stage_rank_buckets(c, s2, "g1k", g1_tile, EC, T, S, g1_q, g1_ends),
                    stage_places(c, s2, "g1p", g1_q, g1["place_i"], SLOTS1),
                    stage_bucket_table(c, s2, "g1t", rank, g1_ends, T, SLOTS1, g1["tiles_of"]),
                    stage_scatter_records(c, s2, "g0s", rec, place_i, scratch["rows0"], table, BY_PRODUCTS))
        with ExitStack() as s1:
            run(c, merge := stage_merge(c, s1, "g0m", lists, table),
                stage_aggregate(c, s1, "g0a", table, tiles_of, scratch["support"], D, c.x,
                                table_ready=merge.merged,
                                aside=CountDegrees(c, s1, "g1d", AGGREGATE_STEPS, g1["rec"], g1["tile"], g1["dinv"])),
                stage_degree_norm(c, s1, "g1n", g1["dinv"], g1["dinv"]))


def layer0_ffn(c, scratch, mean, rstd, g1):
    nc, args = c.nc, c.args
    with ExitStack() as s:
        sb = allocator(nc, s)
        place, weights = sb("f0_place", [P, T, TOPK], I32), sb("f0_weights", [P, T, TOPK])
        experts_of = sb("f0_experts_of", [1, BLOCKS + 1], I32)
        with ExitStack() as s2:
            sb2 = allocator(nc, s2)
            xt = sb2("f0_xt", [P, T, D])
            mean2, rstd2 = sb2("f0_mean2", [P, T]), sb2("f0_rstd2", [P, T])
            logits, probs = sb2("f0_logits", [P, T, EXPERTS]), sb2("f0_probs", [P, T, EXPERTS])
            top_i = sb2("f0_top_i", [P, T, TOPK])
            q, ends = sb2("f0_q", [P, T * TOPK]), sb2("f0_ends", [P, EXPERTS])
            run(c, stage_norm_stats(c, s2, "f0", c.x, mean, rstd),
                normed := stage_normalise(c, s2, "f0n", c.x, mean, rstd, xt),
                stage_norm_stats(c, s2, "f0b", xt, mean2, rstd2),
                stage_project(c, s2, "f0x", xt, D, c.param["f0_router"], EXPERTS,
                              lambda t, ps: [lambda: nc.scalar.copy(flat(logits[:, ds(t, 1), :]), ps)],
                              source_ready=normed.ready, preparer="gpsimd", out_engine="scalar"),
                stage_route(c, s2, "f0r", logits, c.param["f0_bias"], probs, top_i, weights),
                rank := stage_rank_buckets(c, s2, "f0k", flat(top_i[:, :, :]), T * TOPK, EXPERTS, B, q, ends),
                stage_bucket_table(c, s2, "f0t", rank, ends, EXPERTS, BLOCKS + 1, experts_of),
                stage_dispatch(c, s2, "f0d", xt, mean2, rstd2, q[:, :], place, scratch["slots"]))
        with ExitStack() as s2:
            run(c, stage_expert_blocks(c, s2, "f0e", scratch["slots"], scratch["results"], experts_of, args["f0_w1"],
                                       args["f0_w2"], *(c.param["f0_" + n] for n in ("gain", "shift", "bias1", "bias2"))),
                stage_scatter_records(c, s2, "g1s", g1["rec"], g1["place_i"], scratch["rows1"], g1["table"]))
        with ExitStack() as s2:
            run(c, stage_combine(c, s2, "f0c", scratch["results"], place, weights, c.x),
                stage_norm_stats(c, s2, "g1", c.x, mean, rstd))


def layer1_graph(c, scratch, mean, rstd, g1):
    nc, args = c.nc, c.args
    V = nc.vector
    with ExitStack() as s:
        sb = allocator(nc, s)
        table, tiles_of, dinv = g1["table"], g1["tiles_of"], g1["dinv"]
        h1, h2 = sb("g1_h1", [P, T, C1]), sb("g1_h2", [P, T, C2])
        turned = sb("g1_turned", [128, (D + C1) // 128, NODES])
        with ExitStack() as s2:
            run(c, stage_project(c, s2, "g1a", c.x, D, c.param["w1"], C1, lambda t, ps: [
                lambda: V.tensor_scalar(flat(h1[:, ds(t, 1), :]), ps, dinv[:, ds(t, 1)], None, ALU.mult)],
                norm=(mean, rstd), keep_t=turned[:, 0:2, :], dram=(scratch["h1"], h1[:, :, :])))
        with ExitStack() as s2:
            run(c, stage_aggregate_narrow(c, s2, "g1b", table, tiles_of, scratch["h1"], C1, h1),
                normed := stage_batch_norm(c, s2, "g1c", h1, C1, dinv, *(c.param[n] for n in ("b1", "g1", "be1"))),
                stage_project(c, s2, "g1e", h1, C1, c.param["w2"], C2, lambda t, ps: [
                lambda: V.tensor_scalar(flat(h2[:, ds(t, 1), :]), ps, dinv[:, ds(t, 1)], None, ALU.mult)],
                keep_t=turned[:, 2:3, :], source_ready=normed.ready, relu=True,
                preparer="gpsimd", dram=(scratch["h2"], h2[:, :, :])))
        with ExitStack() as s2:
            fc = allocator(nc, s2)("g1_fc", [P, T, D])
            run(c, stage_aggregate_narrow(c, s2, "g1f", table, tiles_of, scratch["h2"], C2, h2,
                                          aside=MultiplyTiles(c, s2, "g1x", AGGREGATE1_STEPS,
                                                              turned, c.param["wfc"], c.param["bfc"], fc)),
                normed := stage_batch_norm(c, s2, "g1g", h2, C2, dinv, *(c.param[n] for n in ("b2", "g2", "be2"))),
                stage_project(c, s2, "g1h", h2, C2, c.param["wfc_end"], D, lambda t, ps: [
                lambda: V.tensor_tensor(flat(fc[:, ds(t, 1), :]), flat(fc[:, ds(t, 1), :]), ps, ALU.add)],
                source_ready=normed.ready, relu=True, preparer="gpsimd"),
                stage_fc_end(c, s2, "g1i", fc, c.x),
                stage_norm_stats(c, s2, "f1", c.x, mean, rstd))


def layer1_ffn(c, out, mean, rstd):
    nc, args = c.nc, c.args
    with ExitStack() as s:
        sb = allocator(nc, s)
        rows_t = sb("f1_rows_t", [128, 2, NODES])
        picked, picked_w = sb("f1_picked", [1, TOPK], I32), sb("f1_picked_w", [128, TOPK])
        with ExitStack() as s2:
            run(c, turn := stage_project(c, s2, "f1a", c.x, D, None, 0, None, norm=(mean, rstd), keep_t=rows_t),
                stage_pick_experts(c, s2, "f1b", turn.kept, rows_t,
                                   c.param["f1_router"], c.param["f1_bias"], picked, picked_w))
        with ExitStack() as s2:
            run(c, stage_shared_ffn(c, s2, "f1c", rows_t, picked, picked_w, args["f1_w1"], args["f1_w2"], args["f1_b1"],
                                    args["f1_b2"], mean, rstd, c.param["gamma"], c.param["beta"], out))


def part(nc, emit):
    with nc.cleanup_on_exit():
        emit()
    nc.all_engine_barrier()


def build(nc, args, out, scratch):
    with ExitStack() as ctx:
        c = Core(nc, ctx, args)
        c.iota, c.ident = c.keep("iota", [128, 512]), c.keep("ident", [128, 128])
        c.ones, c.before = c.keep("ones", [128, 128]), c.keep("before", [128, 128])
        c.x = c.keep("x_now", [P, T, D])
        c.psum = ctx.enter_context(nc.psum_tensor("psum", [128, 8 * 512], F32))
        c.banks = [c.psum[:, b * 512:(b + 1) * 512] for b in range(8)]
        mean, rstd = c.keep("mean", [P, T]), c.keep("rstd", [P, T])
        c.load_params()
        g1 = {"rec": c.keep("g1_rec", [P, EC, 4]), "tile": c.keep("g1_tile", [P, EC]),
              "place_i": c.keep("g1_place_i", [P, EC], I32),
              "dinv": c.keep("g1_dinv", [P, T]), "tiles_of": c.keep("g1_tiles_of", [1, SLOTS1], I32),
              "table": c.keep("g1_table", [S, SLOTS1, 4])}
        part(nc, lambda: layer0_graph(c, scratch, mean, rstd, g1))
        part(nc, lambda: layer0_ffn(c, scratch, mean, rstd, g1))
        part(nc, lambda: layer1_graph(c, scratch, mean, rstd, g1))
        layer1_ffn(c, out, mean, rstd)


def lay_out(inputs):
    def a(name):
        return np.ascontiguousarray(inputs[name])

    def by_partition(w):
        e, k, n = w.shape
        return np.ascontiguousarray(w.reshape(e, k // 128, 128, n).transpose(0, 2, 1, 3))

    def columns(v):
        return np.ascontiguousarray(v.reshape(-1, 128).T)

    return {
        "x": a("x"), "src": a("src"), "dst": a("dst"), "edge_weight": a("edge_weight"), "g0_w": a("L0_gnn_weight"),
        "f0_wr": a("L0_ffn_Wr"), "f0_br": a("L0_ffn_br"),
        "f0_g": columns(a("L0_ffn_ln_g")), "f0_b": columns(a("L0_ffn_ln_b")),
        "f0_w1": by_partition(a("L0_ffn_W1")), "f0_b1": columns(a("L0_ffn_b1")),
        "f0_w2": by_partition(a("L0_ffn_W2")), "f0_b2": a("L0_ffn_b2"),
        "g1_w1": a("L1_gnn_W1"), "g1_b1": a("L1_gnn_b1"), "g1_g1": a("L1_gnn_g1"), "g1_be1": a("L1_gnn_be1"),
        "g1_w2": a("L1_gnn_W2"), "g1_b2": a("L1_gnn_b2"), "g1_g2": a("L1_gnn_g2"), "g1_be2": a("L1_gnn_be2"),
        "g1_wfc": a("L1_gnn_Wfc"), "g1_bfc": a("L1_gnn_bfc"),
        "f1_wr": a("L1_ffn_Wr"), "f1_br": a("L1_ffn_br"), "f1_w1": by_partition(a("L1_ffn_W1")),
        "f1_b1": np.ascontiguousarray(a("L1_ffn_b1").reshape(EXPERTS, H1 // 128, 128).transpose(0, 2, 1)),
        "f1_w2": by_partition(a("L1_ffn_W2")), "f1_b2": a("L1_ffn_b2"),
        "f1_gamma": a("L1_ffn_gamma"), "f1_beta": a("L1_ffn_beta"),
    }


def program(nc, args, out):
    dram = lambda name, shape: nc.dram_tensor(name, shape, F32).ap()
    scratch = {
        "support": dram("support", [NODES, D]), "h1": dram("h1", [NODES, C1]), "h2": dram("h2", [NODES, C2]),
        "rows0": dram("rows0", [S * SLOTS, 4]), "rows1": dram("rows1", [S * SLOTS1, 4]),
        "slots": dram("slots", [(BLOCKS + 1) * B, D]), "results": dram("results", [BLOCKS * B, D]),
    }
    build(nc, args, out, scratch)


def kernel(**inputs):
    import concourse.bacc as bacc
    from concourse.bass_utils import run_bass_kernel_spmd

    nc = bacc.Bacc("TRN2", target_bir_lowering=False, num_devices=1)
    arrays = {"in_" + k: v for k, v in lay_out(inputs).items()}
    args = {k[3:]: nc.dram_tensor(k, v.shape, mybir.dt.from_np(v.dtype), kind="ExternalInput").ap()
            for k, v in arrays.items()}
    out = nc.dram_tensor("out_0_dram", (NODES, D), F32, kind="ExternalOutput").ap()
    program(nc, args, out)
    r = run_bass_kernel_spmd(nc, [arrays], core_ids=[0])
    return r.results[0]["out_0_dram"]
```
